# Optimizing a Trainium2 kernel written in Bass

```python
import numpy as np
import jax
import jax.numpy as jnp

def _softmax(x, axis=-1):
    return jax.nn.softmax(x, axis=axis)

def _gelu(x):
    return jax.nn.gelu(x, approximate=True)

def _silu(x):
    return jax.nn.silu(x)

def _sigmoid(x):
    return jax.nn.sigmoid(x)

def _layernorm(x, axis=-1, eps=1e-05):
    m = jnp.mean(x, axis=axis, keepdims=True)
    v = jnp.var(x, axis=axis, keepdims=True)
    return (x - m) / jnp.sqrt(v + eps)

def _scatter_add(tgt, idx, src, axis=0):
    return tgt.at[idx].add(src)

def _segment_sum(src, seg, n):
    return jax.ops.segment_sum(src, seg, n)
kernel_name = 'mk_adaln_ffn_d2_seqx_r4_9d24b6'

def setup_inputs(seed: int=0):
    np.random.seed(seed)
    _w = jnp.asarray

    def _rec_inputs():
        import jax
        import jax.numpy as jnp
        _rk = jax.random.key(seed)
        x = -7.109e-05 + 0.9999 * jax.random.normal(jax.random.fold_in(_rk, 1), (128, 64, 1024), jnp.float32)
        _lenS = 64 - jax.random.randint(jax.random.fold_in(_rk, 7), (128,), 0, max(1, 64 // 4) + 1, jnp.int32)
        _lenS2 = 64 - jax.random.randint(jax.random.fold_in(_rk, 8), (128,), 0, max(1, 64 // 4) + 1, jnp.int32)
        itok_B_0_15 = jax.random.randint(jax.random.fold_in(_rk, 11), (128,), 0, 16, jnp.int32)
        itok_B_6_15 = jax.random.randint(jax.random.fold_in(_rk, 12), (128,), 6, 16, jnp.int32)
        return (x, itok_B_0_15, itok_B_6_15)
    x, itok_B_0_15, itok_B_6_15 = _rec_inputs()

    def _L0_cond_setup():
        import jax, jax.numpy as jnp
        import numpy as np
        NUM_CONDITIONS = 16
        IN_CH = 64
        OUT_CH = 64
        B = 64
        T = 1024
        key = jax.random.key(seed)
        k_x, k_w, k_c = jax.random.split(key, 3)
        x = jax.random.normal(k_x, (B, IN_CH, T), dtype=jnp.float32)
        bound = float(np.sqrt(6.0 / IN_CH))
        weights = jax.random.uniform(k_w, (NUM_CONDITIONS, IN_CH, OUT_CH), dtype=jnp.float32, minval=-bound, maxval=bound)
        condition = jax.random.randint(k_c, (B,), 0, NUM_CONDITIONS, dtype=jnp.int64)
        return {'x': x, 'weights': weights, 'condition': condition}
    _L0_cond_all = _L0_cond_setup()
    _L0_cond_in = {k: v for k, v in _L0_cond_all.items() if k in ('weights',)}
    del _L0_cond_all

    def _L0_ffn_setup():
        import jax, jax.numpy as jnp
        import numpy as np
        HID, BOT, RDIM, NSLOT, K, VB = (1024, 64, 48, 256, 8, 64)
        TAU_LOW, TAU_HIGH, EARLY_EXIT = (0.5, 2.0, 0.05)

        def _uncertainty(h, Wu1, bu1, Wu2, bu2):
            var = jnp.var(h, axis=-1)
            log_var = jnp.log1p(var)
            norm_var = log_var / (jnp.mean(log_var) + 1e-06)
            learned = (jax.nn.gelu(h @ Wu1.T + bu1) @ Wu2.T + bu2)[..., 0]
            return jnp.clip(norm_var * 0.5 + jax.nn.sigmoid(learned) * 2.5, 0.0, 5.0)
        key = jax.random.key(seed)
        ks = jax.random.split(key, 12)
        B, S = (2, 512)
        return {'hidden_states': jax.random.normal(ks[0], (B, S, HID), dtype=jnp.float32), 'Wq': jax.random.normal(ks[1], (BOT, HID), dtype=jnp.float32) / np.sqrt(HID), 'Wr': jax.random.normal(ks[2], (RDIM, BOT), dtype=jnp.float32) / np.sqrt(BOT), 'aux_keys': jax.random.normal(ks[3], (NSLOT, BOT), dtype=jnp.float32) * 0.01, 'aux_values': jax.random.normal(ks[4], (NSLOT, HID), dtype=jnp.float32) * 0.02, 'Wvd': jax.random.normal(ks[5], (VB, HID), dtype=jnp.float32) * 0.1 / np.sqrt(HID), 'Wvu': jax.random.normal(ks[6], (HID, VB), dtype=jnp.float32) * 0.1 / np.sqrt(VB), 'Wu1': jax.random.normal(ks[7], (HID // 4, HID), dtype=jnp.float32) / np.sqrt(HID), 'bu1': jnp.zeros((HID // 4,), dtype=jnp.float32), 'Wu2': jax.random.normal(ks[8], (1, HID // 4), dtype=jnp.float32) * 0.01, 'bu2': jnp.zeros((1,), dtype=jnp.float32), 'gate_w1': jnp.float32(0.5), 'gate_bias': jnp.float32(-1.0), 'log_rel': jnp.zeros((NSLOT,), dtype=jnp.float32)}
    _L0_ffn_all = _L0_ffn_setup()
    _L0_ffn_in = {k: v for k, v in _L0_ffn_all.items() if k in ('Wq', 'Wr', 'aux_keys', 'aux_values', 'Wvd', 'Wvu', 'Wu1', 'bu1', 'Wu2', 'bu2', 'gate_w1', 'gate_bias', 'log_rel')}
    del _L0_ffn_all

    def _L1_cond_setup():
        import jax, jax.numpy as jnp
        import numpy as np
        B, S, D_IN, D_OUT = (4, 512, 1024, 1024)
        RANK, MAX_LORAS = (16, 32)
        key = jax.random.key(seed)
        ks = jax.random.split(key, 6)
        x = jax.random.normal(ks[0], (B, S, D_IN), dtype=jnp.float32)
        adapter_ids = jax.random.randint(ks[1], (B,), 0, MAX_LORAS)
        base_weight = jax.random.normal(ks[2], (D_OUT, D_IN), dtype=jnp.float32) * D_IN ** (-0.5)
        base_bias = jax.random.normal(ks[3], (D_OUT,), dtype=jnp.float32) * 0.01
        lora_A_w = jax.random.normal(ks[4], (MAX_LORAS, RANK, D_IN), dtype=jnp.float32) * D_IN ** (-0.5)
        lora_B_w = jax.random.normal(ks[5], (MAX_LORAS, D_OUT, RANK), dtype=jnp.float32) * RANK ** (-0.5)
        return {'x': x, 'adapter_ids': adapter_ids, 'base_weight': base_weight, 'base_bias': base_bias, 'lora_A_w': lora_A_w, 'lora_B_w': lora_B_w}
    _L1_cond_all = _L1_cond_setup()
    _L1_cond_in = {k: v for k, v in _L1_cond_all.items() if k in ('base_weight', 'base_bias', 'lora_A_w', 'lora_B_w')}
    del _L1_cond_all

    def _L1_ffn_setup():
        import math
        import jax, jax.numpy as jnp
        import numpy as np
        SCALING = 16.0 / 32.0

        def real_fourier_orthogonal_multiply(c):
            n = c.shape[-1]
            sqrt_n = math.sqrt(n)
            pair_scale = math.sqrt(n / 2.0)
            max_f = (n - 1) // 2
            work = c.astype(jnp.float32)
            dc = (work[..., 0] * sqrt_n)[..., None].astype(jnp.complex64)
            cos = work[..., 1:1 + 2 * max_f:2] * pair_scale
            sin = work[..., 2:2 + 2 * max_f:2] * pair_scale
            mid = (cos - 1j * sin).astype(jnp.complex64)
            parts = [dc, mid]
            if n % 2 == 0:
                parts.append((work[..., -1] * sqrt_n)[..., None].astype(jnp.complex64))
            spectrum = jnp.concatenate(parts, axis=-1)
            return jnp.fft.irfft(spectrum, n=n, axis=-1).astype(c.dtype)
        key = jax.random.key(seed)
        ks = jax.random.split(key, 9)
        B, S, D_in, D_out, R0, R1, E = (4, 512, 1024, 1024, 32, 8, 3)
        x = jax.random.normal(ks[0], (B, S, D_in), dtype=jnp.float32)
        W_base = jax.random.normal(ks[1], (D_out, D_in), dtype=jnp.float32) * 0.02
        b_base = jax.random.normal(ks[2], (D_out,), dtype=jnp.float32) * 0.02
        enc0 = jax.random.normal(ks[3], (R0, D_in), dtype=jnp.float32) * 0.02
        enc1 = jax.random.normal(ks[4], (R1, D_in), dtype=jnp.float32) * 0.02
        coefs0 = jax.random.normal(ks[5], (E, D_out, R0), dtype=jnp.float32) * 0.02
        coefs1 = jax.random.normal(ks[6], (E, D_out, R1), dtype=jnp.float32) * 0.02
        mask0 = jax.random.randint(ks[7], (E, D_out, R0), 0, 2).astype(bool)
        mask1 = jax.random.randint(ks[8], (E, D_out, R1), 0, 2).astype(bool)
        return dict(x=x, W_base=W_base, b_base=b_base, enc0=enc0, enc1=enc1, coefs0=coefs0, coefs1=coefs1, mask0=mask0, mask1=mask1)
    _L1_ffn_all = _L1_ffn_setup()
    _L1_ffn_in = {k: v for k, v in _L1_ffn_all.items() if k in ('W_base', 'b_base', 'enc0', 'enc1', 'coefs0', 'coefs1', 'mask0', 'mask1')}
    del _L1_ffn_all
    return {'x': x, 'itok_B_0_15': itok_B_0_15, 'itok_B_6_15': itok_B_6_15, 'L0_cond_weights': _L0_cond_in['weights'], 'L0_ffn_Wq': _L0_ffn_in['Wq'], 'L0_ffn_Wr': _L0_ffn_in['Wr'], 'L0_ffn_aux_keys': _L0_ffn_in['aux_keys'], 'L0_ffn_aux_values': _L0_ffn_in['aux_values'], 'L0_ffn_Wvd': _L0_ffn_in['Wvd'], 'L0_ffn_Wvu': _L0_ffn_in['Wvu'], 'L0_ffn_Wu1': _L0_ffn_in['Wu1'], 'L0_ffn_bu1': _L0_ffn_in['bu1'], 'L0_ffn_Wu2': _L0_ffn_in['Wu2'], 'L0_ffn_bu2': _L0_ffn_in['bu2'], 'L0_ffn_gate_w1': _L0_ffn_in['gate_w1'], 'L0_ffn_gate_bias': _L0_ffn_in['gate_bias'], 'L0_ffn_log_rel': _L0_ffn_in['log_rel'], 'L1_cond_base_weight': _L1_cond_in['base_weight'], 'L1_cond_base_bias': _L1_cond_in['base_bias'], 'L1_cond_lora_A_w': _L1_cond_in['lora_A_w'], 'L1_cond_lora_B_w': _L1_cond_in['lora_B_w'], 'L1_ffn_W_base': _L1_ffn_in['W_base'], 'L1_ffn_b_base': _L1_ffn_in['b_base'], 'L1_ffn_enc0': _L1_ffn_in['enc0'], 'L1_ffn_enc1': _L1_ffn_in['enc1'], 'L1_ffn_coefs0': _L1_ffn_in['coefs0'], 'L1_ffn_coefs1': _L1_ffn_in['coefs1'], 'L1_ffn_mask0': _L1_ffn_in['mask0'], 'L1_ffn_mask1': _L1_ffn_in['mask1']}

def reference(x, itok_B_0_15, itok_B_6_15, L0_cond_weights, L0_ffn_Wq, L0_ffn_Wr, L0_ffn_aux_keys, L0_ffn_aux_values, L0_ffn_Wvd, L0_ffn_Wvu, L0_ffn_Wu1, L0_ffn_bu1, L0_ffn_Wu2, L0_ffn_bu2, L0_ffn_gate_w1, L0_ffn_gate_bias, L0_ffn_log_rel, L1_cond_base_weight, L1_cond_base_bias, L1_cond_lora_A_w, L1_cond_lora_B_w, L1_ffn_W_base, L1_ffn_b_base, L1_ffn_enc0, L1_ffn_enc1, L1_ffn_coefs0, L1_ffn_coefs1, L1_ffn_mask0, L1_ffn_mask1):
    import jax
    import jax.numpy as jnp

    def _L0_cond_ref(x, weights, condition):
        import jax, jax.numpy as jnp
        import numpy as np
        NUM_CONDITIONS = 16
        IN_CH = 64
        OUT_CH = 64
        B = 64
        T = 1024
        W = weights[condition]
        return jnp.einsum('bct,bcd->bdt', x, W)

    def _L0_ffn_ref(hidden_states, Wq, Wr, aux_keys, aux_values, Wvd, Wvu, Wu1, bu1, Wu2, bu2, gate_w1, gate_bias, log_rel):
        import jax, jax.numpy as jnp
        import numpy as np
        HID, BOT, RDIM, NSLOT, K, VB = (1024, 64, 48, 256, 8, 64)
        TAU_LOW, TAU_HIGH, EARLY_EXIT = (0.5, 2.0, 0.05)

        def _uncertainty(h, Wu1, bu1, Wu2, bu2):
            var = jnp.var(h, axis=-1)
            log_var = jnp.log1p(var)
            norm_var = log_var / (jnp.mean(log_var) + 1e-06)
            learned = (jax.nn.gelu(h @ Wu1.T + bu1) @ Wu2.T + bu2)[..., 0]
            return jnp.clip(norm_var * 0.5 + jax.nn.sigmoid(learned) * 2.5, 0.0, 5.0)
        query = hidden_states @ Wq.T
        rq = query @ Wr.T
        rk = aux_keys @ Wr.T
        router_scores = jnp.einsum('bsr,nr->bsn', rq, rk) / np.sqrt(RDIM) + log_rel
        top_scores, top_idx = jax.lax.top_k(router_scores, K)
        sel_keys = aux_keys[top_idx]
        attn = jnp.einsum('bsd,bskd->bsk', query, sel_keys) / np.sqrt(BOT) + log_rel[top_idx]
        w = jax.nn.softmax(attn, axis=-1)
        sel_vals = aux_values[top_idx]
        aux_out = jnp.einsum('bsk,bskh->bsh', w, sel_vals)
        aux_out = aux_out @ Wvd.T @ Wvu.T
        u = _uncertainty(hidden_states, Wu1, bu1, Wu2, bu2)
        u_norm = jnp.clip((u - TAU_LOW) / (TAU_HIGH - TAU_LOW), 0.0, 1.0)
        gate = jax.nn.sigmoid(gate_w1 * u_norm + gate_bias)
        gate = jnp.where(gate < EARLY_EXIT, 0.0, gate)
        return hidden_states + gate[..., None] * aux_out

    def _L1_cond_ref(x, adapter_ids, base_weight, base_bias, lora_A_w, lora_B_w):
        import jax, jax.numpy as jnp
        import numpy as np
        B, S, D_IN, D_OUT = (4, 512, 1024, 1024)
        RANK, MAX_LORAS = (16, 32)
        result = jnp.einsum('bsd,od->bso', x, base_weight) + base_bias
        A = lora_A_w[adapter_ids]
        Bw = lora_B_w[adapter_ids]
        h = jnp.einsum('bsd,brd->bsr', x, A)
        lora_out = jnp.einsum('bsr,bor->bso', h, Bw)
        result = result + lora_out
        return result.astype(x.dtype)

    def _L1_ffn_ref(x, W_base, b_base, enc0, enc1, coefs0, coefs1, mask0, mask1):
        import math
        import jax, jax.numpy as jnp
        import numpy as np
        SCALING = 16.0 / 32.0

        def real_fourier_orthogonal_multiply(c):
            n = c.shape[-1]
            sqrt_n = math.sqrt(n)
            pair_scale = math.sqrt(n / 2.0)
            max_f = (n - 1) // 2
            work = c.astype(jnp.float32)
            dc = (work[..., 0] * sqrt_n)[..., None].astype(jnp.complex64)
            cos = work[..., 1:1 + 2 * max_f:2] * pair_scale
            sin = work[..., 2:2 + 2 * max_f:2] * pair_scale
            mid = (cos - 1j * sin).astype(jnp.complex64)
            parts = [dc, mid]
            if n % 2 == 0:
                parts.append((work[..., -1] * sqrt_n)[..., None].astype(jnp.complex64))
            spectrum = jnp.concatenate(parts, axis=-1)
            return jnp.fft.irfft(spectrum, n=n, axis=-1).astype(c.dtype)
        base = jnp.einsum('bsd,od->bso', x, W_base) + b_base
        e0 = jnp.einsum('bsd,rd->bsr', x, enc0)
        e1 = jnp.einsum('bsd,rd->bsr', x, enc1)
        w0 = coefs0 * mask0.astype(coefs0.dtype)
        w1 = coefs1 * mask1.astype(coefs1.dtype)
        decoded = jnp.einsum('bsr,eor->ebso', e0, w0) + jnp.einsum('bsr,eor->ebso', e1, w1)
        transformed = real_fourier_orthogonal_multiply(decoded)
        update = transformed.sum(axis=0)
        return base + update * SCALING
    x = x + _L0_ffn_ref(_L0_cond_ref(x, L0_cond_weights, itok_B_0_15), L0_ffn_Wq, L0_ffn_Wr, L0_ffn_aux_keys, L0_ffn_aux_values, L0_ffn_Wvd, L0_ffn_Wvu, L0_ffn_Wu1, L0_ffn_bu1, L0_ffn_Wu2, L0_ffn_bu2, L0_ffn_gate_w1, L0_ffn_gate_bias, L0_ffn_log_rel)
    x = x + _L1_ffn_ref(_L1_cond_ref(x, itok_B_6_15, L1_cond_base_weight, L1_cond_base_bias, L1_cond_lora_A_w, L1_cond_lora_B_w), L1_ffn_W_base, L1_ffn_b_base, L1_ffn_enc0, L1_ffn_enc1, L1_ffn_coefs0, L1_ffn_coefs1, L1_ffn_mask0, L1_ffn_mask1)
    return x

_drawn_inputs = setup_inputs


def setup_inputs(seed=0):
    import zlib

    import numpy as np

    out = dict(_drawn_inputs(seed))
    spreads = {'L0_ffn_bu1': (0.0, 2.0), 'L0_ffn_log_rel': (0.0, 2.0)}
    factors = {'L0_ffn_Wq': 46.146,
     'L0_ffn_Wr': 53.892,
     'L0_ffn_aux_keys': 45.554,
     'L0_ffn_aux_values': 45.303,
     'L0_ffn_Wvd': 45.879,
     'L0_ffn_Wvu': 45.453,
     'L0_ffn_Wu1': 64.0,
     'L0_ffn_Wu2': 64.0,
     'L1_cond_base_bias': 81.204,
     'L1_ffn_b_base': 24.11}
    for name, (base, spread) in spreads.items():
        noise = np.random.default_rng([zlib.crc32(name.encode()), seed]).standard_normal(out[name].shape)
        drawn = base * np.exp(spread * noise) if base else spread * noise
        out[name] = jnp.asarray(drawn.astype(out[name].dtype))
    for name, factor in factors.items():
        out[name] = (out[name] * factor).astype(out[name].dtype)
    return out
```

```python
from contextlib import ExitStack

import numpy as np

import concourse.bass as bass
from concourse import mybir

F32 = mybir.dt.float32
F32R = mybir.dt.float32r
I32 = mybir.dt.int32
U8 = mybir.dt.uint8
ALU = mybir.AluOpType
ACT = mybir.ActivationFunctionType
AX = mybir.AxisListType

P = 128
BATCH, CH, HID = 128, 64, 1024
NT = BATCH * CH // P
KC = HID // P
HALF = HID // 2
NCOND = 16
NLORA, RANK = 32, 16
NUNC = HID // 4
BOT = 64
RDIM = 48
NSLOT = 256
RENC = 40
NEXP = 3
GRP = RANK
NUG, NQG = NUNC // GRP, BOT // GRP
HQW = NUNC + BOT
PAW = HQW + 2 * RANK
LBLK = NLORA * RANK // P
LPB = NLORA // LBLK
NEG = -1.0e30
REPLACED = -3.0e38
VAR_A, VAR_M, VAR_B = 16, 32, 16
TANH_C = 0.7978845608028654


def f(ap):
    return ap.bitcast(F32)


def product3(pe, out, a_hi, a_lo, b_hi, b_lo, start, stop, skip=False):
    pe.matmul(out, a_hi, b_hi, start=start, stop=False, skip_group_check=skip)
    pe.matmul(out, a_hi, b_lo, start=False, stop=False, skip_group_check=skip)
    return pe.matmul(out, a_lo, b_hi, start=False, stop=stop, skip_group_check=skip)


def wait_apart(eng, spacer, signal, count):
    eng.wait_ge(signal, count)
    if not isinstance(count, int):
        eng.memset(spacer, 0.0)


def known_positive(count):
    return not isinstance(count, int) or count > 0


def build(nc, t):
    with ExitStack() as top:
        def sem(name):
            return top.enter_context(nc.semaphore(name))

        def tile(stack, name, shape, dt=F32, side="left"):
            return stack.enter_context(nc.sbuf_tensor(name, shape, dt, side=side))

        t["w_kinds"] = nc.dram_tensor("w_kinds", (NCOND, CH, 4, CH), F32, kind="Internal").ap()
        t["a_split"] = nc.dram_tensor("a_split", (NLORA, P, 2, KC, RANK), F32, kind="Internal").ap()
        t["wa_split"] = nc.dram_tensor("wa_split", (NLORA, P, 2, RANK), F32, kind="Internal").ap()
        t["bk_hi"] = nc.dram_tensor("bk_hi", (NLORA * RANK, HID), F32, kind="Internal").ap()
        t["bk_lo"] = nc.dram_tensor("bk_lo", (NLORA * RANK, HID), F32, kind="Internal").ap()
        t["const_split"] = nc.dram_tensor("const_split", (2, HID), F32, kind="Internal").ap()

        pair = [top.enter_context(nc.psum_tensor(f"pair{n}", [P, HID], F32)) for n in range(4)]

        g = {}
        for name, shape, dt in (
            ("ident", [P, P], F32), ("lora_mask", [2 * RANK, P], F32),
            ("ones", [P, P], F32), ("spacer", [1, 1], F32),
            ("cond_ids", [1, BATCH], I32), ("lora_ids", [1, BATCH], I32),
            ("vd", [P, 2, BOT], F32),
            ("wvu_hi", [P, KC, P], F32R), ("wvu_lo", [P, KC, P], F32R),
            ("router_a", [P, 2 * NSLOT], F32R), ("router_b", [P, 2 * NSLOT], F32R),
            ("var", [P, NT], F32), ("norm_var", [P, NT], F32),
        ):
            g[name] = tile(top, name, shape, dt)

        vstack = top.enter_context(ExitStack())
        v = {}
        for name, shape, dt in (
            ("v_x", [P, 2, HID], F32), ("v_hi", [P, 2, HID], F32R), ("v_lo", [P, 2, HID], F32R),
            ("v_w", [P, 4, 2, P], F32R), ("v_stats", [P, 2, 12], F32), ("v_mv", [P, 2, 2], F32),
        ):
            v[name] = tile(vstack, name, shape, dt)
        v["x_loaded"] = [sem(f"v_x_loaded{r}") for r in range(2)]
        v["w_loaded"] = [sem(f"v_w_loaded{r}") for r in range(4)]
        for name in ("v_hi_ready", "v_lo_ready", "v_mm_done", "v_bn_done", "v_aggr_done", "v_var_ready"):
            v[name] = sem(name)
        v["psum"] = pair[0:2]

        kstack = top.enter_context(ExitStack())
        k_hi, k_lo = setup_block(nc, t, g, v, pair, sem, tile, kstack)
        m_hi = tile(top, "m_hi", [P, KC, HID], F32R, side="right")
        m_lo = tile(top, "m_lo", [P, KC, HID], F32R, side="right")
        fold_block(nc, t, g, v, pair, sem, tile, k_hi, k_lo, m_hi, m_lo)
        kstack.close()
        vstack.close()
        main_block(nc, t, g, pair, sem, tile, m_hi, m_lo)



def var_load(sp, t, g, v, n, slot):
    s = slot % 2
    x_off = sp.snap(n * (P * HID)) if not isinstance(n, int) else n * P * HID
    splits = n - 1
    round2 = sp.snap(splits) if not isinstance(n, int) else splits
    used4 = n - 3
    used = sp.snap(used4) if not isinstance(n, int) else used4
    ids = [sp.value_load(g["cond_ids"][:, bass.ds(n * 2 + b, 1)], min_val=0, max_val=NCOND - 1)
           for b in range(2)]
    offs = [sp.snap(i * (CH * 4 * CH)) for i in ids]
    if known_positive(round2):
        sp.wait_ge(v["v_lo_ready"], round2)
    sp.dma_start(v["v_x"][:, s, :], bass.AP(t["x"].tensor, x_off, [[HID, P], [1, HID]])
                 ).then_inc(v["x_loaded"][s], 16)
    if known_positive(used):
        sp.wait_ge(v["v_mm_done"], used)
    for b in range(2):
        src = bass.AP(t["w_kinds"].tensor, offs[b], [[4 * CH, CH], [CH, 2], [1, CH]])
        sp.dma_start(f(v["v_w"][b * CH:(b + 1) * CH, slot, :, b * CH:(b + 1) * CH]), src
                     ).then_inc(v["w_loaded"][slot], 16)


def var_hi(act, v, n, slot):
    s = slot % 2
    act.wait_ge(v["x_loaded"][s], (n - s) * 8 + 16)
    if known_positive(n - 1):
        act.wait_ge(v["v_mm_done"], n - 1)
    act.copy(v["v_hi"][:, s, :], v["v_x"][:, s, :]).then_inc(v["v_hi_ready"], 1)


def var_lo(pool, v, n, slot):
    s = slot % 2
    ready = n + 1 if isinstance(n, int) else pool.snap(n + 1)
    pool.wait_ge(v["v_hi_ready"], ready)
    pool.tensor_tensor(v["v_lo"][:, s, :], v["v_x"][:, s, :], f(v["v_hi"][:, s, :]),
                       ALU.subtract).then_inc(v["v_lo_ready"], 1)


def var_mm(pe, v, n, slot):
    s = slot % 2
    pe.wait_ge(v["v_lo_ready"], n + 1)
    pe.wait_ge(v["w_loaded"][slot], quarter_count(n, slot))
    if known_positive(n - 1):
        pe.wait_ge(v["v_bn_done"], n - 1)
    w_hi, w_lo = v["v_w"][:, slot, 0, :], v["v_w"][:, slot, 1, :]
    out = v["psum"][s]
    for h in range(2):
        c = slice(h * HALF, (h + 1) * HALF)
        last = product3(pe, out[:, c], w_hi, w_lo, v["v_hi"][:, s, c], v["v_lo"][:, s, c], True, True)
    last.then_inc(v["v_mm_done"], 1)


def quarter_count(n, slot):
    return (n - slot) * 8 + 32


def var_stats(dve, spacer, g, v, n, slot):
    s = slot % 2
    dve.wait_ge(v["v_mm_done"], n + 1)
    if known_positive(n - 1):
        dve.wait_ge(v["v_aggr_done"], n - 1)
    dve.bn_stats(v["v_stats"][:, s, 0:6], v["psum"][s][:, 0:HALF])
    dve.bn_stats(v["v_stats"][:, s, 6:12], v["psum"][s][:, HALF:HID]).then_inc(v["v_bn_done"], 1)
    if known_positive(n - 1):
        dve.wait_ge(v["v_var_ready"], n - 1)
    wait_apart(dve, spacer, v["v_bn_done"], n + 1)
    dve.bn_aggr(v["v_mv"][:, s, :], v["v_stats"][:, s, :]).then_inc(v["v_aggr_done"], 1)
    dve.wait_ge(v["v_aggr_done"], n + 1)
    dve.tensor_copy(g["var"][:, bass.ds(n, 1)], v["v_mv"][:, s, 1:2]).then_inc(v["v_var_ready"], 1)



def setup_block(nc, t, g, v, pair, sem, tile, kstack):
    with ExitStack() as right, ExitStack() as early:
        fourier = tile(right, "fourier", [P, KC, HID], F32, "right")
        kf = tile(right, "kf", [P, KC, HID], F32, "right")
        enc_hi = tile(right, "enc_hi", [RENC, HID], F32R, "right")
        enc_lo = tile(right, "enc_lo", [RENC, HID], F32R, "right")
        cs_hi = tile(right, "cs_hi", [RENC, HID], F32R, "right")
        cs_lo = tile(right, "cs_lo", [RENC, HID], F32R, "right")

        enc = tile(early, "enc", [RENC, HID])
        w_raw = tile(early, "w_raw", [CH, NCOND, CH])
        w_plus = tile(early, "w_plus", [CH, NCOND, CH])
        w_kinds = tile(early, "w_kinds_sb", [CH, NCOND, 4, CH], F32R)
        coefs = tile(early, "coefs", [P, NEXP, KC * RENC])
        masks = tile(early, "masks", [P, NEXP, KC * RENC // 4], I32)
        av_t = tile(early, "av_t", [P, KC, NSLOT])
        wvd_t = tile(early, "wvd_t", [P, KC, BOT])
        wvu = tile(early, "wvu", [P, KC, P])
        a_raw = tile(early, "a_raw", [P, LPB, KC, RANK])
        a_split = tile(early, "a_split_sb", [P, LPB, 2, KC, RANK], F32R)
        wa_split = tile(early, "wa_split_sb", [P, NLORA, 2, RANK], F32R)
        wr = tile(early, "wr", [RDIM, 2 * BOT])
        wtw = tile(early, "wtw", [BOT, 2 * BOT])
        keys = tile(early, "keys", [P, NSLOT])
        router = tile(early, "router", [P, 2 * NSLOT])
        logrel = tile(early, "logrel", [1, 2 * NSLOT])
        logrel_hi = tile(early, "logrel_hi", [1, 2 * NSLOT], F32R)
        logrel_lo = tile(early, "logrel_lo", [1, 2 * NSLOT], F32R)
        early.close()
        k_hi = tile(kstack, "k_hi", [P, KC, HID], F32R)
        k_lo = tile(kstack, "k_lo", [P, KC, HID], F32R)

        names = ("ids_in w_in enc_in coefs_in av_in a_in wvu_in keys_in logrel_in fourier_in wbase_in "
                 "w_stored a_stored wa_stored logrel_placed s_chain p_chain c_chain zeroed w_plus_ready w_hi_ready w_kinds_ready "
                 "enc_hi_ready enc_split wvu_hi_ready wvu_split wsum_ready a_hi_ready a_split_ready "
                 "wa_mm_done wa_split_ready vd_mm_done vd_ready wtw_mm_done wtw_ready g_mm_done "
                 "router_ready cs_mm_done cs_hi_ready cs_split k_mm_done k_sum_ready k_hi_ready "
                 "logrel_split").split()
        s = {n: sem(n) for n in names}
        small = pair[3][:, 0:HALF]
        wa_bank = pair[3][:, HALF:HID]
        kpair = pair[2:4]

        with nc.Block() as block:

            @block.sync
            def _(sp):
                sp.dma_start(w_raw[:], t["cond_w"]).then_inc(s["w_in"], 16)
                sp.dma_start(g["ident"][:], t["ident"]).then_inc(s["w_in"], 16)
                for name in ("cond_ids", "lora_ids"):
                    sp.dma_start(g[name][:], t[name]).then_inc(s["ids_in"], 16)
                sp.dma_start(v["v_x"][:, 0, :], bass.AP(t["x"].tensor, 0, [[HID, P], [1, HID]])
                             ).then_inc(v["x_loaded"][0], 16)
                sp.dma_start(v["v_x"][:, 1, :], bass.AP(t["x"].tensor, P * HID, [[HID, P], [1, HID]])
                             ).then_inc(v["x_loaded"][1], 16)
                sp.wait_ge(s["w_kinds_ready"], 1)
                sp.dma_start(t["w_kinds"].rearrange("n c k d -> c n k d"), f(w_kinds[:])
                             ).then_inc(s["w_stored"], 16)
                sp.wait_ge(s["ids_in"], 32)
                sp.wait_ge(s["w_stored"], 16)
                sp.wait_ge(s["zeroed"], 1)
                for n in range(VAR_A):
                    if n >= 2:
                        var_load(sp, t, g, v, n, n % 4)
                        continue
                    ids = [sp.value_load(g["cond_ids"][:, 2 * n + b:2 * n + b + 1], min_val=0,
                                         max_val=NCOND - 1) for b in range(2)]
                    for b in range(2):
                        off = sp.snap(ids[b] * (CH * 4 * CH))
                        src = bass.AP(t["w_kinds"].tensor, off, [[4 * CH, CH], [CH, 2], [1, CH]])
                        sp.dma_start(f(v["v_w"][b * CH:(b + 1) * CH, n, :, b * CH:(b + 1) * CH]), src
                                     ).then_inc(v["w_loaded"][n], 16)

            @block.scalar
            def _(act):
                for dst, src in ((wvu[:], t["wvu"]), (wr[:], t["wr"]), (g["lora_mask"][:], t["lora_mask"])):
                    act.dma_start(dst, src).then_inc(s["wvu_in"], 16)
                act.dma_start(keys[:], t["keys_t"]).then_inc(s["keys_in"], 16)
                act.dma_start(logrel[:], t["log_rel"]).then_inc(s["logrel_in"], 16)
                act.dma_start(a_raw[:], t["lora_a"][0]).then_inc(s["a_in"], 16)
                act.dma_start(av_t[:], t["av_t"]).then_inc(s["av_in"], 16)
                act.dma_start(wvd_t[:], t["wvd_t"]).then_inc(s["av_in"], 16)
                act.dma_start(coefs[:], t["coefs"]).then_inc(s["coefs_in"], 16)
                act.dma_start(masks[:], t["masks"]).then_inc(s["coefs_in"], 16)
                act.dma_start(enc[:], t["enc"]).then_inc(s["enc_in"], 16)
                for k in range(KC):
                    act.dma_start(fourier[:, k, :], t["fourier"][k]).then_inc(s["fourier_in"], 16)
                for k in range(KC):
                    act.dma_start(kf[:, k, :], t["w_base_t"][k]).then_inc(s["wbase_in"], 16)
                act.wait_ge(s["w_in"], 32)
                act.copy(w_kinds[:, :, 0, :], w_raw[:])
                act.wait_ge(s["w_plus_ready"], 1)
                act.copy(w_kinds[:, :, 2, :], w_plus[:]).then_inc(s["w_hi_ready"], 1)
                act.wait_ge(s["wvu_in"], 48)
                act.copy(g["wvu_hi"][:], wvu[:]).then_inc(s["wvu_hi_ready"], 1)
                for c in range(LBLK):
                    act.wait_ge(s["a_in"], 16 * (c + 1))
                    if c:
                        act.wait_ge(s["wa_mm_done"], c)
                        act.wait_ge(s["a_stored"], 16 * c)
                    act.copy(a_split[:, :, 0], a_raw[:]).then_inc(s["a_hi_ready"], 1)
                    if c + 1 < LBLK:
                        act.wait_ge(s["a_split_ready"], c + 1)
                        act.dma_start(a_raw[:], t["lora_a"][c + 1]).then_inc(s["a_in"], 16)
                    var_hi(act, v, 2 * c, (2 * c) % 4)
                    var_hi(act, v, 2 * c + 1, (2 * c + 1) % 4)
                act.wait_ge(s["enc_in"], 16)
                act.copy(enc_hi[:], enc[:]).then_inc(s["enc_hi_ready"], 1)
                act.wait_ge(s["cs_mm_done"], 1)
                act.mul(cs_hi[:], pair[2][0:RENC, :], 0.5).then_inc(s["cs_hi_ready"], 1)
                act.wait_ge(s["w_stored"], 16)
                act.wait_ge(s["a_stored"], 16 * LBLK)
                act.wait_ge(s["wa_stored"], 16)
                act.wait_ge(s["logrel_placed"], 32)
                for k in range(KC):
                    var_hi(act, v, 8 + k, k % 4)
                    act.wait_ge(s["k_sum_ready"], k + 1)
                    act.copy(k_hi[:, k, :], kf[:, k, :]).then_inc(s["k_hi_ready"], 1)

            @block.gpsimd
            def _(pool):
                pool.memset(g["ones"][:], 1.0)
                pool.memset(f(g["router_b"][:]), 0.0)
                pool.memset(f(v["v_w"][:]), 0.0).then_inc(s["zeroed"], 1)
                pool.wait_ge(s["w_hi_ready"], 1)
                pool.tensor_tensor(w_kinds[:, :, 1, :], w_raw[:], f(w_kinds[:, :, 0, :]), ALU.subtract)
                pool.tensor_tensor(w_kinds[:, :, 3, :], w_plus[:], f(w_kinds[:, :, 2, :]),
                                   ALU.subtract).then_inc(s["w_kinds_ready"], 1)
                pool.wait_ge(s["wvu_hi_ready"], 1)
                pool.tensor_tensor(g["wvu_lo"][:], wvu[:], f(g["wvu_hi"][:]),
                                   ALU.subtract).then_inc(s["wvu_split"], 1)
                for c in range(LBLK):
                    pool.wait_ge(s["a_hi_ready"], c + 1)
                    pool.tensor_tensor(a_split[:, :, 1], a_raw[:], f(a_split[:, :, 0]),
                                       ALU.subtract).then_inc(s["a_split_ready"], 1)
                    pool.wait_ge(s["a_split_ready"], c + 1)
                    pool.dma_start(t["a_split"][c * LPB:(c + 1) * LPB].rearrange("l p s k r -> p l s k r"),
                                   f(a_split[:])).then_inc(s["a_stored"], 16)
                    var_lo(pool, v, 2 * c, (2 * c) % 4)
                    var_lo(pool, v, 2 * c + 1, (2 * c + 1) % 4)
                pool.wait_ge(s["enc_hi_ready"], 1)
                pool.tensor_tensor(enc_lo[:], enc[:], f(enc_hi[:]), ALU.subtract).then_inc(s["enc_split"], 1)
                pool.wait_ge(s["wa_split_ready"], 1)
                pool.dma_start(t["wa_split"].rearrange("l p s r -> p l s r"), f(wa_split[:])
                               ).then_inc(s["wa_stored"], 16)
                pool.wait_ge(s["logrel_split"], 1)
                pool.wait_ge(s["router_ready"], 1)
                pool.dma_start(f(g["router_b"][BOT:BOT + 1, :]), f(logrel_hi[:])).then_inc(s["logrel_placed"], 16)
                pool.dma_start(f(g["router_b"][BOT + 1:BOT + 2, :]), f(logrel_lo[:])).then_inc(s["logrel_placed"], 16)
                pool.wait_ge(s["logrel_placed"], 32)
                pool.wait_ge(s["wa_stored"], 16)
                pool.wait_ge(s["a_stored"], 16 * LBLK)
                for k in range(KC):
                    var_lo(pool, v, 8 + k, k % 4)
                    pool.wait_ge(s["k_hi_ready"], k + 1)
                    pool.tensor_tensor(k_lo[:, k, :], kf[:, k, :], f(k_hi[:, k, :]), ALU.subtract)
                pool.drain()

            @block.tensor
            def _(pe):
                pe.wait_ge(s["wvu_in"], 48)
                pe.matmul(small[0:BOT, 0:2 * BOT], wr[:, 0:BOT], wr[:], start=True, stop=True
                          ).then_inc(s["wtw_mm_done"], 1)
                pe.wait_ge(s["keys_in"], 16)
                pe.wait_ge(s["wtw_ready"], 1)
                pe.matmul(small[:, 0:NSLOT], wtw[:], keys[0:BOT, :], start=True, stop=True
                          ).then_inc(s["g_mm_done"], 1)
                for c in range(LBLK):
                    pe.wait_ge(s["wvu_split"], 1)
                    pe.wait_ge(s["a_split_ready"], c + 1)
                    for k in range(KC):
                        last = product3(pe, wa_bank[:, c * P:(c + 1) * P],
                                        g["wvu_hi"][:, k, :], g["wvu_lo"][:, k, :],
                                        a_split[:, :, 0, k, :], a_split[:, :, 1, k, :], k == 0, k == KC - 1)
                    last.then_inc(s["wa_mm_done"], 1)
                    var_mm(pe, v, 2 * c, (2 * c) % 4)
                    var_mm(pe, v, 2 * c + 1, (2 * c + 1) % 4)
                pe.wait_ge(s["av_in"], 32)
                pe.wait_ge(s["router_ready"], 1)
                for b in range(2):
                    for k in range(KC):
                        last = pe.matmul(small[:, b * BOT:(b + 1) * BOT], av_t[:, k, b * P:(b + 1) * P],
                                         wvd_t[:, k, :], start=(k == 0), stop=(k == KC - 1))
                last.then_inc(s["vd_mm_done"], 1)
                pe.wait_ge(s["wsum_ready"], 1)
                pe.wait_ge(s["fourier_in"], 16 * KC)
                for h in range(2):
                    for k in range(KC):
                        last = pe.matmul(pair[2][0:RENC, h * HALF:(h + 1) * HALF],
                                         coefs[:, 0, k * RENC:(k + 1) * RENC],
                                         fourier[:, k, h * HALF:(h + 1) * HALF],
                                         start=(k == 0), stop=(k == KC - 1))
                last.then_inc(s["cs_mm_done"], 1)
                pe.wait_ge(s["cs_split"], 1)
                pe.wait_ge(s["enc_split"], 1)
                pe.wait_ge(s["vd_ready"], 1)
                pe.wait_ge(s["wa_split_ready"], 1)
                for k in range(KC):
                    if k >= 2:
                        pe.wait_ge(s["k_sum_ready"], k - 1)
                    for h in range(2):
                        c = slice(h * HALF, (h + 1) * HALF)
                        e = slice(k * P, (k + 1) * P)
                        last = product3(pe, kpair[k % 2][:, c], enc_hi[:, e], enc_lo[:, e],
                                        cs_hi[:, c], cs_lo[:, c], True, True)
                    last.then_inc(s["k_mm_done"], 1)
                    var_mm(pe, v, 8 + k, k % 4)

            @block.vector
            def _(dve):
                spacer = g["spacer"][:]
                chain = [0]

                def link(ins):
                    chain[0] += 1
                    ins.then_inc(s["s_chain"], 1)
                    dve.wait_ge(s["s_chain"], chain[0])

                dve.wait_ge(s["w_in"], 32)
                id_b = g["ident"][0:CH, 0:CH].unsqueeze(1).broadcast_to([CH, NCOND, CH])
                dve.tensor_tensor(w_plus[:], w_raw[:], id_b, ALU.add).then_inc(s["w_plus_ready"], 1)
                dve.wait_ge(s["wtw_mm_done"], 1)
                dve.tensor_copy(wtw[:], small[0:BOT, 0:2 * BOT]).then_inc(s["wtw_ready"], 1)
                dve.wait_ge(s["g_mm_done"], 1)
                dve.tensor_scalar(router[:, 0:NSLOT], small[:, 0:NSLOT], float(RDIM) ** -0.5, None, ALU.mult)
                link(dve.tensor_scalar(router[:, NSLOT:], keys[:], float(BOT) ** -0.5, None, ALU.mult))
                link(dve.tensor_copy(g["router_a"][:], router[:]))
                dve.wait_ge(s["zeroed"], 1)
                dve.tensor_tensor(g["router_b"][0:BOT, :], router[0:BOT, :], f(g["router_a"][0:BOT, :]),
                                  ALU.subtract).then_inc(s["router_ready"], 1)
                dve.wait_ge(s["logrel_in"], 16)
                link(dve.tensor_copy(logrel_hi[:], logrel[:]))
                dve.tensor_tensor(logrel_lo[:], logrel[:], f(logrel_hi[:]), ALU.subtract
                                  ).then_inc(s["logrel_split"], 1)
                dve.wait_ge(s["coefs_in"], 32)
                link(dve.tensor_tensor(coefs[:], coefs[:], masks[:].bitcast(U8), ALU.mult))
                link(dve.tensor_tensor(coefs[:, 0, :], coefs[:, 0, :], coefs[:, 1, :], ALU.add))
                dve.tensor_tensor(coefs[:, 0, :], coefs[:, 0, :], coefs[:, 2, :], ALU.add
                                  ).then_inc(s["wsum_ready"], 1)
                for n in range(2 * LBLK):
                    var_stats(dve, spacer, g, v, n, n % 4)
                dve.wait_ge(s["wa_mm_done"], LBLK)
                wa3 = wa_bank.rearrange("p (l r) -> p l r", r=RANK)
                link(dve.tensor_copy(wa_split[:, :, 0, :], wa3))
                dve.tensor_tensor(wa_split[:, :, 1, :], wa3, f(wa_split[:, :, 0, :]), ALU.subtract
                                  ).then_inc(s["wa_split_ready"], 1)
                dve.wait_ge(s["vd_mm_done"], 1)
                dve.tensor_copy(g["vd"][:], small[:, 0:2 * BOT].rearrange("p (b v) -> p b v", b=2)
                                ).then_inc(s["vd_ready"], 1)
                dve.wait_ge(s["cs_hi_ready"], 1)
                dve.scalar_tensor_tensor(cs_lo[:], pair[2][0:RENC, :], 0.5, f(cs_hi[:]), ALU.mult,
                                         ALU.subtract).then_inc(s["cs_split"], 1)
                dve.wait_ge(s["wbase_in"], 16 * KC)
                for k in range(KC):
                    dve.wait_ge(s["k_mm_done"], k + 1)
                    dve.tensor_tensor(kf[:, k, :], kf[:, k, :], kpair[k % 2][:, :], ALU.add
                                      ).then_inc(s["k_sum_ready"], 1)
                    var_stats(dve, spacer, g, v, 8 + k, k % 4)
    return k_hi, k_lo



def fold_block(nc, t, g, v, pair, sem, tile, k_hi, k_lo, m_hi, m_lo):
    with ExitStack() as st:
        blk_raw = tile(st, "blk_raw", [P, KC, P])
        blk_hi = tile(st, "blk_hi", [P, 2, KC, P], F32R)
        blk_lo = tile(st, "blk_lo", [P, 2, KC, P], F32R)
        bk_hi = tile(st, "bk_hi_sb", [P, HID], F32R)
        bk_lo = tile(st, "bk_lo_sb", [P, HID], F32R)
        bb = tile(st, "bb", [P, KC])
        b_base = tile(st, "b_base", [1, HID])
        u = {n: tile(st, "lv_" + n, [P, NT]) for n in ("u", "d", "m", "ln", "num", "log")}
        col = tile(st, "col", [P, 4])
        part = v["v_x"]
        const_hi, const_lo = v["v_hi"], v["v_lo"]

        names = ("raw_loaded bhi_ready blo_ready blk_done evac_hi_ready banks_free bk_stored bias_in "
                 "f_chain lnu_ready lsum_in mean_done part_ready const_mm_done const_hi_ready "
                 "const_ready const_stored diag_chain").split()
        s = {n: sem(n) for n in names}
        zpair = pair[2:4]
        NM = KC
        per = VAR_M // NM

        with nc.Block() as block:

            @block.sync
            def _(sp):
                sp.dma_start(bb[:], t["cond_bias"]).then_inc(s["bias_in"], 16)
                sp.dma_start(b_base[:], t["b_base"]).then_inc(s["bias_in"], 16)

                def load_block(b):
                    off = b * (P * HID) if isinstance(b, int) else sp.snap(b * (P * HID))
                    if known_positive(b):
                        sp.wait_ge(s["blo_ready"], b if isinstance(b, int) else split)
                    sp.dma_start(blk_raw[:], bass.AP(t["left_blocks"].tensor, off, [[HID, P], [P, KC], [1, P]])
                                 ).then_inc(s["raw_loaded"], 16)

                def var_loads(b):
                    for q in range(per):
                        var_load(sp, t, g, v, b * per + (VAR_A + q), q)

                load_block(0)
                with sp.Fori(0, NM + LBLK - 1) as b:
                    split = sp.snap(b + 1)
                    load_block(b + 1)
                    var_loads(b)
                var_loads(NM + LBLK - 1)

            @block.scalar
            def _(act):
                def block_hi(b, i):
                    act.wait_ge(s["raw_loaded"], b * 16 + 16)
                    act.copy(blk_hi[:, i], blk_raw[:]).then_inc(s["bhi_ready"], 1)

                def row_hi(b, q):
                    var_hi(act, v, b * per + (VAR_A + q), q % per)

                def one(b, i, evac, last=False):
                    row_hi(b, 1)
                    row_hi(b, 2)
                    if not last:
                        block_hi(b + 1, 1 - i)
                    row_hi(b, 3)
                    if not last:
                        row_hi(b, 4)
                    act.wait_ge(s["blk_done"], b + 1)
                    evac(zpair[i])

                def evac_m(b):
                    def go(z):
                        act.copy(m_hi[:, bass.ds(b, 1), :].rearrange("p a n -> p (a n)"), z[:]
                                 ).then_inc(s["evac_hi_ready"], 1)
                    return go

                def evac_bk(b):
                    def go(z):
                        if b > NM:
                            act.wait_ge(s["bk_stored"], (b - NM) * 32)
                        act.copy(bk_hi[:], z[:]).then_inc(s["evac_hi_ready"], 1)
                    return go

                block_hi(0, 0)
                row_hi(0, 0)
                with act.Fori(0, NM // 2) as j:
                    b = j * 2
                    one(b, 0, evac_m(b))
                    one(b + 1, 1, evac_m(b + 1))
                for b in range(NM, NM + LBLK):
                    one(b, b % 2, evac_bk(b), b == NM + LBLK - 1)
                act.wait_ge(s["f_chain"], 1)
                act.activation(u["ln"][:], u["u"][:], ACT.Ln).then_inc(s["lnu_ready"], 1)
                act.wait_ge(s["const_mm_done"], 1)
                act.wait_ge(s["bias_in"], 32)

            @block.gpsimd
            def _(pool):
                def row_lo(b, q):
                    var_lo(pool, v, b * per + (VAR_A + q), q % per)

                def split(b, i):
                    ready = b + 1 if isinstance(b, int) else pool.snap(b + 1)
                    pool.wait_ge(s["bhi_ready"], ready)
                    pool.tensor_tensor(blk_lo[:, i], blk_raw[:], f(blk_hi[:, i]), ALU.subtract
                                       ).then_inc(s["blo_ready"], 1)

                def one(b, i, last=False):
                    row_lo(b, 1)
                    row_lo(b, 2)
                    if not last:
                        split(b + 1, 1 - i)
                    row_lo(b, 3)
                    if not last:
                        row_lo(b, 4)

                split(0, 0)
                row_lo(0, 0)
                with pool.Fori(0, NM // 2) as j:
                    b = j * 2
                    one(b, 0)
                    one(b + 1, 1)

                def store(b):
                    rows = (b - NM) * (P * HID)
                    pool.wait_ge(s["banks_free"], b + 3)
                    pool.dma_start(bass.AP(t["bk_hi"].tensor, rows, [[HID, P], [1, HID]]), f(bk_hi[:])
                                   ).then_inc(s["bk_stored"], 16)
                    pool.dma_start(bass.AP(t["bk_lo"].tensor, rows, [[HID, P], [1, HID]]), f(bk_lo[:])
                                   ).then_inc(s["bk_stored"], 16)

                for b in range(NM, NM + LBLK):
                    one(b, b % 2, b == NM + LBLK - 1)
                    store(b)
                pool.wait_ge(s["bk_stored"], 32 * LBLK)
                pool.wait_ge(s["const_ready"], 1)
                pool.dma_start(t["const_split"][0:1, :], f(const_hi[0:1, 0, :])).then_inc(s["const_stored"], 16)
                pool.dma_start(t["const_split"][1:2, :], f(const_lo[0:1, 0, :])).then_inc(s["const_stored"], 16)
                pool.wait_ge(s["const_stored"], 32)

            @block.tensor
            def _(pe):
                def one(b, i):
                    pe.wait_ge(s["blo_ready"], b + 1)
                    pe.wait_ge(s["banks_free"], b + 1)
                    z = zpair[i]
                    for q in range(per):
                        h, k0 = q // 2, (q % 2) * (KC // 2)
                        c = slice(h * HALF, (h + 1) * HALF)
                        for k in range(k0, k0 + KC // 2):
                            last = product3(pe, z[:, c], blk_hi[:, i, k, :], blk_lo[:, i, k, :],
                                            k_hi[:, k, c], k_lo[:, k, c], k == 0, k == KC - 1)
                        if q == per - 1:
                            last.then_inc(s["blk_done"], 1)
                        var_mm(pe, v, b * per + (VAR_A + q), q)

                with pe.Fori(0, NM // 2) as j:
                    b = j * 2
                    one(b, 0)
                    one(b + 1, 1)
                with pe.Fori(0, LBLK // 2) as j:
                    b = j * 2 + NM
                    one(b, 0)
                    one(b + 1, 1)
                pe.wait_ge(s["lsum_in"], 1)
                pe.matmul(pair[0][:, 0:1], g["ones"][:], col[:, 0:1], start=True, stop=True
                          ).then_inc(s["mean_done"], 1)
                pe.wait_ge(s["part_ready"], 1)
                for h in range(2):
                    c = slice(h * HALF, (h + 1) * HALF)
                    last = pe.matmul(pair[1][0:1, c], g["ones"][:, 0:1], part[:, 0, c], start=True, stop=True)
                last.then_inc(s["const_mm_done"], 1)

            @block.vector
            def _(dve):
                spacer = g["spacer"][:]
                chain = [0]

                def link(ins):
                    chain[0] += 1
                    ins.then_inc(s["f_chain"], 1)
                    dve.wait_ge(s["f_chain"], chain[0])

                def one(b, i, lo_dst, guard=None):
                    for q in range(per):
                        var_stats(dve, spacer, g, v, b * per + (VAR_A + q), q)
                    dve.wait_ge(s["evac_hi_ready"], b + 1)
                    src, hi = lo_dst
                    dve.tensor_tensor(src, zpair[i][:], f(hi), ALU.subtract).then_inc(s["banks_free"], 1)

                def m_dst(b):
                    a = m_lo[:, bass.ds(b, 1), :].rearrange("p a n -> p (a n)")
                    h = m_hi[:, bass.ds(b, 1), :].rearrange("p a n -> p (a n)")
                    return a, h

                dve.memset(col[:], 0.0).then_inc(s["banks_free"], 2)
                with dve.Fori(0, NM // 2) as j:
                    b = j * 2
                    one(b, 0, m_dst(b))
                    one(b + 1, 1, m_dst(b + 1))
                with dve.Fori(0, LBLK // 2) as j:
                    b = j * 2 + NM
                    one(b, 0, (bk_lo[:], bk_hi[:]))
                    one(b + 1, 1, (bk_lo[:], bk_hi[:]))

                var = g["var"][:]
                dve.wait_ge(v["v_var_ready"], NT)
                link(dve.tensor_scalar(u["u"][:], var, 1.0, None, ALU.add))
                link(dve.tensor_scalar(u["d"][:], u["u"][:], -1.0, None, ALU.add))
                link(dve.tensor_scalar(u["m"][:], u["d"][:], 0.0, None, ALU.is_equal))
                link(dve.tensor_tensor(u["d"][:], u["d"][:], u["m"][:], ALU.add))
                link(dve.reciprocal(u["d"][:], u["d"][:]))
                dve.wait_ge(s["lnu_ready"], 1)
                link(dve.tensor_tensor(u["num"][:], u["ln"][:], u["m"][:], ALU.add))
                link(dve.tensor_tensor(u["num"][:], u["num"][:], u["d"][:], ALU.mult))
                link(dve.tensor_tensor(u["log"][:], u["num"][:], var, ALU.mult))
                dve.tensor_reduce(col[:, 0:1], u["log"][:], AX.X, ALU.add).then_inc(s["lsum_in"], 1)
                dve.wait_ge(s["bias_in"], 32)
                for k in range(KC):
                    for kk, src in ((0, k_hi), (1, k_lo)):
                        if k == 0 and kk == 0:
                            link(dve.tensor_scalar(part[:, 0, :], f(src[:, k, :]), bb[:, k:k + 1], None, ALU.mult))
                        else:
                            link(dve.scalar_tensor_tensor(part[:, 0, :], f(src[:, k, :]), bb[:, k:k + 1],
                                                          part[:, 0, :], ALU.mult, ALU.add))
                dve.tensor_tensor(part[0:1, 0, :], part[0:1, 0, :], b_base[:], ALU.add
                                  ).then_inc(s["part_ready"], 1)
                dve.wait_ge(s["mean_done"], 1)
                link(dve.tensor_scalar(col[:, 1:2], pair[0][:, 0:1], 1.0 / (NT * P), 1e-6, ALU.mult, ALU.add))
                link(dve.reciprocal(col[:, 2:3], col[:, 1:2]))
                link(dve.tensor_scalar(u["num"][:], u["log"][:], col[:, 2:3], 0.5, ALU.mult, ALU.mult))
                link(dve.tensor_scalar(g["norm_var"][:], u["num"][:], 1.25, None, ALU.add))
                dve.wait_ge(s["const_mm_done"], 1)
                link(dve.tensor_copy(const_hi[0:1, 0, :], pair[1][0:1, :]))
                dve.tensor_tensor(const_lo[0:1, 0, :], pair[1][0:1, :], f(const_hi[0:1, 0, :]), ALU.subtract
                                  ).then_inc(s["const_ready"], 1)



def main_block(nc, t, g, pair, sem, tile, m_hi, m_lo):
    with ExitStack() as st:
        b = {}
        for name, shape, dt in (
            ("narrow", [P, 2 + NUG + NQG + 2, 2, KC, GRP], F32R),
            ("xt", [P, 2, HID], F32), ("xt_hi", [P, 2, HID], F32R), ("xt_lo", [P, 2, HID], F32R),
            ("pm_hi", [P, HID], F32R), ("pm_lo", [P, HID], F32R),
            ("pa_hi", [P, 2, PAW], F32R), ("pa_lo", [P, 2, PAW], F32R),
            ("out_sb", [P, 2, HID], F32),
            ("rhs_a", [P, HID], F32R), ("rhs_b", [P, 2, HID], F32R), ("rhs_c", [P, 2, HID], F32R),
            ("bd", [P, 2, 4, P], F32R), ("wa", [P, 2, 2, 2, RANK], F32R),
            ("lhs_a", [P, P], F32R), ("lhs_b", [P, P], F32R), ("lhs_c", [P, P], F32R),
            ("query", [P, P], F32R), ("q_a", [P, P], F32R), ("q_b", [P, P], F32R),
            ("u_sb", [P, P], F32R), ("e_t", [P, 2, P], F32), ("hm", [2 * RANK, P], F32),
            ("z", [P, NUNC], F32), ("z2", [P, NUNC], F32),
            ("arg", [P, NUNC], F32), ("th", [P, NUNC], F32), ("gelu", [P, NUNC], F32), ("dot", [P, NUNC], F32),
            ("bu1", [P, NUNC], F32), ("wu2", [P, NUNC], F32),
            ("rest", [P, NSLOT], F32), ("penalty", [P, NSLOT], F32), ("logits", [P, NSLOT], F32),
            ("probs", [P, NSLOT], F32),
            ("top8", [P, 8], F32), ("col", [P, 16], F32), ("gates", [P, 8], F32),
        ):
            b[name] = tile(st, "t_" + name, shape, dt)

        def wu_raw():
            return b["out_sb"][:].rearrange("p a (g c) -> p (a g) c", c=KC * GRP)

        def wq_raw(half):
            return b[("probs", "logits")[half]][:].rearrange("p (g c) -> p g c", c=KC * GRP)

        def wu_groups(part):
            return b["narrow"][:, 2:2 + NUG, part].rearrange("p g k r -> p g (k r)")

        def wq_groups(half, part):
            first = 2 + NUG + half * (NQG // 2)
            return b["narrow"][:, first:first + NQG // 2, part].rearrange("p g k r -> p g (k r)")

        col = b["col"]
        ROWMAX, NEGMAX, ESUM, LSUM, LTANH, UNC, CLIP, SCALED, UNORM, GTANH, GATE, GATED, RSUM, SCALE = range(14)

        def c1(n):
            return col[:, n:n + 1]

        HQ = (slice(2 * RANK, PAW), slice(0, HQW))
        LORA = (slice(0, 2 * RANK), slice(HQW, PAW))
        A_GROUP = (0, 2 + NUG + NQG)

        out_ps = pair[0]
        pm_ps = pair[1]
        pa_ps = pair[2][:, 0:HALF]
        mix_ps = pair[2][:, HALF:HID]
        score_ps = pair[3][:, 0:HALF]
        misc_ps = pair[3][:, HALF:HID]

        loaded = {n: [sem(f"{n}_loaded{p}") for p in range(2)] for n in ("xt", "lora")}
        moved = [sem(f"out_slot_moved{p}") for p in range(2)]
        names = ("wq_in row_in gate_in const_in wu_hi_ready wu_split wq_hi_ready wq_split cleared "
                 "diag_ready v_mm_ready va_ready vb_ready gates_ready m_chain "
                 "xhi_ready xlo_ready s1a_done s1b_done mixq_done qt_done score_done et_done u_done ut_done "
                 "h_done out_done pa_hi_ready pa_lo_ready pm_hi0_ready pm_hi1_ready pm_lo0_ready pm_lo1_ready "
                 "q_hi_ready q_split z_ready z2_ready arg_ready tanh_ready gelu_ready lsum_ready "
                 "ltanh_ready unc_ready clip_ready scaled_ready unorm_ready gtanh_ready gate_ready gated_ready "
                 "qt_ready top8_ready rest_ready penalty_ready logits_ready negmax_ready exp_ready rsum_ready "
                 "scale_ready et_ready uhi_ready u_split ut_ready hm_ready hhi_ready h_ready out_ready").split()
        s = {n: sem("m_" + n) for n in names}
        LPT = 16 * 12

        with nc.Block() as block:

            @block.sync
            def _(sp):
                for p in range(2):
                    sp.dma_start(b["out_sb"][:, p, :], t["wu1_t"][:, p, :]).then_inc(moved[p], 16)
                sp.dma_start(b["probs"][:], t["wq_t"][:, 0:NSLOT]).then_inc(s["wq_in"], 16)
                sp.dma_start(b["logits"][:], t["wq_t"][:, NSLOT:]).then_inc(s["wq_in"], 16)
                sp.dma_start(b["bu1"][:], t["bu1"]).then_inc(s["row_in"], 16)
                sp.dma_start(b["wu2"][:], t["wu2"]).then_inc(s["row_in"], 16)
                sp.dma_start(b["gates"][:, 0:3], t["gate_params"]).then_inc(s["gate_in"], 16)

                def load_x(i, p):
                    off = sp.snap(i * (P * HID)) if not isinstance(i, int) else i * P * HID
                    split = sp.snap(i - 1) if not isinstance(i, int) else i - 1
                    if known_positive(split):
                        sp.wait_ge(s["xlo_ready"], split)
                    sp.dma_start(b["xt"][:, p, :], bass.AP(t["x_t"].tensor, off, [[HID, P], [1, HID]])
                                 ).then_inc(loaded["xt"][p], 16)

                def load_picked(i, p):
                    used = sp.snap(i - 1) if not isinstance(i, int) else i - 1
                    cond = [sp.value_load(g["cond_ids"][:, bass.ds(i * 2 + n, 1)], min_val=0,
                                          max_val=NCOND - 1) for n in range(2)]
                    lora = [sp.value_load(g["lora_ids"][:, bass.ds(i * 2 + n, 1)], min_val=0,
                                          max_val=NLORA - 1) for n in range(2)]
                    w_off = [sp.snap(c * (CH * 4 * CH)) for c in cond]
                    a_off = [sp.snap(c * (P * 2 * KC * RANK)) for c in lora]
                    wa_off = [sp.snap(c * (P * 2 * RANK)) for c in lora]
                    bk_off = [sp.snap(c * (RANK * HID)) for c in lora]
                    if known_positive(used):
                        sp.wait_ge(s["out_done"], used)
                    done = loaded["lora"][p]
                    for n in range(2):
                        rows = slice(n * CH, (n + 1) * CH)
                        sp.dma_start(f(b["bd"][rows, p, :, rows]),
                                     bass.AP(t["w_kinds"].tensor, w_off[n], [[4 * CH, CH], [CH, 4], [1, CH]])
                                     ).then_inc(done, 16)
                        sp.dma_start(f(b["narrow"][:, A_GROUP[p] + n]),
                                     bass.AP(t["a_split"].tensor, a_off[n], [[2 * KC * RANK, P], [1, 2 * KC * RANK]])
                                     ).then_inc(done, 16)
                        sp.dma_start(f(b["wa"][:, p, :, n, :]),
                                     bass.AP(t["wa_split"].tensor, wa_off[n], [[2 * RANK, P], [RANK, 2], [1, RANK]])
                                     ).then_inc(done, 16)
                        bk_h = bass.AP(t["bk_hi"].tensor, bk_off[n], [[HID, RANK], [1, HID]])
                        bk_l = bass.AP(t["bk_lo"].tensor, bk_off[n], [[HID, RANK], [1, HID]])
                        for base, dst, src in ((BOT, "rhs_b", bk_h), (BOT + 2 * RANK, "rhs_b", bk_h),
                                               (0, "rhs_c", bk_l)):
                            r0 = base + n * RANK
                            sp.dma_start(f(b[dst][r0:r0 + RANK, p, :]), src).then_inc(done, 16)

                def store(j, p):
                    off = sp.snap(j * (P * HID)) if not isinstance(j, int) else j * P * HID
                    ready = sp.snap(j + 1) if not isinstance(j, int) else j + 1
                    sp.wait_ge(s["out_ready"], ready)
                    sp.dma_start(bass.AP(t["out"].tensor, off, [[HID, P], [1, HID]]), b["out_sb"][:, p, :]
                                 ).then_inc(moved[p], 16)

                load_x(0, 0)
                for p in range(2):
                    sp.dma_start(f(b["rhs_c"][2 * RANK:2 * RANK + 2, p, :]), t["const_split"]
                                 ).then_inc(s["const_in"], 16)
                sp.wait_ge(s["cleared"], 1)
                load_x(1, 1)
                load_picked(0, 0)
                load_x(2, 0)
                load_picked(1, 1)
                with sp.Fori(0, NT // 2 - 2) as j:
                    i = j * 2 + 2
                    load_x(i + 1, 1)
                    load_picked(i, 0)
                    store(i - 2, 0)
                    load_x(i + 2, 0)
                    load_picked(i + 1, 1)
                    store(i - 1, 1)
                load_x(NT - 1, 1)
                load_picked(NT - 2, 0)
                store(NT - 4, 0)
                load_picked(NT - 1, 1)
                store(NT - 3, 1)
                store(NT - 2, 0)
                store(NT - 1, 1)
                for p in range(2):
                    sp.wait_ge(moved[p], 16 * (NT // 2 + 1))

            def steps(eng, step):
                step(0, 0)
                with eng.Fori(0, NT // 2 - 1) as j:
                    n = j * 2 + 1
                    step(n, 1)
                    step(n + 1, 0)
                step(NT - 1, 1)
                step(NT, 0)

            def has_new(n):
                return not isinstance(n, int) or n < NT

            def has_old(n):
                return not isinstance(n, int) or n > 0

            def arrived(n, p, each):
                return (n - p) * (each // 2) + each

            @block.scalar
            def _(act):
                for p in range(2):
                    act.wait_ge(moved[p], 16)
                act.copy(wu_groups(0), wu_raw()).then_inc(s["wu_hi_ready"], 1)
                act.wait_ge(s["wq_in"], 32)
                act.copy(wq_groups(0, 0), wq_raw(0))
                act.copy(wq_groups(1, 0), wq_raw(1)).then_inc(s["wq_hi_ready"], 1)

                def split_x(i, p):
                    act.wait_ge(loaded["xt"][p], arrived(i, p, 16))
                    if known_positive(i - 1):
                        act.wait_ge(s["s1b_done"], i - 1)
                    act.copy(b["xt_hi"][:, p, :], b["xt"][:, p, :]).then_inc(s["xhi_ready"], 1)

                split_x(0, 0)
                act.wait_ge(s["v_mm_ready"], 1)
                act.copy(b["rhs_a"][:], out_ps[:]).then_inc(s["va_ready"], 1)
                act.wait_ge(s["gates_ready"], 1)

                def step(n, p):
                    if has_old(n):
                        act.wait_ge(s["s1b_done"], n)
                        act.copy(b["pm_hi"][:, 0:HALF], pm_ps[:, 0:HALF]).then_inc(s["pm_hi0_ready"], 1)
                        act.copy(b["pm_hi"][:, HALF:], pm_ps[:, HALF:]).then_inc(s["pm_hi1_ready"], 1)
                        act.wait_ge(s["ut_done"], n)
                        act.copy(b["lhs_a"][:], misc_ps[:, 0:P])
                        act.copy(b["lhs_b"][0:BOT, :], misc_ps[0:BOT, 0:P]).then_inc(s["ut_ready"], 1)
                    if has_new(n):
                        act.wait_ge(s["s1a_done"], n + 1)
                        act.copy(b["pa_hi"][:, p, :], pa_ps[:, 0:PAW]).then_inc(s["pa_hi_ready"], 1)
                    if not isinstance(n, int) or n + 1 < NT:
                        split_x(n + 1, 1 - p)
                    if has_old(n):
                        act.wait_ge(s["out_done"], n)
                        act.wait_ge(moved[1 - p], arrived(n - 1, 1 - p, 16))
                        act.copy(b["out_sb"][:, 1 - p, :], out_ps[:]).then_inc(s["out_ready"], 1)
                    if has_new(n):
                        act.wait_ge(s["qt_done"], n + 1)
                        act.copy(b["q_a"][:], misc_ps[:, 0:P])
                        act.copy(b["q_b"][0:BOT, :], misc_ps[0:BOT, 0:P]).then_inc(s["qt_ready"], 1)
                        act.wait_ge(s["z_ready"], n + 1)
                        act.activation(b["z2"][:], b["z"][:], ACT.Square, scale=0.044715 ** 0.5
                                       ).then_inc(s["z2_ready"], 1)
                        act.wait_ge(s["arg_ready"], n + 1)
                        act.activation(b["th"][:], b["arg"][:], ACT.Tanh, scale=TANH_C
                                       ).then_inc(s["tanh_ready"], 1)
                        act.wait_ge(s["negmax_ready"], n + 1)
                        act.activation(b["probs"][:], b["logits"][:], ACT.Exp, bias=c1(NEGMAX),
                                       accum_out=c1(ESUM)).then_inc(s["exp_ready"], 1)
                        act.wait_ge(s["et_done"], n + 1)
                        act.copy(b["e_t"][:].rearrange("p c n -> p (c n)"), misc_ps[:, P:3 * P]
                                 ).then_inc(s["et_ready"], 1)
                        act.wait_ge(s["lsum_ready"], n + 1)
                        act.activation(c1(LTANH), c1(LSUM), ACT.Tanh, scale=0.25, bias=b["gates"][:, 3:4]
                                       ).then_inc(s["ltanh_ready"], 1)
                        act.wait_ge(s["ltanh_ready"], n + 1)
                        act.activation(c1(UNC), c1(LTANH), ACT.Identity, scale=1.25,
                                       bias=g["norm_var"][:, bass.ds(n, 1)]).then_inc(s["unc_ready"], 1)
                        act.wait_ge(s["unorm_ready"], n + 1)
                        act.activation(c1(GTANH), c1(UNORM), ACT.Tanh, scale=b["gates"][:, 4:5],
                                       bias=b["gates"][:, 5:6]).then_inc(s["gtanh_ready"], 1)

                steps(act, step)

            @block.gpsimd
            def _(pool):
                pool.memset(f(b["bd"][:]), 0.0).then_inc(s["cleared"], 1)
                pool.wait_ge(s["wu_hi_ready"], 1)
                pool.tensor_tensor(wu_groups(1), wu_raw(), f(wu_groups(0)), ALU.subtract
                                   ).then_inc(s["wu_split"], 1)

                def split_x(i, p):
                    ready = i + 1 if isinstance(i, int) else pool.snap(i + 1)
                    pool.wait_ge(s["xhi_ready"], ready)
                    pool.tensor_tensor(b["xt_lo"][:, p, :], b["xt"][:, p, :], f(b["xt_hi"][:, p, :]),
                                       ALU.subtract).then_inc(s["xlo_ready"], 1)

                split_x(0, 0)

                def step(n, p):
                    if not isinstance(n, int) or n + 1 < NT:
                        split_x(n + 1, 1 - p)

                steps(pool, step)

            @block.tensor
            def _(pe):
                pe.wait_ge(s["diag_ready"], 1)
                for h in range(2):
                    c = slice(h * HALF, (h + 1) * HALF)
                    for k in range(KC):
                        last = product3(pe, out_ps[:, c], g["wvu_hi"][:, k, :], g["wvu_lo"][:, k, :],
                                        m_hi[:, k, c], m_lo[:, k, c], k == 0, k == KC - 1)
                last.then_inc(s["v_mm_ready"], 1)
                pe.wait_ge(s["wu_split"], 1)
                pe.wait_ge(s["wq_split"], 1)
                pe.wait_ge(s["cleared"], 1)
                pe.wait_ge(s["const_in"], 32)
                pe.wait_ge(s["vb_ready"], 1)

                def step(n, p):
                    o = 1 - p
                    if has_new(n):
                        pe.wait_ge(s["xlo_ready"], n + 1)
                        pe.wait_ge(loaded["lora"][p], arrived(n, p, LPT))
                        if known_positive(n):
                            pe.wait_ge(s["pa_lo_ready"], n)
                    for k in range(KC):
                        if has_new(n):
                            x_h = b["xt_hi"][:, p, k * P:(k + 1) * P]
                            x_l = b["xt_lo"][:, p, k * P:(k + 1) * P]
                            g0 = 2 * p
                            n_h, n_l = (b["narrow"][:, g0:g0 + 2 + NUG + NQG, part, k, :] for part in range(2))
                            last = product3(pe, pa_ps[:, 0:PAW], x_h, x_l, n_h, n_l, k == 0, k == KC - 1)
                            if k == KC - 1:
                                last.then_inc(s["s1a_done"], 1)
                        if not has_old(n):
                            continue
                        if k == 0:
                            pe.wait_ge(s["et_ready"], n)
                            for c in range(2):
                                last = pe.matmul(misc_ps[:, 3 * P:3 * P + BOT], b["e_t"][:, c, :], g["vd"][:, c, :],
                                                 start=(c == 0), stop=(c == 1))
                            last.then_inc(s["u_done"], 1)
                        if k == 4:
                            pe.wait_ge(s["u_split"], n)
                            pe.transpose(misc_ps[:, 0:P], f(b["u_sb"][:]), g["ident"][:]).then_inc(s["ut_done"], 1)
                        if k == KC - 1:
                            pe.wait_ge(s["ut_ready"], n)
                            lo_ps = misc_ps[0:2 * RANK, P:2 * P]
                            w_h, w_l = b["bd"][:, o, 2, :], b["bd"][:, o, 3, :]
                            product3(pe, lo_ps, b["pa_hi"][:, o, LORA[o]], b["pa_lo"][:, o, LORA[o]],
                                     w_h, w_l, True, False)
                            pe.matmul(lo_ps, b["wa"][:, o, 0].rearrange("p n r -> p (n r)"), b["lhs_a"][:], start=False, stop=False)
                            pe.matmul(lo_ps, b["wa"][0:BOT, o, 1].rearrange("p n r -> p (n r)"), b["lhs_b"][0:BOT, :], start=False,
                                      stop=True).then_inc(s["h_done"], 1)
                    if has_old(n):
                        pe.wait_ge(s["pm_lo1_ready"], n)
                        w_h, w_l = b["bd"][:, o, 2, :], b["bd"][:, o, 3, :]
                        cs = [slice(0, HALF), slice(HALF, HID)]
                        for lhs, rhs, start in ((w_h, "pm_hi", True), (w_h, "pm_lo", False), (w_l, "pm_hi", False)):
                            for c in cs:
                                pe.matmul(out_ps[:, c], lhs, b[rhs][:, c], start=start, stop=False)
                        pe.wait_ge(s["h_ready"], n)
                        nc_rows = 2 * RANK + 2
                        for lhs, rhs, end in ((b["lhs_a"][:], b["rhs_a"][:], False),
                                              (b["lhs_b"][:], b["rhs_b"][:, o, :], False),
                                              (b["lhs_c"][0:nc_rows, :], b["rhs_c"][0:nc_rows, o, :], True)):
                            for c in cs:
                                last = pe.matmul(out_ps[:, c], lhs, rhs[:, c], start=False, stop=end)
                        last.then_inc(s["out_done"], 1)
                    if has_new(n):
                        pe.wait_ge(s["pa_lo_ready"], n + 1)
                        if known_positive(n):
                            pe.wait_ge(s["z_ready"], n)
                        product3(pe, mix_ps[:, 0:HQW], b["bd"][:, p, 0, :], b["bd"][:, p, 1, :],
                                 b["pa_hi"][:, p, HQ[p]], b["pa_lo"][:, p, HQ[p]],
                                 True, True).then_inc(s["mixq_done"], 1)
                        if known_positive(n):
                            pe.wait_ge(s["pm_lo1_ready"], n)
                        for k in range(KC):
                            x_h = b["xt_hi"][:, p, k * P:(k + 1) * P]
                            x_l = b["xt_lo"][:, p, k * P:(k + 1) * P]
                            first, end = k == 0, k == KC - 1
                            for lhs, m, a, z in ((x_h, m_hi, first, False), (x_h, m_lo, False, False),
                                                 (x_l, m_hi, False, end)):
                                for h in range(2):
                                    c = slice(h * HALF, (h + 1) * HALF)
                                    last = pe.matmul(pm_ps[:, c], lhs, m[:, k, c], start=a, stop=z)
                            if end:
                                last.then_inc(s["s1b_done"], 1)
                            if k == 0:
                                pe.wait_ge(s["q_split"], n + 1)
                                if known_positive(n):
                                    pe.wait_ge(s["hm_ready"], n)
                                pe.transpose(misc_ps[:, 0:P], f(b["query"][:]), g["ident"][:]
                                             ).then_inc(s["qt_done"], 1)
                            if k == 2:
                                pe.wait_ge(s["qt_ready"], n + 1)
                                if known_positive(n):
                                    pe.wait_ge(s["logits_ready"], n)
                                pe.matmul(score_ps, b["q_a"][:], g["router_a"][:], start=True, stop=False)
                                pe.matmul(score_ps, b["q_b"][0:BOT + 2, :], g["router_b"][0:BOT + 2, :],
                                          start=False, stop=True).then_inc(s["score_done"], 1)
                            if k == 6:
                                pe.wait_ge(s["exp_ready"], n + 1)
                                for c in range(2):
                                    last = pe.transpose(misc_ps[:, (c + 1) * P:(c + 2) * P],
                                                        b["probs"][:, c * P:(c + 1) * P], g["ident"][:])
                                last.then_inc(s["et_done"], 1)

                steps(pe, step)

            @block.vector
            def _(dve):
                spacer = g["spacer"][:]
                chain = [0]

                def link(ins):
                    chain[0] += 1
                    ins.then_inc(s["m_chain"], 1)
                    dve.wait_ge(s["m_chain"], chain[0])

                dve.memset(f(b["q_b"][BOT:P, :]), 1.0)
                dve.memset(f(b["lhs_c"][2 * RANK:BOT, :]), 1.0)
                for k in range(KC):
                    d = slice(k * P, (k + 1) * P)
                    tmp = b["rest"][:, 0:P] if k % 2 == 0 else b["rest"][:, P:2 * P]
                    link(dve.tensor_tensor(tmp, f(m_hi[:, k, d]), f(m_lo[:, k, d]), ALU.add))
                    link(dve.tensor_tensor(tmp, tmp, g["ident"][:], ALU.add))
                    link(dve.tensor_copy(m_hi[:, k, d], tmp))
                    link(dve.tensor_tensor(m_lo[:, k, d], tmp, f(m_hi[:, k, d]), ALU.subtract))
                dve.memset(b["top8"][:], 0.0).then_inc(s["diag_ready"], 1)
                dve.wait_ge(s["wq_hi_ready"], 1)
                for half in range(2):
                    last = dve.tensor_tensor(wq_groups(half, 1), wq_raw(half), f(wq_groups(half, 0)), ALU.subtract)
                last.then_inc(s["wq_split"], 1)
                dve.wait_ge(s["gate_in"], 16)
                dve.tensor_scalar(b["gates"][:, 3:6], b["gates"][:, 0:3], 0.5, None, ALU.mult
                                  ).then_inc(s["gates_ready"], 1)
                dve.wait_ge(s["va_ready"], 1)
                for p in range(2):
                    last = dve.tensor_tensor(b["rhs_b"][0:BOT, p, :], out_ps[0:BOT, :],
                                             f(b["rhs_a"][0:BOT, :]), ALU.subtract)
                last.then_inc(s["vb_ready"], 1)
                dve.wait_ge(s["row_in"], 32)

                def step(n, p):
                    if has_old(n):
                        dve.wait_ge(s["pm_hi0_ready"], n)
                        dve.tensor_tensor(b["pm_lo"][:, 0:HALF], pm_ps[:, 0:HALF], f(b["pm_hi"][:, 0:HALF]),
                                          ALU.subtract).then_inc(s["pm_lo0_ready"], 1)
                        u_ps = misc_ps[:, 3 * P:3 * P + BOT]
                        dve.wait_ge(s["u_done"], n)
                        dve.wait_ge(s["scale_ready"], n)
                        dve.tensor_scalar(b["u_sb"][:, 0:BOT], u_ps, c1(SCALE), None, ALU.mult
                                          ).then_inc(s["uhi_ready"], 1)
                        dve.wait_ge(s["uhi_ready"], n)
                        dve.scalar_tensor_tensor(b["u_sb"][:, BOT:], u_ps, c1(SCALE), f(b["u_sb"][:, 0:BOT]),
                                                 ALU.mult, ALU.subtract).then_inc(s["u_split"], 1)
                        dve.wait_ge(s["pm_hi1_ready"], n)
                        dve.tensor_tensor(b["pm_lo"][:, HALF:], pm_ps[:, HALF:], f(b["pm_hi"][:, HALF:]),
                                          ALU.subtract).then_inc(s["pm_lo1_ready"], 1)
                        dve.wait_ge(s["h_done"], n)
                        dve.tensor_tensor(b["hm"][:], misc_ps[0:2 * RANK, P:2 * P], g["lora_mask"][:], ALU.mult
                                          ).then_inc(s["hm_ready"], 1)
                        dve.wait_ge(s["hm_ready"], n)
                        dve.tensor_copy(b["lhs_c"][0:2 * RANK, :], b["hm"][:]).then_inc(s["hhi_ready"], 1)
                        dve.tensor_copy(b["lhs_b"][BOT:BOT + 2 * RANK, :], b["hm"][:])
                        dve.wait_ge(s["hhi_ready"], n)
                        dve.tensor_tensor(b["lhs_b"][BOT + 2 * RANK:, :], b["hm"][:], f(b["lhs_c"][0:2 * RANK, :]),
                                          ALU.subtract).then_inc(s["h_ready"], 1)
                    if has_new(n):
                        dve.wait_ge(s["pa_hi_ready"], n + 1)
                        dve.tensor_tensor(b["pa_lo"][:, p, :], pa_ps[:, 0:PAW], f(b["pa_hi"][:, p, :]),
                                          ALU.subtract).then_inc(s["pa_lo_ready"], 1)
                        q_ps = mix_ps[:, NUNC:NUNC + BOT]
                        dve.wait_ge(s["mixq_done"], n + 1)
                        dve.tensor_copy(b["query"][:, 0:BOT], q_ps).then_inc(s["q_hi_ready"], 1)
                        dve.wait_ge(s["q_hi_ready"], n + 1)
                        dve.tensor_tensor(b["query"][:, BOT:], q_ps, f(b["query"][:, 0:BOT]), ALU.subtract
                                          ).then_inc(s["q_split"], 1)
                        dve.tensor_tensor(b["z"][:], mix_ps[:, 0:NUNC], b["bu1"][:], ALU.add
                                          ).then_inc(s["z_ready"], 1)
                        dve.wait_ge(s["z2_ready"], n + 1)
                        dve.scalar_tensor_tensor(b["arg"][:], b["z2"][:], 1.0, b["z"][:], ALU.add, ALU.mult
                                                 ).then_inc(s["arg_ready"], 1)
                        wait_apart(dve, spacer, s["score_done"], n + 1)
                        dve.max(b["top8"][:], score_ps[:, 0:NSLOT]).then_inc(s["top8_ready"], 1)
                        wait_apart(dve, spacer, s["top8_ready"], n + 1)
                        dve.match_replace(b["rest"][:], b["top8"][:], score_ps[:, 0:NSLOT], REPLACED
                                          ).then_inc(s["rest_ready"], 1)
                        dve.wait_ge(s["rest_ready"], n + 1)
                        dve.tensor_scalar(b["penalty"][:], b["rest"][:], REPLACED, NEG, ALU.not_equal, ALU.mult
                                          ).then_inc(s["penalty_ready"], 1)
                        wait_apart(dve, spacer, s["penalty_ready"], n + 1)
                        dve.tensor_tensor_reduce(out=b["logits"][:], in0=b["penalty"][:],
                                                 in1=score_ps[:, NSLOT:2 * NSLOT], scale=1.0, scalar=-3.0e38,
                                                 op0=ALU.add, op1=ALU.max, accum_out=c1(ROWMAX)
                                                 ).then_inc(s["logits_ready"], 1)
                        dve.wait_ge(s["logits_ready"], n + 1)
                        dve.tensor_scalar(c1(NEGMAX), c1(ROWMAX), -1.0, None, ALU.mult
                                          ).then_inc(s["negmax_ready"], 1)
                        dve.wait_ge(s["tanh_ready"], n + 1)
                        dve.scalar_tensor_tensor(b["gelu"][:], b["th"][:], 1.0, b["z"][:], ALU.add, ALU.mult
                                                 ).then_inc(s["gelu_ready"], 1)
                        dve.wait_ge(s["gelu_ready"], n + 1)
                        dve.tensor_tensor_reduce(out=b["dot"][:], in0=b["gelu"][:], in1=b["wu2"][:], scale=1.0,
                                                 scalar=0.0, op0=ALU.mult, op1=ALU.add, accum_out=c1(LSUM)
                                                 ).then_inc(s["lsum_ready"], 1)
                        dve.wait_ge(s["exp_ready"], n + 1)
                        dve.reciprocal(c1(RSUM), c1(ESUM)).then_inc(s["rsum_ready"], 1)
                        dve.wait_ge(s["unc_ready"], n + 1)
                        dve.tensor_scalar(c1(CLIP), c1(UNC), 0.0, 5.0, ALU.max, ALU.min).then_inc(s["clip_ready"], 1)
                        dve.wait_ge(s["clip_ready"], n + 1)
                        dve.tensor_scalar(c1(SCALED), c1(CLIP), -0.5, 1.0 / 1.5, ALU.add, ALU.mult
                                          ).then_inc(s["scaled_ready"], 1)
                        dve.wait_ge(s["scaled_ready"], n + 1)
                        dve.tensor_scalar(c1(UNORM), c1(SCALED), 0.0, 1.0, ALU.max, ALU.min
                                          ).then_inc(s["unorm_ready"], 1)
                        dve.wait_ge(s["gtanh_ready"], n + 1)
                        dve.tensor_scalar(c1(GATE), c1(GTANH), 0.5, 0.5, ALU.mult, ALU.add).then_inc(s["gate_ready"], 1)
                        dve.wait_ge(s["gate_ready"], n + 1)
                        dve.scalar_tensor_tensor(c1(GATED), c1(GATE), 0.05, c1(GATE), ALU.is_ge, ALU.mult
                                                 ).then_inc(s["gated_ready"], 1)
                        dve.wait_ge(s["gated_ready"], n + 1)
                        dve.wait_ge(s["rsum_ready"], n + 1)
                        dve.tensor_tensor(c1(SCALE), c1(GATED), c1(RSUM), ALU.mult).then_inc(s["scale_ready"], 1)

                steps(dve, step)



def fourier_matrix(n):
    m = np.zeros((n, n))
    pos = np.arange(n)
    m[0] = n ** -0.5
    for fr in range(1, (n - 1) // 2 + 1):
        ang = 2 * np.pi * ((fr * pos) % n) / n
        m[2 * fr - 1] = np.sqrt(2.0 / n) * np.cos(ang)
        m[2 * fr] = np.sqrt(2.0 / n) * np.sin(ang)
    m[n - 1] = n ** -0.5 * (1 - 2 * (pos % 2))
    return m.astype(np.float32)


def kernel(**inputs):
    import concourse.bacc as bacc
    from concourse.bass_utils import run_bass_kernel_spmd

    a = {k: np.asarray(x) for k, x in inputs.items()}

    def chunks(m):
        return m.reshape(KC, P, -1).transpose(1, 0, 2)

    def groups(m):
        return m.T.reshape(KC, P, -1, GRP).transpose(1, 2, 0, 3).reshape(P, -1)

    x = a["x"].reshape(NT, P, HID)
    lora_a = a["L1_cond_lora_A_w"]
    lora_b = a["L1_cond_lora_B_w"]
    coefs = np.concatenate([a["L1_ffn_coefs0"], a["L1_ffn_coefs1"]], axis=2)
    masks = np.concatenate([a["L1_ffn_mask0"], a["L1_ffn_mask1"]], axis=2).view(np.uint8)

    def expert(m):
        return m.reshape(NEXP, KC, P, RENC).transpose(2, 0, 1, 3).reshape(P, NEXP, KC * RENC)

    rows = np.broadcast_to
    wvu = chunks(a["L0_ffn_Wvu"])
    data = {
        "x": x,
        "x_t": x.reshape(NT, P, KC, P).transpose(0, 3, 2, 1).reshape(NT, P, HID),
        "cond_ids": a["itok_B_0_15"].reshape(1, BATCH),
        "lora_ids": a["itok_B_6_15"].reshape(1, BATCH),
        "cond_w": a["L0_cond_weights"].transpose(1, 0, 2),
        "ident": np.eye(P, dtype=np.float32),
        "lora_mask": np.kron(np.eye(2), np.ones((RANK, CH))).astype(np.float32),
        "wvu": np.concatenate([wvu, wvu], axis=2),
        "wr": np.concatenate([a["L0_ffn_Wr"]] * 2, axis=1),
        "keys_t": np.concatenate([a["L0_ffn_aux_keys"].T] * 2, axis=0),
        "log_rel": np.concatenate([a["L0_ffn_log_rel"]] * 2).reshape(1, 2 * NSLOT),
        "lora_a": lora_a.reshape(LBLK, LPB, RANK, KC, P).transpose(0, 4, 1, 3, 2),
        "av_t": chunks(a["L0_ffn_aux_values"].T),
        "wvd_t": chunks(a["L0_ffn_Wvd"].T),
        "coefs": expert(coefs),
        "masks": np.ascontiguousarray(expert(masks)).view(np.int32),
        "enc": np.concatenate([a["L1_ffn_enc0"], a["L1_ffn_enc1"]], axis=0),
        "fourier": fourier_matrix(HID).reshape(KC, P, HID),
        "w_base_t": a["L1_ffn_W_base"].T.reshape(KC, P, HID),
        "left_blocks": np.concatenate([
            a["L1_cond_base_weight"].reshape(KC, P, KC, P).transpose(2, 1, 0, 3),
            lora_b.reshape(LBLK, LPB, KC, P, RANK).transpose(0, 3, 2, 1, 4).reshape(LBLK, P, KC, P)]),
        "cond_bias": a["L1_cond_base_bias"].reshape(KC, P).T,
        "b_base": a["L1_ffn_b_base"].reshape(1, HID),
        "wu1_t": groups(a["L0_ffn_Wu1"]).reshape(P, 2, HID),
        "wq_t": groups(a["L0_ffn_Wq"]),
        "bu1": rows(a["L0_ffn_bu1"].reshape(1, NUNC), (P, NUNC)),
        "wu2": rows(a["L0_ffn_Wu2"].reshape(1, NUNC), (P, NUNC)),
        "gate_params": np.stack([rows(a[n].reshape(-1)[:1], (P,)) for n in
                                 ("L0_ffn_bu2", "L0_ffn_gate_w1", "L0_ffn_gate_bias")], axis=1),
    }
    nc = bacc.Bacc("TRN2", target_bir_lowering=False, num_devices=1)
    arrays, aps = {}, {}
    for name, value in data.items():
        value = np.ascontiguousarray(value)
        arrays["in_" + name] = value
        aps[name] = nc.dram_tensor("in_" + name, value.shape, mybir.dt.from_np(value.dtype),
                                   kind="ExternalInput").ap()
    aps["out"] = nc.dram_tensor("out", (NT, P, HID), F32, kind="ExternalOutput").ap()
    build(nc, aps)
    r = run_bass_kernel_spmd(nc, [arrays], core_ids=[0])
    return np.asarray(r.results[0]["out"]).reshape(BATCH, CH, HID)
```

```python
from contextlib import ExitStack

import numpy as np

import concourse.bass as bass
from concourse import mybir

F32 = mybir.dt.float32
F32R = mybir.dt.float32r
I32 = mybir.dt.int32
U8 = mybir.dt.uint8
ALU = mybir.AluOpType
ACT = mybir.ActivationFunctionType
AX = mybir.AxisListType

P = 128
BATCH, CH, HID = 128, 64, 1024
NT = BATCH * CH // P
KC = HID // P
HALF = HID // 2
NCOND = 16
NLORA, RANK = 32, 16
NUNC = HID // 4
BOT = 64
RDIM = 48
NSLOT = 256
RENC = 40
NEXP = 3
GRP = RANK
NUG, NQG = NUNC // GRP, BOT // GRP
HQW = NUNC + BOT
PAW = HQW + 2 * RANK
LBLK = NLORA * RANK // P
LPB = NLORA // LBLK
NEG = -1.0e30
REPLACED = -3.0e38
VAR_A = 16
TANH_C = 0.7978845608028654


def f(ap):
    return ap.bitcast(F32)


def product3(pe, out, a_hi, a_lo, b_hi, b_lo, start, stop, skip=False):
    pe.matmul(out, a_hi, b_hi, start=start, stop=False, skip_group_check=skip)
    pe.matmul(out, a_hi, b_lo, start=False, stop=False, skip_group_check=skip)
    return pe.matmul(out, a_lo, b_hi, start=False, stop=stop, skip_group_check=skip)


def wait_apart(eng, spacer, signal, count):
    eng.wait_ge(signal, count)
    if not isinstance(count, int):
        eng.memset(spacer, 0.0)


def known_positive(count):
    return not isinstance(count, int) or count > 0


def build(nc, t):
    with ExitStack() as top:
        def sem(name):
            return top.enter_context(nc.semaphore(name))

        def tile(stack, name, shape, dt=F32, side="left"):
            return stack.enter_context(nc.sbuf_tensor(name, shape, dt, side=side))

        t["w_kinds"] = nc.dram_tensor("w_kinds", (NCOND, CH, 4, CH), F32, kind="Internal").ap()
        t["a_split"] = nc.dram_tensor("a_split", (NLORA, P, 2, KC, RANK), F32, kind="Internal").ap()
        t["wa_split"] = nc.dram_tensor("wa_split", (NLORA, P, 2, RANK), F32, kind="Internal").ap()
        t["bk_hi"] = nc.dram_tensor("bk_hi", (NLORA * RANK, HID), F32, kind="Internal").ap()
        t["bk_lo"] = nc.dram_tensor("bk_lo", (NLORA * RANK, HID), F32, kind="Internal").ap()

        pair = [top.enter_context(nc.psum_tensor(f"pair{n}", [P, HID], F32)) for n in range(4)]

        g = {}
        for name, shape, dt in (
            ("ident", [P, P], F32), ("ident_r", [P, P], F32R), ("lora_mask", [2 * RANK, P], F32),
            ("ones", [P, P], F32), ("spacer", [1, 1], F32),
            ("cond_ids", [1, BATCH], I32), ("lora_ids", [1, BATCH], I32),
            ("vd", [P, 2, BOT], F32),
            ("wvu_hi", [P, KC, P], F32R), ("wvu_lo", [P, KC, P], F32R),
            ("router_a", [P, 2 * NSLOT], F32R), ("router_b", [P, 2 * NSLOT], F32R),
            ("var", [P, NT], F32), ("norm_var", [P, NT], F32), ("const_part", [P, HID], F32),
        ):
            g[name] = tile(top, name, shape, dt)

        vstack = top.enter_context(ExitStack())
        v = {}
        for name, shape, dt in (
            ("v_x", [P, 2, HID], F32), ("v_hi", [P, 2, HID], F32R), ("v_lo", [P, 2, HID], F32R),
            ("v_w", [P, 4, 2, P], F32R), ("v_stats", [P, 2, 12], F32), ("v_mv", [P, 2, 2], F32),
        ):
            v[name] = tile(vstack, name, shape, dt)
        v["x_loaded"] = [sem(f"v_x_loaded{r}") for r in range(2)]
        v["w_loaded"] = [sem(f"v_w_loaded{r}") for r in range(4)]
        for name in ("v_hi_ready", "v_lo_ready", "v_mm_done", "v_bn_done", "v_aggr_done", "v_var_ready"):
            v[name] = sem(name)
        v["psum"] = pair[0:2]

        kstack = top.enter_context(ExitStack())
        k_hi, k_lo = setup_block(nc, t, g, v, pair, sem, tile, kstack)
        m_hi = tile(top, "m_hi", [P, KC, HID], F32R, side="right")
        m_lo = tile(top, "m_lo", [P, KC, HID], F32R, side="right")
        fold_block(nc, t, g, v, pair, sem, tile, k_hi, k_lo, m_hi, m_lo)
        kstack.close()
        vstack.close()
        main_block(nc, t, g, pair, sem, tile, m_hi, m_lo)



def var_load(sp, t, g, v, n, slot):
    s = slot % 2
    x_off = sp.snap(n * (P * HID)) if not isinstance(n, int) else n * P * HID
    splits = n - 1
    round2 = sp.snap(splits) if not isinstance(n, int) else splits
    used4 = n - 3
    used = sp.snap(used4) if not isinstance(n, int) else used4
    ids = [sp.value_load(g["cond_ids"][:, bass.ds(n * 2 + b, 1)], min_val=0, max_val=NCOND - 1)
           for b in range(2)]
    offs = [sp.snap(i * (CH * 4 * CH)) for i in ids]
    if known_positive(round2):
        sp.wait_ge(v["v_lo_ready"], round2)
    sp.dma_start(v["v_x"][:, s, :], bass.AP(t["x"].tensor, x_off, [[HID, P], [1, HID]])
                 ).then_inc(v["x_loaded"][s], 16)
    if known_positive(used):
        sp.wait_ge(v["v_mm_done"], used)
    for b in range(2):
        src = bass.AP(t["w_kinds"].tensor, offs[b], [[4 * CH, CH], [CH, 2], [1, CH]])
        sp.dma_start(f(v["v_w"][b * CH:(b + 1) * CH, slot, :, b * CH:(b + 1) * CH]), src
                     ).then_inc(v["w_loaded"][slot], 16)


def var_hi(act, v, n, slot):
    s = slot % 2
    act.wait_ge(v["x_loaded"][s], (n - s) * 8 + 16)
    if known_positive(n - 1):
        act.wait_ge(v["v_mm_done"], n - 1)
    act.copy(v["v_hi"][:, s, :], v["v_x"][:, s, :]).then_inc(v["v_hi_ready"], 1)


def var_lo(pool, v, n, slot):
    s = slot % 2
    ready = n + 1 if isinstance(n, int) else pool.snap(n + 1)
    pool.wait_ge(v["v_hi_ready"], ready)
    pool.tensor_tensor(v["v_lo"][:, s, :], v["v_x"][:, s, :], f(v["v_hi"][:, s, :]),
                       ALU.subtract).then_inc(v["v_lo_ready"], 1)


def var_mm(pe, v, n, slot):
    s = slot % 2
    pe.wait_ge(v["v_lo_ready"], n + 1)
    pe.wait_ge(v["w_loaded"][slot], quarter_count(n, slot))
    if known_positive(n - 1):
        pe.wait_ge(v["v_bn_done"], n - 1)
    w_hi, w_lo = v["v_w"][:, slot, 0, :], v["v_w"][:, slot, 1, :]
    out = v["psum"][s]
    for h in range(2):
        c = slice(h * HALF, (h + 1) * HALF)
        last = product3(pe, out[:, c], w_hi, w_lo, v["v_hi"][:, s, c], v["v_lo"][:, s, c], True, True)
    last.then_inc(v["v_mm_done"], 1)


def quarter_count(n, slot):
    return (n - slot) * 8 + 32


def var_stats(dve, spacer, g, v, n, slot):
    s = slot % 2
    dve.wait_ge(v["v_mm_done"], n + 1)
    if known_positive(n - 1):
        dve.wait_ge(v["v_aggr_done"], n - 1)
    dve.bn_stats(v["v_stats"][:, s, 0:6], v["psum"][s][:, 0:HALF])
    dve.bn_stats(v["v_stats"][:, s, 6:12], v["psum"][s][:, HALF:HID]).then_inc(v["v_bn_done"], 1)
    if known_positive(n - 1):
        dve.wait_ge(v["v_var_ready"], n - 1)
    wait_apart(dve, spacer, v["v_bn_done"], n + 1)
    dve.bn_aggr(v["v_mv"][:, s, :], v["v_stats"][:, s, :]).then_inc(v["v_aggr_done"], 1)
    dve.wait_ge(v["v_aggr_done"], n + 1)
    dve.tensor_copy(g["var"][:, bass.ds(n, 1)], v["v_mv"][:, s, 1:2]).then_inc(v["v_var_ready"], 1)



def setup_block(nc, t, g, v, pair, sem, tile, kstack):
    with ExitStack() as right, ExitStack() as early:
        fourier = tile(right, "fourier", [P, KC, HID], F32, "right")
        kf = tile(right, "kf", [P, KC, HID], F32, "right")
        enc_hi = tile(right, "enc_hi", [RENC, HID], F32R, "right")
        enc_lo = tile(right, "enc_lo", [RENC, HID], F32R, "right")
        cs_hi = tile(right, "cs_hi", [RENC, HID], F32R, "right")
        cs_lo = tile(right, "cs_lo", [RENC, HID], F32R, "right")

        enc = tile(early, "enc", [RENC, HID])
        w_raw = tile(early, "w_raw", [CH, NCOND, CH])
        w_plus = tile(early, "w_plus", [CH, NCOND, CH])
        w_kinds = tile(early, "w_kinds_sb", [CH, NCOND, 4, CH], F32R)
        coefs = tile(early, "coefs", [P, NEXP, KC * RENC])
        masks = tile(early, "masks", [P, NEXP, KC * RENC // 4], I32)
        av_t = tile(early, "av_t", [P, KC, NSLOT])
        wvd_t = tile(early, "wvd_t", [P, KC, BOT])
        wvu = tile(early, "wvu", [P, KC, P])
        a_raw = tile(early, "a_raw", [P, LPB, KC, RANK])
        a_split = tile(early, "a_split_sb", [P, LPB, 2, KC, RANK], F32R)
        wa_split = tile(early, "wa_split_sb", [P, NLORA, 2, RANK], F32R)
        wr = tile(early, "wr", [RDIM, 2 * BOT])
        wtw = tile(early, "wtw", [BOT, 2 * BOT])
        keys = tile(early, "keys", [P, NSLOT])
        router = tile(early, "router", [P, 2 * NSLOT])
        logrel = tile(early, "logrel", [1, 2 * NSLOT])
        logrel_hi = tile(early, "logrel_hi", [1, 2 * NSLOT], F32R)
        logrel_lo = tile(early, "logrel_lo", [1, 2 * NSLOT], F32R)
        early.close()
        k_hi = tile(kstack, "k_hi", [P, KC, HID], F32R)
        k_lo = tile(kstack, "k_lo", [P, KC, HID], F32R)

        names = ("ids_in w_in enc_in coefs_in av_in a_in wvu_in keys_in logrel_in fourier_in wbase_in "
                 "w_stored a_stored wa_stored logrel_placed s_chain zeroed w_plus_ready w_hi_ready w_kinds_ready "
                 "enc_hi_ready enc_split wvu_hi_ready wvu_split wsum_ready a_hi_ready a_split_ready "
                 "wa_mm_done wa_split_ready vd_mm_done vd_ready wtw_mm_done wtw_ready g_mm_done "
                 "router_ready cs_mm_done cs_hi_ready cs_split k_mm_done k_sum_ready k_hi_ready "
                 "logrel_split").split()
        s = {n: sem(n) for n in names}
        small = pair[3][:, 0:HALF]
        wa_bank = pair[3][:, HALF:HID]
        kpair = pair[2:4]

        with nc.Block() as block:

            @block.sync
            def _(sp):
                sp.dma_start(w_raw[:], t["cond_w"]).then_inc(s["w_in"], 16)
                sp.dma_start(g["ident"][:], t["ident"]).then_inc(s["w_in"], 16)
                for name in ("cond_ids", "lora_ids"):
                    sp.dma_start(g[name][:], t[name]).then_inc(s["ids_in"], 16)
                sp.dma_start(v["v_x"][:, 0, :], bass.AP(t["x"].tensor, 0, [[HID, P], [1, HID]])
                             ).then_inc(v["x_loaded"][0], 16)
                sp.dma_start(v["v_x"][:, 1, :], bass.AP(t["x"].tensor, P * HID, [[HID, P], [1, HID]])
                             ).then_inc(v["x_loaded"][1], 16)
                sp.wait_ge(s["w_kinds_ready"], 1)
                sp.dma_start(t["w_kinds"].rearrange("n c k d -> c n k d"), f(w_kinds[:])
                             ).then_inc(s["w_stored"], 16)
                sp.wait_ge(s["ids_in"], 32)
                sp.wait_ge(s["w_stored"], 16)
                sp.wait_ge(s["zeroed"], 1)
                for n in range(VAR_A):
                    if n >= 2:
                        var_load(sp, t, g, v, n, n % 4)
                        continue
                    ids = [sp.value_load(g["cond_ids"][:, 2 * n + b:2 * n + b + 1], min_val=0,
                                         max_val=NCOND - 1) for b in range(2)]
                    for b in range(2):
                        off = sp.snap(ids[b] * (CH * 4 * CH))
                        src = bass.AP(t["w_kinds"].tensor, off, [[4 * CH, CH], [CH, 2], [1, CH]])
                        sp.dma_start(f(v["v_w"][b * CH:(b + 1) * CH, n, :, b * CH:(b + 1) * CH]), src
                                     ).then_inc(v["w_loaded"][n], 16)

            @block.scalar
            def _(act):
                for dst, src in ((wvu[:], t["wvu"]), (wr[:], t["wr"]), (g["lora_mask"][:], t["lora_mask"])):
                    act.dma_start(dst, src).then_inc(s["wvu_in"], 16)
                act.dma_start(keys[:], t["keys_t"]).then_inc(s["keys_in"], 16)
                act.dma_start(logrel[:], t["log_rel"]).then_inc(s["logrel_in"], 16)
                act.dma_start(a_raw[:], t["lora_a"][0]).then_inc(s["a_in"], 16)
                act.dma_start(av_t[:], t["av_t"]).then_inc(s["av_in"], 16)
                act.dma_start(wvd_t[:], t["wvd_t"]).then_inc(s["av_in"], 16)
                act.dma_start(coefs[:], t["coefs"]).then_inc(s["coefs_in"], 16)
                act.dma_start(masks[:], t["masks"]).then_inc(s["coefs_in"], 16)
                act.dma_start(enc[:], t["enc"]).then_inc(s["enc_in"], 16)
                for k in range(KC):
                    act.dma_start(fourier[:, k, :], t["fourier"][k]).then_inc(s["fourier_in"], 16)
                for k in range(KC):
                    act.dma_start(kf[:, k, :], t["w_base_t"][k]).then_inc(s["wbase_in"], 16)
                act.wait_ge(s["w_in"], 32)
                act.copy(w_kinds[:, :, 0, :], w_raw[:])
                act.wait_ge(s["w_plus_ready"], 1)
                act.copy(w_kinds[:, :, 2, :], w_plus[:]).then_inc(s["w_hi_ready"], 1)
                act.wait_ge(s["wvu_in"], 48)
                act.copy(g["wvu_hi"][:], wvu[:]).then_inc(s["wvu_hi_ready"], 1)
                for c in range(LBLK):
                    act.wait_ge(s["a_in"], 16 * (c + 1))
                    if c:
                        act.wait_ge(s["wa_mm_done"], c)
                        act.wait_ge(s["a_stored"], 16 * c)
                    act.copy(a_split[:, :, 0], a_raw[:]).then_inc(s["a_hi_ready"], 1)
                    if c + 1 < LBLK:
                        act.wait_ge(s["a_split_ready"], c + 1)
                        act.dma_start(a_raw[:], t["lora_a"][c + 1]).then_inc(s["a_in"], 16)
                    var_hi(act, v, 2 * c, (2 * c) % 4)
                    var_hi(act, v, 2 * c + 1, (2 * c + 1) % 4)
                act.wait_ge(s["enc_in"], 16)
                act.copy(enc_hi[:], enc[:]).then_inc(s["enc_hi_ready"], 1)
                act.wait_ge(s["cs_mm_done"], 1)
                act.mul(cs_hi[:], pair[2][0:RENC, :], 0.5).then_inc(s["cs_hi_ready"], 1)
                act.wait_ge(s["w_stored"], 16)
                act.wait_ge(s["a_stored"], 16 * LBLK)
                act.wait_ge(s["wa_stored"], 16)
                act.wait_ge(s["logrel_placed"], 32)
                for k in range(KC):
                    var_hi(act, v, 8 + k, k % 4)
                    act.wait_ge(s["k_sum_ready"], k + 1)
                    act.copy(k_hi[:, k, :], kf[:, k, :]).then_inc(s["k_hi_ready"], 1)

            @block.gpsimd
            def _(pool):
                pool.memset(g["ones"][:], 1.0)
                pool.memset(f(g["router_b"][:]), 0.0)
                pool.memset(f(v["v_w"][:]), 0.0).then_inc(s["zeroed"], 1)
                pool.wait_ge(s["w_hi_ready"], 1)
                pool.tensor_tensor(w_kinds[:, :, 1, :], w_raw[:], f(w_kinds[:, :, 0, :]), ALU.subtract)
                pool.tensor_tensor(w_kinds[:, :, 3, :], w_plus[:], f(w_kinds[:, :, 2, :]),
                                   ALU.subtract).then_inc(s["w_kinds_ready"], 1)
                pool.wait_ge(s["wvu_hi_ready"], 1)
                pool.tensor_tensor(g["wvu_lo"][:], wvu[:], f(g["wvu_hi"][:]),
                                   ALU.subtract).then_inc(s["wvu_split"], 1)
                for c in range(LBLK):
                    pool.wait_ge(s["a_hi_ready"], c + 1)
                    pool.tensor_tensor(a_split[:, :, 1], a_raw[:], f(a_split[:, :, 0]),
                                       ALU.subtract).then_inc(s["a_split_ready"], 1)
                    pool.wait_ge(s["a_split_ready"], c + 1)
                    pool.dma_start(t["a_split"][c * LPB:(c + 1) * LPB].rearrange("l p s k r -> p l s k r"),
                                   f(a_split[:])).then_inc(s["a_stored"], 16)
                    var_lo(pool, v, 2 * c, (2 * c) % 4)
                    var_lo(pool, v, 2 * c + 1, (2 * c + 1) % 4)
                pool.wait_ge(s["enc_hi_ready"], 1)
                pool.tensor_tensor(enc_lo[:], enc[:], f(enc_hi[:]), ALU.subtract).then_inc(s["enc_split"], 1)
                pool.wait_ge(s["wa_split_ready"], 1)
                pool.dma_start(t["wa_split"].rearrange("l p s r -> p l s r"), f(wa_split[:])
                               ).then_inc(s["wa_stored"], 16)
                pool.wait_ge(s["logrel_split"], 1)
                pool.wait_ge(s["router_ready"], 1)
                pool.dma_start(f(g["router_b"][BOT:BOT + 1, :]), f(logrel_hi[:])).then_inc(s["logrel_placed"], 16)
                pool.dma_start(f(g["router_b"][BOT + 1:BOT + 2, :]), f(logrel_lo[:])).then_inc(s["logrel_placed"], 16)
                pool.wait_ge(s["logrel_placed"], 32)
                pool.wait_ge(s["wa_stored"], 16)
                pool.wait_ge(s["a_stored"], 16 * LBLK)
                for k in range(KC):
                    var_lo(pool, v, 8 + k, k % 4)
                    pool.wait_ge(s["k_hi_ready"], k + 1)
                    pool.tensor_tensor(k_lo[:, k, :], kf[:, k, :], f(k_hi[:, k, :]), ALU.subtract)
                pool.drain()

            @block.tensor
            def _(pe):
                pe.wait_ge(s["wvu_in"], 48)
                pe.matmul(small[0:BOT, 0:2 * BOT], wr[:, 0:BOT], wr[:], start=True, stop=True
                          ).then_inc(s["wtw_mm_done"], 1)
                pe.wait_ge(s["keys_in"], 16)
                pe.wait_ge(s["wtw_ready"], 1)
                pe.matmul(small[:, 0:NSLOT], wtw[:], keys[0:BOT, :], start=True, stop=True
                          ).then_inc(s["g_mm_done"], 1)
                for c in range(LBLK):
                    pe.wait_ge(s["wvu_split"], 1)
                    pe.wait_ge(s["a_split_ready"], c + 1)
                    for k in range(KC):
                        last = product3(pe, wa_bank[:, c * P:(c + 1) * P],
                                        g["wvu_hi"][:, k, :], g["wvu_lo"][:, k, :],
                                        a_split[:, :, 0, k, :], a_split[:, :, 1, k, :], k == 0, k == KC - 1)
                    last.then_inc(s["wa_mm_done"], 1)
                    var_mm(pe, v, 2 * c, (2 * c) % 4)
                    var_mm(pe, v, 2 * c + 1, (2 * c + 1) % 4)
                pe.wait_ge(s["av_in"], 32)
                pe.wait_ge(s["router_ready"], 1)
                for b in range(2):
                    for k in range(KC):
                        last = pe.matmul(small[:, b * BOT:(b + 1) * BOT], av_t[:, k, b * P:(b + 1) * P],
                                         wvd_t[:, k, :], start=(k == 0), stop=(k == KC - 1))
                last.then_inc(s["vd_mm_done"], 1)
                pe.wait_ge(s["wsum_ready"], 1)
                pe.wait_ge(s["fourier_in"], 16 * KC)
                for h in range(2):
                    for k in range(KC):
                        last = pe.matmul(pair[2][0:RENC, h * HALF:(h + 1) * HALF],
                                         coefs[:, 0, k * RENC:(k + 1) * RENC],
                                         fourier[:, k, h * HALF:(h + 1) * HALF],
                                         start=(k == 0), stop=(k == KC - 1))
                last.then_inc(s["cs_mm_done"], 1)
                pe.wait_ge(s["cs_split"], 1)
                pe.wait_ge(s["enc_split"], 1)
                pe.wait_ge(s["vd_ready"], 1)
                pe.wait_ge(s["wa_split_ready"], 1)
                for k in range(KC):
                    if k >= 2:
                        pe.wait_ge(s["k_sum_ready"], k - 1)
                    for h in range(2):
                        c = slice(h * HALF, (h + 1) * HALF)
                        e = slice(k * P, (k + 1) * P)
                        last = product3(pe, kpair[k % 2][:, c], enc_hi[:, e], enc_lo[:, e],
                                        cs_hi[:, c], cs_lo[:, c], True, True)
                    last.then_inc(s["k_mm_done"], 1)
                    var_mm(pe, v, 8 + k, k % 4)

            @block.vector
            def _(dve):
                spacer = g["spacer"][:]
                chain = [0]

                def link(ins):
                    chain[0] += 1
                    ins.then_inc(s["s_chain"], 1)
                    dve.wait_ge(s["s_chain"], chain[0])

                dve.wait_ge(s["w_in"], 32)
                id_b = g["ident"][0:CH, 0:CH].unsqueeze(1).broadcast_to([CH, NCOND, CH])
                dve.tensor_tensor(w_plus[:], w_raw[:], id_b, ALU.add).then_inc(s["w_plus_ready"], 1)
                dve.wait_ge(s["wtw_mm_done"], 1)
                dve.tensor_copy(wtw[:], small[0:BOT, 0:2 * BOT]).then_inc(s["wtw_ready"], 1)
                dve.wait_ge(s["g_mm_done"], 1)
                dve.tensor_scalar(router[:, 0:NSLOT], small[:, 0:NSLOT], float(RDIM) ** -0.5, None, ALU.mult)
                link(dve.tensor_scalar(router[:, NSLOT:], keys[:], float(BOT) ** -0.5, None, ALU.mult))
                link(dve.tensor_copy(g["router_a"][:], router[:]))
                dve.wait_ge(s["zeroed"], 1)
                dve.tensor_tensor(g["router_b"][0:BOT, :], router[0:BOT, :], f(g["router_a"][0:BOT, :]),
                                  ALU.subtract).then_inc(s["router_ready"], 1)
                dve.wait_ge(s["logrel_in"], 16)
                link(dve.tensor_copy(logrel_hi[:], logrel[:]))
                dve.tensor_tensor(logrel_lo[:], logrel[:], f(logrel_hi[:]), ALU.subtract
                                  ).then_inc(s["logrel_split"], 1)
                dve.wait_ge(s["coefs_in"], 32)
                link(dve.tensor_tensor(coefs[:], coefs[:], masks[:].bitcast(U8), ALU.mult))
                link(dve.tensor_tensor(coefs[:, 0, :], coefs[:, 0, :], coefs[:, 1, :], ALU.add))
                dve.tensor_tensor(coefs[:, 0, :], coefs[:, 0, :], coefs[:, 2, :], ALU.add
                                  ).then_inc(s["wsum_ready"], 1)
                for n in range(2 * LBLK):
                    var_stats(dve, spacer, g, v, n, n % 4)
                dve.wait_ge(s["wa_mm_done"], LBLK)
                wa3 = wa_bank.rearrange("p (l r) -> p l r", r=RANK)
                link(dve.tensor_copy(wa_split[:, :, 0, :], wa3))
                dve.tensor_tensor(wa_split[:, :, 1, :], wa3, f(wa_split[:, :, 0, :]), ALU.subtract
                                  ).then_inc(s["wa_split_ready"], 1)
                dve.wait_ge(s["vd_mm_done"], 1)
                dve.tensor_copy(g["vd"][:], small[:, 0:2 * BOT].rearrange("p (b v) -> p b v", b=2)
                                ).then_inc(s["vd_ready"], 1)
                dve.wait_ge(s["cs_hi_ready"], 1)
                dve.scalar_tensor_tensor(cs_lo[:], pair[2][0:RENC, :], 0.5, f(cs_hi[:]), ALU.mult,
                                         ALU.subtract).then_inc(s["cs_split"], 1)
                dve.wait_ge(s["wbase_in"], 16 * KC)
                for k in range(KC):
                    dve.wait_ge(s["k_mm_done"], k + 1)
                    dve.tensor_tensor(kf[:, k, :], kf[:, k, :], kpair[k % 2][:, :], ALU.add
                                      ).then_inc(s["k_sum_ready"], 1)
                    var_stats(dve, spacer, g, v, 8 + k, k % 4)
    return k_hi, k_lo




def fold_block(nc, t, g, v, pair, sem, tile, k_hi, k_lo, m_hi, m_lo):
    with ExitStack() as st:
        blk_raw = tile(st, "blk_raw", [P, KC, P])
        blk_hi = tile(st, "blk_hi", [P, 2, KC, P], F32R)
        blk_lo = tile(st, "blk_lo", [P, 2, KC, P], F32R)
        bk_hi = tile(st, "bk_hi_sb", [P, HID], F32R)
        bk_lo = tile(st, "bk_lo_sb", [P, HID], F32R)
        bb = tile(st, "bb", [P, KC])

        names = ("raw_loaded bhi_ready blo_ready blk_done evac_hi_ready banks_free bk_stored bias_in "
                 "part_cleared c_chain").split()
        s = {n: sem(n) for n in names}
        zpair = pair[2:4]
        NB = LBLK + KC
        per = (NT - VAR_A) // NB

        with nc.Block() as block:

            @block.sync
            def _(sp):
                sp.dma_start(bb[:], t["cond_bias"]).then_inc(s["bias_in"], 16)
                sp.wait_ge(s["part_cleared"], 1)
                sp.dma_start(g["const_part"][0:1, :], t["b_base"]).then_inc(s["bias_in"], 16)

                def load_block(b):
                    split = b if isinstance(b, int) else sp.snap(b)
                    off = b * (P * HID) if isinstance(b, int) else sp.snap(b * (P * HID))
                    if known_positive(b):
                        sp.wait_ge(s["blo_ready"], split)
                    sp.dma_start(blk_raw[:], bass.AP(t["left_blocks"].tensor, off, [[HID, P], [P, KC], [1, P]])
                                 ).then_inc(s["raw_loaded"], 16)

                def row_load(b, q):
                    var_load(sp, t, g, v, b * per + (VAR_A + q), q % per)

                load_block(0)
                row_load(0, 0)
                load_block(1)
                with sp.Fori(0, NB - 2) as b:
                    for q in range(1, per + 1):
                        row_load(b, q)
                    load_block(b + 2)
                for q in range(1, 2 * per):
                    row_load(NB - 2, q)

            @block.scalar
            def _(act):
                def block_hi(b, i):
                    act.wait_ge(s["raw_loaded"], b * 16 + 16)
                    act.copy(blk_hi[:, i], blk_raw[:]).then_inc(s["bhi_ready"], 1)

                def row_hi(b, q):
                    var_hi(act, v, b * per + (VAR_A + q), q % per)

                def one(b, i, evac, last=False):
                    row_hi(b, 1)
                    row_hi(b, 2)
                    if not last:
                        block_hi(b + 1, 1 - i)
                    row_hi(b, 3)
                    if not last:
                        row_hi(b, 4)
                    act.wait_ge(s["blk_done"], b + 1)
                    evac(zpair[i])

                def evac_m(b):
                    def go(z):
                        act.copy(m_hi[:, bass.ds(b - LBLK, 1), :].rearrange("p a n -> p (a n)"), z[:]
                                 ).then_inc(s["evac_hi_ready"], 1)
                    return go

                def evac_bk(b):
                    def go(z):
                        if b:
                            act.wait_ge(s["bk_stored"], b * 32)
                        act.copy(bk_hi[:], z[:]).then_inc(s["evac_hi_ready"], 1)
                    return go

                def store(b):
                    act.wait_ge(s["banks_free"], b + 3)
                    for part, src in (("bk_hi", bk_hi), ("bk_lo", bk_lo)):
                        act.dma_start(t[part][b * P:(b + 1) * P, :], f(src[:])).then_inc(s["bk_stored"], 16)

                block_hi(0, 0)
                row_hi(0, 0)
                for b in range(LBLK):
                    one(b, b % 2, evac_bk(b))
                    store(b)
                with act.Fori(0, KC // 2 - 1) as j:
                    b = j * 2 + LBLK
                    one(b, 0, evac_m(b))
                    one(b + 1, 1, evac_m(b + 1))
                one(NB - 2, 0, evac_m(NB - 2))
                one(NB - 1, 1, evac_m(NB - 1), last=True)
                act.wait_ge(s["bk_stored"], 32 * LBLK)

            @block.gpsimd
            def _(pool):
                def row_lo(b, q):
                    var_lo(pool, v, b * per + (VAR_A + q), q % per)

                def split(b, i):
                    ready = b + 1 if isinstance(b, int) else pool.snap(b + 1)
                    pool.wait_ge(s["bhi_ready"], ready)
                    pool.tensor_tensor(blk_lo[:, i], blk_raw[:], f(blk_hi[:, i]), ALU.subtract
                                       ).then_inc(s["blo_ready"], 1)

                def one(b, i, last=False):
                    row_lo(b, 1)
                    row_lo(b, 2)
                    if not last:
                        split(b + 1, 1 - i)
                    row_lo(b, 3)
                    if not last:
                        row_lo(b, 4)

                split(0, 0)
                row_lo(0, 0)
                with pool.Fori(0, NB // 2 - 1) as j:
                    b = j * 2
                    one(b, 0)
                    one(b + 1, 1)
                one(NB - 2, 0)
                one(NB - 1, 1, last=True)

            @block.tensor
            def _(pe):
                def one(b, i, identity=False):
                    pe.wait_ge(s["blo_ready"], b + 1)
                    pe.wait_ge(s["banks_free"], b + 1)
                    z = zpair[i]
                    for q in range(per):
                        h, k0 = q // 2, (q % 2) * (KC // 2)
                        c = slice(h * HALF, (h + 1) * HALF)
                        for k in range(k0, k0 + KC // 2):
                            last = product3(pe, z[:, c], blk_hi[:, i, k, :], blk_lo[:, i, k, :],
                                            k_hi[:, k, c], k_lo[:, k, c], k == 0,
                                            k == KC - 1 and not identity, skip=identity)
                        if q == per - 1:
                            if identity:
                                d = z[:, bass.ds((b - LBLK) * P, P)]
                                last = pe.matmul(d, g["ident_r"][:], g["ident_r"][:], start=False, stop=True,
                                                 skip_group_check=True)
                            last.then_inc(s["blk_done"], 1)
                        var_mm(pe, v, b * per + (VAR_A + q), q)

                with pe.Fori(0, LBLK // 2) as j:
                    b = j * 2
                    one(b, 0)
                    one(b + 1, 1)
                with pe.Fori(0, KC // 2) as j:
                    b = j * 2 + LBLK
                    one(b, 0, identity=True)
                    one(b + 1, 1, identity=True)

            @block.vector
            def _(dve):
                spacer = g["spacer"][:]
                def one(b, i, lo, hi, beside=None):
                    for q in range(per):
                        var_stats(dve, spacer, g, v, b * per + (VAR_A + q), q)
                        if beside is not None:
                            beside(b, q)
                    dve.wait_ge(s["evac_hi_ready"], b + 1)
                    dve.tensor_tensor(lo, zpair[i][:], f(hi), ALU.subtract).then_inc(s["banks_free"], 1)

                def const_step(b, q):
                    n = b * per + q
                    k, src = n // 2, (k_hi, k_lo)[n % 2]
                    if n:
                        dve.wait_ge(s["c_chain"], n)
                    else:
                        dve.wait_ge(s["bias_in"], 32)
                    dve.scalar_tensor_tensor(part[:], f(src[:, k, :]), bb[:, k:k + 1], part[:], ALU.mult,
                                             ALU.add).then_inc(s["c_chain"], 1)

                def m_rows(b):
                    return [m[:, bass.ds(b - LBLK, 1), :].rearrange("p a n -> p (a n)") for m in (m_lo, m_hi)]

                part = g["const_part"]
                dve.memset(part[:], 0.0).then_inc(s["part_cleared"], 1)
                dve.tensor_copy(g["ident_r"][:], g["ident"][:]).then_inc(s["banks_free"], 2)
                for b in range(LBLK):
                    one(b, b % 2, bk_lo[:], bk_hi[:], const_step)
                with dve.Fori(0, KC // 2) as j:
                    b = j * 2 + LBLK
                    one(b, 0, *m_rows(b))
                    one(b + 1, 1, *m_rows(b + 1))



def main_block(nc, t, g, pair, sem, tile, m_hi, m_lo):
    with ExitStack() as st:
        b = {}
        for name, shape, dt in (
            ("narrow", [P, 2 + NUG + NQG + 2, 2, KC, GRP], F32R),
            ("xt", [P, 2, HID], F32), ("xt_hi", [P, 2, HID], F32R), ("xt_lo", [P, 2, HID], F32R),
            ("pm_hi", [P, HID], F32R), ("pm_lo", [P, HID], F32R),
            ("pa_hi", [P, 2, PAW], F32R), ("pa_lo", [P, 2, PAW], F32R),
            ("out_sb", [P, 2, HID], F32),
            ("rhs_a", [P, HID], F32R), ("rhs_b", [P, 2, HID], F32R), ("rhs_c", [P, 2, HID], F32R),
            ("bd", [P, 2, 4, P], F32R), ("wa", [P, 2, 2, 2, RANK], F32R),
            ("lhs_a", [P, P], F32R), ("lhs_b", [P, P], F32R), ("lhs_c", [P, P], F32R),
            ("query", [P, P], F32R), ("q_a", [P, P], F32R), ("q_b", [P, P], F32R),
            ("u_sb", [P, P], F32R), ("e_t", [P, 2, P], F32), ("hm", [2 * RANK, P], F32),
            ("z", [P, NUNC], F32), ("z2", [P, NUNC], F32),
            ("arg", [P, NUNC], F32), ("th", [P, NUNC], F32), ("gelu", [P, NUNC], F32), ("dot", [P, NUNC], F32),
            ("bu1", [P, NUNC], F32), ("wu2", [P, NUNC], F32),
            ("rest", [P, NSLOT], F32), ("penalty", [P, NSLOT], F32), ("logits", [P, NSLOT], F32),
            ("probs", [P, NSLOT], F32),
            ("top8", [P, 8], F32), ("col", [P, 16], F32), ("gates", [P, 8], F32),
            ("mean", [P, 4], F32), ("lv_u", [P, NT], F32), ("lv_d", [P, NT], F32), ("lv_is1", [P, NT], F32),
            ("lv_ln", [P, NT], F32), ("lv_num", [P, NT], F32), ("lv_log", [P, NT], F32),
        ):
            b[name] = tile(st, "t_" + name, shape, dt)

        def wu_raw():
            return b["out_sb"][:].rearrange("p a (g c) -> p (a g) c", c=KC * GRP)

        def wq_raw(half):
            return b[("probs", "logits")[half]][:].rearrange("p (g c) -> p g c", c=KC * GRP)

        def wu_groups(part):
            return b["narrow"][:, 2:2 + NUG, part].rearrange("p g k r -> p g (k r)")

        def wq_groups(half, part):
            first = 2 + NUG + half * (NQG // 2)
            return b["narrow"][:, first:first + NQG // 2, part].rearrange("p g k r -> p g (k r)")

        col = b["col"]
        ROWMAX, NEGMAX, ESUM, LSUM, LTANH, UNC, CLIP, SCALED, UNORM, GTANH, GATE, GATED, RSUM, SCALE = range(14)

        def c1(n):
            return col[:, n:n + 1]

        HQ = (slice(2 * RANK, PAW), slice(0, HQW))
        LORA = (slice(0, 2 * RANK), slice(HQW, PAW))
        A_GROUP = (0, 2 + NUG + NQG)

        out_ps = pair[0]
        pm_ps = pair[1]
        pa_ps = pair[2][:, 0:HALF]
        mix_ps = pair[2][:, HALF:HID]
        score_ps = pair[3][:, 0:HALF]
        misc_ps = pair[3][:, HALF:HID]

        loaded = {n: [sem(f"{n}_loaded{p}") for p in range(2)] for n in ("xt", "lora")}
        moved = [sem(f"out_slot_moved{p}") for p in range(2)]
        names = ("wq_in row_in gate_in const_cleared const_done const_hi_ready const_placed lvu_ready ln_ready lsum1_ready "
                 "mean_done norm_ready wu_hi_ready wu_split wq_hi_ready wq_split cleared "
                 "v_mm_ready va_ready vb_ready gates_ready m_chain "
                 "xhi_ready xlo_ready s1a_done s1b_done mixq_done qt_done score_done et_done u_done ut_done "
                 "h_done out_done pa_hi_ready pa_lo_ready pm_hi0_ready pm_hi1_ready pm_lo0_ready pm_lo1_ready "
                 "q_hi_ready q_split z_ready z2_ready arg_ready tanh_ready gelu_ready lsum_ready "
                 "ltanh_ready unc_ready clip_ready scaled_ready unorm_ready gtanh_ready gate_ready gated_ready "
                 "qt_ready top8_ready rest_ready penalty_ready logits_ready negmax_ready exp_ready rsum_ready "
                 "scale_ready et_ready uhi_ready u_split ut_ready hm_ready hhi_ready h_ready out_ready").split()
        s = {n: sem("m_" + n) for n in names}
        LPT = 16 * 12

        with nc.Block() as block:

            @block.sync
            def _(sp):
                sp.dma_start(b["xt"][:, 0, :], bass.AP(t["x_t"].tensor, 0, [[HID, P], [1, HID]])
                             ).then_inc(loaded["xt"][0], 16)
                for p in range(2):
                    sp.dma_start(b["out_sb"][:, p, :], t["wu1_t"][:, p, :]).then_inc(moved[p], 16)
                sp.dma_start(b["probs"][:], t["wq_t"][:, 0:NSLOT]).then_inc(s["wq_in"], 16)
                sp.dma_start(b["logits"][:], t["wq_t"][:, NSLOT:]).then_inc(s["wq_in"], 16)

                def load_x(i, p):
                    off = sp.snap(i * (P * HID)) if not isinstance(i, int) else i * P * HID
                    split = sp.snap(i - 1) if not isinstance(i, int) else i - 1
                    if known_positive(split):
                        sp.wait_ge(s["xlo_ready"], split)
                    sp.dma_start(b["xt"][:, p, :], bass.AP(t["x_t"].tensor, off, [[HID, P], [1, HID]])
                                 ).then_inc(loaded["xt"][p], 16)

                def load_picked(i, p):
                    used = sp.snap(i - 1) if not isinstance(i, int) else i - 1
                    cond = [sp.value_load(g["cond_ids"][:, bass.ds(i * 2 + n, 1)], min_val=0,
                                          max_val=NCOND - 1) for n in range(2)]
                    lora = [sp.value_load(g["lora_ids"][:, bass.ds(i * 2 + n, 1)], min_val=0,
                                          max_val=NLORA - 1) for n in range(2)]
                    w_off = [sp.snap(c * (CH * 4 * CH)) for c in cond]
                    a_off = [sp.snap(c * (P * 2 * KC * RANK)) for c in lora]
                    wa_off = [sp.snap(c * (P * 2 * RANK)) for c in lora]
                    bk_off = [sp.snap(c * (RANK * HID)) for c in lora]
                    if known_positive(used):
                        sp.wait_ge(s["out_done"], used)
                    done = loaded["lora"][p]
                    for n in range(2):
                        rows = slice(n * CH, (n + 1) * CH)
                        sp.dma_start(f(b["bd"][rows, p, :, rows]),
                                     bass.AP(t["w_kinds"].tensor, w_off[n], [[4 * CH, CH], [CH, 4], [1, CH]])
                                     ).then_inc(done, 16)
                        sp.dma_start(f(b["narrow"][:, A_GROUP[p] + n]),
                                     bass.AP(t["a_split"].tensor, a_off[n], [[2 * KC * RANK, P], [1, 2 * KC * RANK]])
                                     ).then_inc(done, 16)
                        sp.dma_start(f(b["wa"][:, p, :, n, :]),
                                     bass.AP(t["wa_split"].tensor, wa_off[n], [[2 * RANK, P], [RANK, 2], [1, RANK]])
                                     ).then_inc(done, 16)
                        bk_h = bass.AP(t["bk_hi"].tensor, bk_off[n], [[HID, RANK], [1, HID]])
                        bk_l = bass.AP(t["bk_lo"].tensor, bk_off[n], [[HID, RANK], [1, HID]])
                        for base, dst, src in ((BOT, "rhs_b", bk_h), (BOT + 2 * RANK, "rhs_b", bk_h),
                                               (0, "rhs_c", bk_l)):
                            r0 = base + n * RANK
                            sp.dma_start(f(b[dst][r0:r0 + RANK, p, :]), src).then_inc(done, 16)

                def store(j, p):
                    off = sp.snap(j * (P * HID)) if not isinstance(j, int) else j * P * HID
                    ready = sp.snap(j + 1) if not isinstance(j, int) else j + 1
                    sp.wait_ge(s["out_ready"], ready)
                    sp.dma_start(bass.AP(t["out"].tensor, off, [[HID, P], [1, HID]]), b["out_sb"][:, p, :]
                                 ).then_inc(moved[p], 16)

                sp.wait_ge(s["cleared"], 1)
                load_picked(0, 0)
                load_x(1, 1)
                sp.dma_start(b["bu1"][:], t["bu1"]).then_inc(s["row_in"], 16)
                sp.dma_start(b["wu2"][:], t["wu2"]).then_inc(s["row_in"], 16)
                sp.dma_start(b["gates"][:, 0:3], t["gate_params"]).then_inc(s["gate_in"], 16)
                load_x(2, 0)
                load_picked(1, 1)
                with sp.Fori(0, NT // 2 - 2) as j:
                    i = j * 2 + 2
                    load_x(i + 1, 1)
                    load_picked(i, 0)
                    store(i - 2, 0)
                    load_x(i + 2, 0)
                    load_picked(i + 1, 1)
                    store(i - 1, 1)
                load_x(NT - 1, 1)
                load_picked(NT - 2, 0)
                store(NT - 4, 0)
                load_picked(NT - 1, 1)
                store(NT - 3, 1)
                store(NT - 2, 0)
                store(NT - 1, 1)
                for p in range(2):
                    sp.wait_ge(moved[p], 16 * (NT // 2 + 1))

            def steps(eng, step):
                step(0, 0)
                with eng.Fori(0, NT // 2 - 1) as j:
                    n = j * 2 + 1
                    step(n, 1)
                    step(n + 1, 0)
                step(NT - 1, 1)
                step(NT, 0)

            def has_new(n):
                return not isinstance(n, int) or n < NT

            def has_old(n):
                return not isinstance(n, int) or n > 0

            def arrived(n, p, each):
                return (n - p) * (each // 2) + each

            @block.scalar
            def _(act):
                def split_x(i, p):
                    act.wait_ge(loaded["xt"][p], arrived(i, p, 16))
                    if known_positive(i - 1):
                        act.wait_ge(s["s1b_done"], i - 1)
                    act.copy(b["xt_hi"][:, p, :], b["xt"][:, p, :]).then_inc(s["xhi_ready"], 1)

                act.wait_ge(s["lvu_ready"], 1)
                act.activation(b["lv_ln"][:], b["lv_u"][:], ACT.Ln).then_inc(s["ln_ready"], 1)
                split_x(0, 0)
                for p in range(2):
                    act.wait_ge(moved[p], 16)
                act.copy(wu_groups(0), wu_raw()).then_inc(s["wu_hi_ready"], 1)
                act.wait_ge(s["wq_in"], 32)
                act.copy(wq_groups(0, 0), wq_raw(0))
                act.copy(wq_groups(1, 0), wq_raw(1)).then_inc(s["wq_hi_ready"], 1)
                act.wait_ge(s["const_done"], 1)
                act.wait_ge(s["const_cleared"], 1)
                for row in (2 * RANK, BOT):
                    for p in range(2):
                        last = act.copy(b["rhs_c"][row:row + 1, p, :], pm_ps[row:row + 1, :])
                last.then_inc(s["const_hi_ready"], 1)
                act.wait_ge(s["v_mm_ready"], 1)
                act.copy(b["rhs_a"][:], out_ps[:]).then_inc(s["va_ready"], 1)
                act.wait_ge(s["gates_ready"], 1)

                def step(n, p):
                    if has_old(n):
                        act.wait_ge(s["s1b_done"], n)
                        act.copy(b["pm_hi"][:, 0:HALF], pm_ps[:, 0:HALF]).then_inc(s["pm_hi0_ready"], 1)
                        act.copy(b["pm_hi"][:, HALF:], pm_ps[:, HALF:]).then_inc(s["pm_hi1_ready"], 1)
                        act.wait_ge(s["ut_done"], n)
                        act.copy(b["lhs_a"][:], misc_ps[:, 0:P])
                        act.copy(b["lhs_b"][0:BOT, :], misc_ps[0:BOT, 0:P]).then_inc(s["ut_ready"], 1)
                    if has_new(n):
                        act.wait_ge(s["s1a_done"], n + 1)
                        act.copy(b["pa_hi"][:, p, :], pa_ps[:, 0:PAW]).then_inc(s["pa_hi_ready"], 1)
                    if not isinstance(n, int) or n + 1 < NT:
                        split_x(n + 1, 1 - p)
                    if has_old(n):
                        act.wait_ge(s["out_done"], n)
                        act.wait_ge(moved[1 - p], arrived(n - 1, 1 - p, 16))
                        act.copy(b["out_sb"][:, 1 - p, :], out_ps[:]).then_inc(s["out_ready"], 1)
                    if has_new(n):
                        act.wait_ge(s["qt_done"], n + 1)
                        act.copy(b["q_a"][:], misc_ps[:, 0:P])
                        act.copy(b["q_b"][0:BOT, :], misc_ps[0:BOT, 0:P]).then_inc(s["qt_ready"], 1)
                        act.wait_ge(s["z_ready"], n + 1)
                        act.activation(b["z2"][:], b["z"][:], ACT.Square, scale=0.044715 ** 0.5
                                       ).then_inc(s["z2_ready"], 1)
                        act.wait_ge(s["arg_ready"], n + 1)
                        act.activation(b["th"][:], b["arg"][:], ACT.Tanh, scale=TANH_C
                                       ).then_inc(s["tanh_ready"], 1)
                        act.wait_ge(s["negmax_ready"], n + 1)
                        act.activation(b["probs"][:], b["logits"][:], ACT.Exp, bias=c1(NEGMAX),
                                       accum_out=c1(ESUM)).then_inc(s["exp_ready"], 1)
                        act.wait_ge(s["et_done"], n + 1)
                        act.copy(b["e_t"][:].rearrange("p c n -> p (c n)"), misc_ps[:, P:3 * P]
                                 ).then_inc(s["et_ready"], 1)
                        act.wait_ge(s["lsum_ready"], n + 1)
                        act.activation(c1(LTANH), c1(LSUM), ACT.Tanh, scale=0.25, bias=b["gates"][:, 3:4]
                                       ).then_inc(s["ltanh_ready"], 1)
                        if not has_old(n):
                            act.wait_ge(s["norm_ready"], 1)
                        act.wait_ge(s["ltanh_ready"], n + 1)
                        act.activation(c1(UNC), c1(LTANH), ACT.Identity, scale=1.25,
                                       bias=g["norm_var"][:, bass.ds(n, 1)]).then_inc(s["unc_ready"], 1)
                        act.wait_ge(s["unorm_ready"], n + 1)
                        act.activation(c1(GTANH), c1(UNORM), ACT.Tanh, scale=b["gates"][:, 4:5],
                                       bias=b["gates"][:, 5:6]).then_inc(s["gtanh_ready"], 1)

                steps(act, step)

            @block.gpsimd
            def _(pool):
                pool.memset(f(b["bd"][:]), 0.0).then_inc(s["cleared"], 1)

                def split_x(i, p):
                    ready = i + 1 if isinstance(i, int) else pool.snap(i + 1)
                    pool.wait_ge(s["xhi_ready"], ready)
                    pool.tensor_tensor(b["xt_lo"][:, p, :], b["xt"][:, p, :], f(b["xt_hi"][:, p, :]),
                                       ALU.subtract).then_inc(s["xlo_ready"], 1)

                split_x(0, 0)

                def step(n, p):
                    if not isinstance(n, int) or n + 1 < NT:
                        split_x(n + 1, 1 - p)

                steps(pool, step)

            @block.tensor
            def _(pe):
                for h in range(2):
                    c = slice(h * HALF, (h + 1) * HALF)
                    last = pe.matmul(pm_ps[:, c], g["ones"][:], g["const_part"][:, c], start=True, stop=True)
                last.then_inc(s["const_done"], 1)
                for h in range(2):
                    c = slice(h * HALF, (h + 1) * HALF)
                    for k in range(KC):
                        last = product3(pe, out_ps[:, c], g["wvu_hi"][:, k, :], g["wvu_lo"][:, k, :],
                                        m_hi[:, k, c], m_lo[:, k, c], k == 0, k == KC - 1)
                last.then_inc(s["v_mm_ready"], 1)
                pe.wait_ge(s["wu_split"], 1)
                pe.wait_ge(s["wq_split"], 1)
                pe.wait_ge(s["cleared"], 1)

                def step(n, p):
                    o = 1 - p
                    if has_new(n):
                        pe.wait_ge(s["xlo_ready"], n + 1)
                        pe.wait_ge(loaded["lora"][p], arrived(n, p, LPT))
                        if known_positive(n):
                            pe.wait_ge(s["pa_lo_ready"], n)
                    for k in range(KC):
                        if has_new(n):
                            x_h = b["xt_hi"][:, p, k * P:(k + 1) * P]
                            x_l = b["xt_lo"][:, p, k * P:(k + 1) * P]
                            g0 = 2 * p
                            n_h, n_l = (b["narrow"][:, g0:g0 + 2 + NUG + NQG, part, k, :] for part in range(2))
                            last = product3(pe, pa_ps[:, 0:PAW], x_h, x_l, n_h, n_l, k == 0, k == KC - 1)
                            if k == KC - 1:
                                last.then_inc(s["s1a_done"], 1)
                        if not has_old(n):
                            if k == KC // 2:
                                pe.wait_ge(s["vb_ready"], 1)
                                pe.wait_ge(s["lsum1_ready"], 1)
                                pe.matmul(out_ps[:, 0:1], g["ones"][:], b["mean"][:, 0:1], start=True, stop=True
                                          ).then_inc(s["mean_done"], 1)
                            continue
                        if k == 0:
                            pe.wait_ge(s["et_ready"], n)
                            for c in range(2):
                                last = pe.matmul(misc_ps[:, 3 * P:3 * P + BOT], b["e_t"][:, c, :], g["vd"][:, c, :],
                                                 start=(c == 0), stop=(c == 1))
                            last.then_inc(s["u_done"], 1)
                        if k == 4:
                            pe.wait_ge(s["u_split"], n)
                            pe.transpose(misc_ps[:, 0:P], f(b["u_sb"][:]), g["ident"][:]).then_inc(s["ut_done"], 1)
                        if k == KC - 1:
                            pe.wait_ge(s["ut_ready"], n)
                            lo_ps = misc_ps[0:2 * RANK, P:2 * P]
                            w_h, w_l = b["bd"][:, o, 2, :], b["bd"][:, o, 3, :]
                            product3(pe, lo_ps, b["pa_hi"][:, o, LORA[o]], b["pa_lo"][:, o, LORA[o]],
                                     w_h, w_l, True, False)
                            pe.matmul(lo_ps, b["wa"][:, o, 0].rearrange("p n r -> p (n r)"), b["lhs_a"][:], start=False, stop=False)
                            pe.matmul(lo_ps, b["wa"][0:BOT, o, 1].rearrange("p n r -> p (n r)"), b["lhs_b"][0:BOT, :], start=False,
                                      stop=True).then_inc(s["h_done"], 1)
                    if has_old(n):
                        pe.wait_ge(s["pm_lo1_ready"], n)
                        w_h, w_l = b["bd"][:, o, 2, :], b["bd"][:, o, 3, :]
                        cs = [slice(0, HALF), slice(HALF, HID)]
                        for lhs, rhs, start in ((w_h, "pm_hi", True), (w_h, "pm_lo", False), (w_l, "pm_hi", False)):
                            for c in cs:
                                pe.matmul(out_ps[:, c], lhs, b[rhs][:, c], start=start, stop=False)
                        pe.wait_ge(s["h_ready"], n)
                        nc_rows = BOT + 1
                        for lhs, rhs, end in ((b["lhs_a"][:], b["rhs_a"][:], False),
                                              (b["lhs_b"][:], b["rhs_b"][:, o, :], False),
                                              (b["lhs_c"][0:nc_rows, :], b["rhs_c"][0:nc_rows, o, :], True)):
                            for c in cs:
                                last = pe.matmul(out_ps[:, c], lhs, rhs[:, c], start=False, stop=end)
                        last.then_inc(s["out_done"], 1)
                    if has_new(n):
                        pe.wait_ge(s["pa_lo_ready"], n + 1)
                        if known_positive(n):
                            pe.wait_ge(s["z_ready"], n)
                        product3(pe, mix_ps[:, 0:HQW], b["bd"][:, p, 0, :], b["bd"][:, p, 1, :],
                                 b["pa_hi"][:, p, HQ[p]], b["pa_lo"][:, p, HQ[p]],
                                 True, True).then_inc(s["mixq_done"], 1)
                        if known_positive(n):
                            pe.wait_ge(s["pm_lo1_ready"], n)
                        if not has_old(n):
                            pe.wait_ge(s["const_placed"], 1)
                        for k in range(KC):
                            x_h = b["xt_hi"][:, p, k * P:(k + 1) * P]
                            x_l = b["xt_lo"][:, p, k * P:(k + 1) * P]
                            first, end = k == 0, k == KC - 1
                            for lhs, m, a, z in ((x_h, m_hi, first, False), (x_h, m_lo, False, False),
                                                 (x_l, m_hi, False, end)):
                                for h in range(2):
                                    c = slice(h * HALF, (h + 1) * HALF)
                                    last = pe.matmul(pm_ps[:, c], lhs, m[:, k, c], start=a, stop=z)
                            if end:
                                last.then_inc(s["s1b_done"], 1)
                            if k == 0:
                                pe.wait_ge(s["q_split"], n + 1)
                                if known_positive(n):
                                    pe.wait_ge(s["hm_ready"], n)
                                pe.transpose(misc_ps[:, 0:P], f(b["query"][:]), g["ident"][:]
                                             ).then_inc(s["qt_done"], 1)
                            if k == 2:
                                pe.wait_ge(s["qt_ready"], n + 1)
                                if known_positive(n):
                                    pe.wait_ge(s["logits_ready"], n)
                                pe.matmul(score_ps, b["q_a"][:], g["router_a"][:], start=True, stop=False)
                                pe.matmul(score_ps, b["q_b"][0:BOT + 2, :], g["router_b"][0:BOT + 2, :],
                                          start=False, stop=True).then_inc(s["score_done"], 1)
                            if k == 6:
                                pe.wait_ge(s["exp_ready"], n + 1)
                                for c in range(2):
                                    last = pe.transpose(misc_ps[:, (c + 1) * P:(c + 2) * P],
                                                        b["probs"][:, c * P:(c + 1) * P], g["ident"][:])
                                last.then_inc(s["et_done"], 1)

                steps(pe, step)

            @block.vector
            def _(dve):
                spacer = g["spacer"][:]
                chain = [0]

                def link(ins):
                    chain[0] += 1
                    ins.then_inc(s["m_chain"], 1)
                    dve.wait_ge(s["m_chain"], chain[0])

                var = g["var"][:]
                dve.tensor_scalar(b["lv_u"][:], var, 1.0, None, ALU.add).then_inc(s["lvu_ready"], 1)
                dve.wait_ge(s["lvu_ready"], 1)
                link(dve.tensor_scalar(b["lv_d"][:], b["lv_u"][:], -1.0, None, ALU.add))
                link(dve.tensor_scalar(b["lv_is1"][:], b["lv_d"][:], 0.0, None, ALU.is_equal))
                link(dve.tensor_tensor(b["lv_d"][:], b["lv_d"][:], b["lv_is1"][:], ALU.add))
                link(dve.reciprocal(b["lv_d"][:], b["lv_d"][:]))
                dve.wait_ge(s["ln_ready"], 1)
                link(dve.tensor_tensor(b["lv_num"][:], b["lv_ln"][:], b["lv_is1"][:], ALU.add))
                link(dve.tensor_tensor(b["lv_num"][:], b["lv_num"][:], b["lv_d"][:], ALU.mult))
                link(dve.tensor_tensor(b["lv_log"][:], b["lv_num"][:], var, ALU.mult))
                dve.tensor_reduce(b["mean"][:, 0:1], b["lv_log"][:], AX.X, ALU.add).then_inc(s["lsum1_ready"], 1)
                dve.memset(f(b["q_b"][BOT:P, :]), 1.0)
                dve.memset(f(b["lhs_c"][:]), 1.0)
                dve.memset(f(b["rhs_c"][2 * RANK:BOT, :, :]), 0.0).then_inc(s["const_cleared"], 1)
                dve.wait_ge(s["wu_hi_ready"], 1)
                dve.tensor_tensor(wu_groups(1), wu_raw(), f(wu_groups(0)), ALU.subtract
                                  ).then_inc(s["wu_split"], 1)
                dve.wait_ge(s["wq_hi_ready"], 1)
                for half in range(2):
                    last = dve.tensor_tensor(wq_groups(half, 1), wq_raw(half), f(wq_groups(half, 0)), ALU.subtract)
                last.then_inc(s["wq_split"], 1)
                dve.wait_ge(s["const_hi_ready"], 1)
                for p in range(2):
                    last = dve.tensor_tensor(b["rhs_c"][BOT:BOT + 1, p, :], pm_ps[BOT:BOT + 1, :],
                                             f(b["rhs_c"][BOT:BOT + 1, p, :]), ALU.subtract)
                last.then_inc(s["const_placed"], 1)
                dve.wait_ge(s["gate_in"], 16)
                dve.tensor_scalar(b["gates"][:, 3:6], b["gates"][:, 0:3], 0.5, None, ALU.mult
                                  ).then_inc(s["gates_ready"], 1)
                dve.wait_ge(s["va_ready"], 1)
                for p in range(2):
                    last = dve.tensor_tensor(b["rhs_b"][0:BOT, p, :], out_ps[0:BOT, :],
                                             f(b["rhs_a"][0:BOT, :]), ALU.subtract)
                last.then_inc(s["vb_ready"], 1)
                dve.wait_ge(s["mean_done"], 1)
                link(dve.tensor_scalar(b["mean"][:, 1:2], out_ps[:, 0:1], 1.0 / (NT * P), 1e-6, ALU.mult, ALU.add))
                link(dve.reciprocal(b["mean"][:, 2:3], b["mean"][:, 1:2]))
                link(dve.tensor_scalar(b["lv_num"][:], b["lv_log"][:], b["mean"][:, 2:3], 0.5, ALU.mult, ALU.mult))
                dve.tensor_scalar(g["norm_var"][:], b["lv_num"][:], 1.25, None, ALU.add
                                  ).then_inc(s["norm_ready"], 1)
                dve.wait_ge(s["row_in"], 32)

                def step(n, p):
                    if has_old(n):
                        dve.wait_ge(s["pm_hi0_ready"], n)
                        dve.tensor_tensor(b["pm_lo"][:, 0:HALF], pm_ps[:, 0:HALF], f(b["pm_hi"][:, 0:HALF]),
                                          ALU.subtract).then_inc(s["pm_lo0_ready"], 1)
                        u_ps = misc_ps[:, 3 * P:3 * P + BOT]
                        dve.wait_ge(s["u_done"], n)
                        dve.wait_ge(s["scale_ready"], n)
                        dve.tensor_scalar(b["u_sb"][:, 0:BOT], u_ps, c1(SCALE), None, ALU.mult
                                          ).then_inc(s["uhi_ready"], 1)
                        dve.wait_ge(s["uhi_ready"], n)
                        dve.scalar_tensor_tensor(b["u_sb"][:, BOT:], u_ps, c1(SCALE), f(b["u_sb"][:, 0:BOT]),
                                                 ALU.mult, ALU.subtract).then_inc(s["u_split"], 1)
                        dve.wait_ge(s["pm_hi1_ready"], n)
                        dve.tensor_tensor(b["pm_lo"][:, HALF:], pm_ps[:, HALF:], f(b["pm_hi"][:, HALF:]),
                                          ALU.subtract).then_inc(s["pm_lo1_ready"], 1)
                        dve.wait_ge(s["h_done"], n)
                        dve.tensor_tensor(b["hm"][:], misc_ps[0:2 * RANK, P:2 * P], g["lora_mask"][:], ALU.mult
                                          ).then_inc(s["hm_ready"], 1)
                        dve.wait_ge(s["hm_ready"], n)
                        dve.tensor_copy(b["lhs_c"][0:2 * RANK, :], b["hm"][:]).then_inc(s["hhi_ready"], 1)
                        dve.tensor_copy(b["lhs_b"][BOT:BOT + 2 * RANK, :], b["hm"][:])
                        dve.wait_ge(s["hhi_ready"], n)
                        dve.tensor_tensor(b["lhs_b"][BOT + 2 * RANK:, :], b["hm"][:], f(b["lhs_c"][0:2 * RANK, :]),
                                          ALU.subtract).then_inc(s["h_ready"], 1)
                    if has_new(n):
                        dve.wait_ge(s["pa_hi_ready"], n + 1)
                        dve.tensor_tensor(b["pa_lo"][:, p, :], pa_ps[:, 0:PAW], f(b["pa_hi"][:, p, :]),
                                          ALU.subtract).then_inc(s["pa_lo_ready"], 1)
                        q_ps = mix_ps[:, NUNC:NUNC + BOT]
                        dve.wait_ge(s["mixq_done"], n + 1)
                        dve.tensor_copy(b["query"][:, 0:BOT], q_ps).then_inc(s["q_hi_ready"], 1)
                        dve.wait_ge(s["q_hi_ready"], n + 1)
                        dve.tensor_tensor(b["query"][:, BOT:], q_ps, f(b["query"][:, 0:BOT]), ALU.subtract
                                          ).then_inc(s["q_split"], 1)
                        dve.tensor_tensor(b["z"][:], mix_ps[:, 0:NUNC], b["bu1"][:], ALU.add
                                          ).then_inc(s["z_ready"], 1)
                        dve.wait_ge(s["z2_ready"], n + 1)
                        dve.scalar_tensor_tensor(b["arg"][:], b["z2"][:], 1.0, b["z"][:], ALU.add, ALU.mult
                                                 ).then_inc(s["arg_ready"], 1)
                        wait_apart(dve, spacer, s["score_done"], n + 1)
                        dve.max(b["top8"][:], score_ps[:, 0:NSLOT]).then_inc(s["top8_ready"], 1)
                        wait_apart(dve, spacer, s["top8_ready"], n + 1)
                        dve.match_replace(b["rest"][:], b["top8"][:], score_ps[:, 0:NSLOT], REPLACED
                                          ).then_inc(s["rest_ready"], 1)
                        dve.wait_ge(s["rest_ready"], n + 1)
                        dve.tensor_scalar(b["penalty"][:], b["rest"][:], REPLACED, NEG, ALU.not_equal, ALU.mult
                                          ).then_inc(s["penalty_ready"], 1)
                        wait_apart(dve, spacer, s["penalty_ready"], n + 1)
                        dve.tensor_tensor_reduce(out=b["logits"][:], in0=b["penalty"][:],
                                                 in1=score_ps[:, NSLOT:2 * NSLOT], scale=1.0, scalar=-3.0e38,
                                                 op0=ALU.add, op1=ALU.max, accum_out=c1(ROWMAX)
                                                 ).then_inc(s["logits_ready"], 1)
                        dve.wait_ge(s["logits_ready"], n + 1)
                        dve.tensor_scalar(c1(NEGMAX), c1(ROWMAX), -1.0, None, ALU.mult
                                          ).then_inc(s["negmax_ready"], 1)
                        dve.wait_ge(s["tanh_ready"], n + 1)
                        dve.scalar_tensor_tensor(b["gelu"][:], b["th"][:], 1.0, b["z"][:], ALU.add, ALU.mult
                                                 ).then_inc(s["gelu_ready"], 1)
                        dve.wait_ge(s["gelu_ready"], n + 1)
                        dve.tensor_tensor_reduce(out=b["dot"][:], in0=b["gelu"][:], in1=b["wu2"][:], scale=1.0,
                                                 scalar=0.0, op0=ALU.mult, op1=ALU.add, accum_out=c1(LSUM)
                                                 ).then_inc(s["lsum_ready"], 1)
                        dve.wait_ge(s["exp_ready"], n + 1)
                        dve.reciprocal(c1(RSUM), c1(ESUM)).then_inc(s["rsum_ready"], 1)
                        dve.wait_ge(s["unc_ready"], n + 1)
                        dve.tensor_scalar(c1(CLIP), c1(UNC), 0.0, 5.0, ALU.max, ALU.min).then_inc(s["clip_ready"], 1)
                        dve.wait_ge(s["clip_ready"], n + 1)
                        dve.tensor_scalar(c1(SCALED), c1(CLIP), -0.5, 1.0 / 1.5, ALU.add, ALU.mult
                                          ).then_inc(s["scaled_ready"], 1)
                        dve.wait_ge(s["scaled_ready"], n + 1)
                        dve.tensor_scalar(c1(UNORM), c1(SCALED), 0.0, 1.0, ALU.max, ALU.min
                                          ).then_inc(s["unorm_ready"], 1)
                        dve.wait_ge(s["gtanh_ready"], n + 1)
                        dve.tensor_scalar(c1(GATE), c1(GTANH), 0.5, 0.5, ALU.mult, ALU.add).then_inc(s["gate_ready"], 1)
                        dve.wait_ge(s["gate_ready"], n + 1)
                        dve.scalar_tensor_tensor(c1(GATED), c1(GATE), 0.05, c1(GATE), ALU.is_ge, ALU.mult
                                                 ).then_inc(s["gated_ready"], 1)
                        dve.wait_ge(s["gated_ready"], n + 1)
                        dve.wait_ge(s["rsum_ready"], n + 1)
                        dve.tensor_tensor(c1(SCALE), c1(GATED), c1(RSUM), ALU.mult).then_inc(s["scale_ready"], 1)

                steps(dve, step)



def fourier_matrix(n):
    m = np.zeros((n, n))
    pos = np.arange(n)
    m[0] = n ** -0.5
    for fr in range(1, (n - 1) // 2 + 1):
        ang = 2 * np.pi * ((fr * pos) % n) / n
        m[2 * fr - 1] = np.sqrt(2.0 / n) * np.cos(ang)
        m[2 * fr] = np.sqrt(2.0 / n) * np.sin(ang)
    m[n - 1] = n ** -0.5 * (1 - 2 * (pos % 2))
    return m.astype(np.float32)


def kernel(**inputs):
    import concourse.bacc as bacc
    from concourse.bass_utils import run_bass_kernel_spmd

    a = {k: np.asarray(x) for k, x in inputs.items()}

    def chunks(m):
        return m.reshape(KC, P, -1).transpose(1, 0, 2)

    def groups(m):
        return m.T.reshape(KC, P, -1, GRP).transpose(1, 2, 0, 3).reshape(P, -1)

    x = a["x"].reshape(NT, P, HID)
    lora_a = a["L1_cond_lora_A_w"]
    lora_b = a["L1_cond_lora_B_w"]
    coefs = np.concatenate([a["L1_ffn_coefs0"], a["L1_ffn_coefs1"]], axis=2)
    masks = np.concatenate([a["L1_ffn_mask0"], a["L1_ffn_mask1"]], axis=2).view(np.uint8)

    def expert(m):
        return m.reshape(NEXP, KC, P, RENC).transpose(2, 0, 1, 3).reshape(P, NEXP, KC * RENC)

    rows = np.broadcast_to
    wvu = chunks(a["L0_ffn_Wvu"])
    data = {
        "x": x,
        "x_t": x.reshape(NT, P, KC, P).transpose(0, 3, 2, 1).reshape(NT, P, HID),
        "cond_ids": a["itok_B_0_15"].reshape(1, BATCH),
        "lora_ids": a["itok_B_6_15"].reshape(1, BATCH),
        "cond_w": a["L0_cond_weights"].transpose(1, 0, 2),
        "ident": np.eye(P, dtype=np.float32),
        "lora_mask": np.kron(np.eye(2), np.ones((RANK, CH))).astype(np.float32),
        "wvu": np.concatenate([wvu, wvu], axis=2),
        "wr": np.concatenate([a["L0_ffn_Wr"]] * 2, axis=1),
        "keys_t": np.concatenate([a["L0_ffn_aux_keys"].T] * 2, axis=0),
        "log_rel": np.concatenate([a["L0_ffn_log_rel"]] * 2).reshape(1, 2 * NSLOT),
        "lora_a": lora_a.reshape(LBLK, LPB, RANK, KC, P).transpose(0, 4, 1, 3, 2),
        "av_t": chunks(a["L0_ffn_aux_values"].T),
        "wvd_t": chunks(a["L0_ffn_Wvd"].T),
        "coefs": expert(coefs),
        "masks": np.ascontiguousarray(expert(masks)).view(np.int32),
        "enc": np.concatenate([a["L1_ffn_enc0"], a["L1_ffn_enc1"]], axis=0),
        "fourier": fourier_matrix(HID).reshape(KC, P, HID),
        "w_base_t": a["L1_ffn_W_base"].T.reshape(KC, P, HID),
        "left_blocks": np.concatenate([
            lora_b.reshape(LBLK, LPB, KC, P, RANK).transpose(0, 3, 2, 1, 4).reshape(LBLK, P, KC, P),
            a["L1_cond_base_weight"].reshape(KC, P, KC, P).transpose(2, 1, 0, 3)]),
        "cond_bias": a["L1_cond_base_bias"].reshape(KC, P).T,
        "b_base": a["L1_ffn_b_base"].reshape(1, HID),
        "wu1_t": groups(a["L0_ffn_Wu1"]).reshape(P, 2, HID),
        "wq_t": groups(a["L0_ffn_Wq"]),
        "bu1": rows(a["L0_ffn_bu1"].reshape(1, NUNC), (P, NUNC)),
        "wu2": rows(a["L0_ffn_Wu2"].reshape(1, NUNC), (P, NUNC)),
        "gate_params": np.stack([rows(a[n].reshape(-1)[:1], (P,)) for n in
                                 ("L0_ffn_bu2", "L0_ffn_gate_w1", "L0_ffn_gate_bias")], axis=1),
    }
    nc = bacc.Bacc("TRN2", target_bir_lowering=False, num_devices=1)
    arrays, aps = {}, {}
    for name, value in data.items():
        value = np.ascontiguousarray(value)
        arrays["in_" + name] = value
        aps[name] = nc.dram_tensor("in_" + name, value.shape, mybir.dt.from_np(value.dtype),
                                   kind="ExternalInput").ap()
    aps["out"] = nc.dram_tensor("out", (NT, P, HID), F32, kind="ExternalOutput").ap()
    build(nc, aps)
    r = run_bass_kernel_spmd(nc, [arrays], core_ids=[0])
    return np.asarray(r.results[0]["out"]).reshape(BATCH, CH, HID)
```

```python
from contextlib import ExitStack

import numpy as np

import concourse.bass as bass
from concourse import mybir

F32 = mybir.dt.float32
F32R = mybir.dt.float32r
I32 = mybir.dt.int32
U8 = mybir.dt.uint8
ALU = mybir.AluOpType
ACT = mybir.ActivationFunctionType
AX = mybir.AxisListType

P = 128
BATCH, CH, HID = 128, 64, 1024
NT = BATCH * CH // P
KC = HID // P
HALF = HID // 2
NCOND = 16
NLORA, RANK = 32, 16
NUNC = HID // 4
BOT = 64
RDIM = 48
NSLOT = 256
RENC = 40
NEXP = 3
GRP = RANK
NUG, NQG = NUNC // GRP, BOT // GRP
HQW = NUNC + BOT
PAW = HQW + 2 * RANK
LBLK = NLORA * RANK // P
LPB = NLORA // LBLK
NEG = -1.0e30
REPLACED = -3.0e38
VAR_A = 16
TANH_C = 0.7978845608028654


def f(ap):
    return ap.bitcast(F32)


def product3(pe, out, a_hi, a_lo, b_hi, b_lo, start, stop, skip=False):
    pe.matmul(out, a_hi, b_hi, start=start, stop=False, skip_group_check=skip)
    pe.matmul(out, a_hi, b_lo, start=False, stop=False, skip_group_check=skip)
    return pe.matmul(out, a_lo, b_hi, start=False, stop=stop, skip_group_check=skip)


def wait_apart(eng, spacer, signal, count):
    eng.wait_ge(signal, count)
    if not isinstance(count, int):
        eng.memset(spacer, 0.0)


def known_positive(count):
    return not isinstance(count, int) or count > 0


def build(nc, t):
    with ExitStack() as top:
        def sem(name):
            return top.enter_context(nc.semaphore(name))

        def tile(stack, name, shape, dt=F32, side="left"):
            return stack.enter_context(nc.sbuf_tensor(name, shape, dt, side=side))

        t["w_kinds"] = nc.dram_tensor("w_kinds", (NCOND, CH, 4, CH), F32, kind="Internal").ap()
        t["wa_split"] = nc.dram_tensor("wa_split", (NLORA, P, 2, RANK), F32, kind="Internal").ap()
        t["bk_hi"] = nc.dram_tensor("bk_hi", (NLORA * RANK, HID), F32, kind="Internal").ap()
        t["bk_lo"] = nc.dram_tensor("bk_lo", (NLORA * RANK, HID), F32, kind="Internal").ap()

        pair = [top.enter_context(nc.psum_tensor(f"pair{n}", [P, HID], F32)) for n in range(4)]

        g = {}
        for name, shape, dt in (
            ("ident", [P, P], F32), ("ident_r", [P, P], F32R), ("lora_mask", [2 * RANK, P], F32),
            ("ones", [P, P], F32), ("spacer", [1, 1], F32),
            ("cond_ids", [1, BATCH], I32), ("lora_ids", [1, BATCH], I32),
            ("vd", [P, 2, BOT], F32),
            ("wvu_hi", [P, KC, P], F32R),
            ("router_a", [P, 2 * NSLOT], F32R), ("router_b", [P, 2 * NSLOT], F32R),
            ("var", [P, NT], F32), ("norm_var", [P, NT], F32), ("const_part", [P, HID], F32),
        ):
            g[name] = tile(top, name, shape, dt)
        with ExitStack() as passing:
            g["wvu_raw"] = tile(passing, "wvu_raw", [P, KC, P])
        g["wvu_lo"] = tile(top, "wvu_lo", [P, KC, P], F32R)

        vstack = top.enter_context(ExitStack())
        v = {}
        for name, shape, dt in (
            ("v_x", [P, 4, HID], F32), ("v_hi", [P, 2, HID], F32R), ("v_lo", [P, 2, HID], F32R),
            ("v_w", [P, 4, 2, P], F32R), ("v_stats", [P, 2, 12], F32), ("v_mv", [P, 2, 2], F32),
        ):
            v[name] = tile(vstack, name, shape, dt)
        v["x_loaded"] = [sem(f"v_x_loaded{r}") for r in range(4)]
        v["w_loaded"] = [sem(f"v_w_loaded{r}") for r in range(4)]
        for name in ("v_hi_ready", "v_lo_ready", "v_mm_done", "v_bn_done", "v_aggr_done", "v_var_ready"):
            v[name] = sem(name)
        v["psum"] = pair[0:2]

        kstack = top.enter_context(ExitStack())
        g["blk_raw"] = tile(kstack, "blk_raw", [P, KC, P])
        g["raw_loaded"] = sem("raw_loaded")
        k_hi, k_lo = setup_block(nc, t, g, v, pair, sem, tile, kstack)
        m_hi = tile(top, "m_hi", [P, KC, HID], F32R, side="right")
        m_lo = tile(top, "m_lo", [P, KC, HID], F32R, side="right")
        fold_block(nc, t, g, v, pair, sem, tile, k_hi, k_lo, m_hi, m_lo)
        kstack.close()
        vstack.close()
        main_block(nc, t, g, pair, sem, tile, m_hi, m_lo)



def var_load(sp, t, g, v, n, slot):
    x_off = sp.snap(n * (P * HID)) if not isinstance(n, int) else n * P * HID
    used = sp.snap(n - 3) if not isinstance(n, int) else n - 3
    ids = [sp.value_load(g["cond_ids"][:, bass.ds(n * 2 + b, 1)], min_val=0, max_val=NCOND - 1)
           for b in range(2)]
    offs = [sp.snap(i * (CH * 4 * CH)) for i in ids]
    if known_positive(used):
        sp.wait_ge(v["v_lo_ready"], used)
    sp.dma_start(v["v_x"][:, slot, :], bass.AP(t["x"].tensor, x_off, [[HID, P], [1, HID]])
                 ).then_inc(v["x_loaded"][slot], 16)
    if known_positive(used):
        sp.wait_ge(v["v_mm_done"], used)
    for b in range(2):
        src = bass.AP(t["w_kinds"].tensor, offs[b], [[4 * CH, CH], [CH, 2], [1, CH]])
        sp.dma_start(f(v["v_w"][b * CH:(b + 1) * CH, slot, :, b * CH:(b + 1) * CH]), src
                     ).then_inc(v["w_loaded"][slot], 16)


def var_hi(act, v, n, slot):
    s = slot % 2
    act.wait_ge(v["x_loaded"][slot], (n - slot) * 4 + 16)
    if known_positive(n - 1):
        act.wait_ge(v["v_mm_done"], n - 1)
    act.copy(v["v_hi"][:, s, :], v["v_x"][:, slot, :]).then_inc(v["v_hi_ready"], 1)


def var_lo(pool, v, n, slot):
    s = slot % 2
    ready = n + 1 if isinstance(n, int) else pool.snap(n + 1)
    pool.wait_ge(v["v_hi_ready"], ready)
    pool.tensor_tensor(v["v_lo"][:, s, :], v["v_x"][:, slot, :], f(v["v_hi"][:, s, :]),
                       ALU.subtract).then_inc(v["v_lo_ready"], 1)


def var_mm(pe, v, n, slot):
    s = slot % 2
    pe.wait_ge(v["v_lo_ready"], n + 1)
    pe.wait_ge(v["w_loaded"][slot], quarter_count(n, slot))
    if known_positive(n - 1):
        pe.wait_ge(v["v_bn_done"], n - 1)
    w_hi, w_lo = v["v_w"][:, slot, 0, :], v["v_w"][:, slot, 1, :]
    out = v["psum"][s]
    for h in range(2):
        c = slice(h * HALF, (h + 1) * HALF)
        last = product3(pe, out[:, c], w_hi, w_lo, v["v_hi"][:, s, c], v["v_lo"][:, s, c], True, True)
    last.then_inc(v["v_mm_done"], 1)


def quarter_count(n, slot):
    return (n - slot) * 8 + 32


def var_stats(dve, spacer, g, v, n, slot):
    s = slot % 2
    dve.wait_ge(v["v_mm_done"], n + 1)
    if known_positive(n - 1):
        dve.wait_ge(v["v_aggr_done"], n - 1)
    dve.bn_stats(v["v_stats"][:, s, 0:6], v["psum"][s][:, 0:HALF])
    dve.bn_stats(v["v_stats"][:, s, 6:12], v["psum"][s][:, HALF:HID]).then_inc(v["v_bn_done"], 1)
    if known_positive(n - 1):
        dve.wait_ge(v["v_var_ready"], n - 1)
    wait_apart(dve, spacer, v["v_bn_done"], n + 1)
    dve.bn_aggr(v["v_mv"][:, s, :], v["v_stats"][:, s, :]).then_inc(v["v_aggr_done"], 1)
    dve.wait_ge(v["v_aggr_done"], n + 1)
    dve.tensor_copy(g["var"][:, bass.ds(n, 1)], v["v_mv"][:, s, 1:2]).then_inc(v["v_var_ready"], 1)



BESIDE = {0: [("CS", 0)], 1: [("CS", 1)], 2: [("CS", 2)], 3: [("K", 0), ("WA", 0)], 4: [("K", 1)],
          5: [("K", 2)], 6: [("K", 3), ("WA", 1)], 7: [("K", 4)], 8: [("K", 5)],
          9: [("K", 6), ("WA", 2)], 10: [("K", 7)], 11: [("VD", 0)], 12: [("WA", 3)]}
CS_PARTS = (range(0, 4), range(4, 6), range(6, 8))


def beside(n, kind):
    return dict(BESIDE.get(n, ())).get(kind)


def setup_block(nc, t, g, v, pair, sem, tile, kstack):
    with ExitStack() as early:
        with ExitStack() as passing:
            fourier = tile(passing, "fourier", [P, KC, HID])
            kf = tile(passing, "kf", [P, KC, HID])
        k_hi = tile(kstack, "k_hi", [P, KC, HID], F32R)
        k_lo = tile(kstack, "k_lo", [P, KC, HID], F32R)

        def small_tile(name, shape, dt=F32):
            return tile(early, name, shape, dt, "right")

        with ExitStack() as passing:
            enc = tile(passing, "enc", [RENC, HID], F32, "right")
        enc_lo = small_tile("enc_lo", [RENC, HID], F32R)
        enc_hi = small_tile("enc_hi", [RENC, HID], F32R)
        cs_hi = small_tile("cs_hi", [RENC, HID], F32R)
        cs_lo = small_tile("cs_lo", [RENC, HID], F32R)
        w_raw = small_tile("w_raw", [CH, NCOND, CH])
        w_plus = small_tile("w_plus", [CH, NCOND, CH])
        w_kinds = small_tile("w_kinds_sb", [CH, NCOND, 4, CH], F32R)
        coefs = small_tile("coefs", [P, NEXP, KC * RENC])
        masks = small_tile("masks", [P, NEXP, KC * RENC // 4], I32)
        av_t = small_tile("av_t", [P, KC, NSLOT])
        wvd_t = small_tile("wvd_t", [P, KC, BOT])
        wvu = g["wvu_raw"]
        a_raw = small_tile("a_raw", [P, LPB, KC, RANK])
        a_hi = small_tile("a_hi", [P, LPB, KC, RANK], F32R)
        a_lo = small_tile("a_lo", [P, LPB, KC, RANK], F32R)
        wa_split = small_tile("wa_split_sb", [P, NLORA, 2, RANK], F32R)
        wr = small_tile("wr", [RDIM, 2 * BOT])
        wtw = small_tile("wtw", [BOT, 2 * BOT])
        keys = small_tile("keys", [P, NSLOT])
        router = small_tile("router", [P, 2 * NSLOT])
        logrel = small_tile("logrel", [1, NSLOT])
        logrel_hi = small_tile("logrel_hi", [1, NSLOT], F32R)
        logrel_lo = small_tile("logrel_lo", [1, NSLOT], F32R)

        names = ("ids_in base_in w_in enc_in coefs_in av_in a_in wvu_in wr_in keys_in logrel_in "
                 "w_stored wa_stored logrel_placed s_chain zeroed w_plus_ready w_hi_ready w_kinds_ready "
                 "enc_hi_ready enc_split wvu_hi_ready wvu_split wsum_ready a_hi_ready a_split_ready "
                 "wa_mm_done wa_split_ready vd_mm_done wtw_mm_done wtw_ready g_mm_done "
                 "router_ready cs_mm_done cs_hi_ready cs_split k_mm_done k_sum_ready k_hi_ready "
                 "logrel_split").split()
        s = {n: sem(n) for n in names}
        fourier_in = [sem(f"fourier_in{k}") for k in range(KC // 2)]
        wbase_in = [sem(f"wbase_in{k}") for k in range(KC // 2)]
        k_ps = pair[2]
        small = pair[3][:, 0:HALF]
        wa_bank = pair[3][:, HALF:HID]
        LEFT, RIGHT = slice(0, HALF), slice(HALF, HID)

        with nc.Block() as block:

            @block.sync
            def _(sp):
                def load_two(dst, src, k, done):
                    sp.dma_start(dst[:, 2 * k:2 * k + 2, :], t[src][2 * k:2 * k + 2].rearrange("k p n -> p k n")
                                 ).then_inc(done[k], 16)

                def load_rows(n):
                    sp.dma_start(v["v_x"][:, n, :], bass.AP(t["x"].tensor, n * P * HID, [[HID, P], [1, HID]])
                                 ).then_inc(v["x_loaded"][n], 16)

                sp.dma_start(w_raw[:], t["cond_w"]).then_inc(s["w_in"], 16)
                sp.dma_start(g["ident"][:], t["ident"]).then_inc(s["w_in"], 16)
                for name in ("cond_ids", "lora_ids"):
                    sp.dma_start(g[name][:], t[name]).then_inc(s["ids_in"], 16)
                sp.dma_start(coefs[:], t["coefs"]).then_inc(s["coefs_in"], 16)
                sp.dma_start(masks[:], t["masks"]).then_inc(s["coefs_in"], 16)
                load_two(fourier, "fourier", 0, fourier_in)
                load_rows(0)
                load_two(fourier, "fourier", 1, fourier_in)
                sp.wait_ge(s["w_kinds_ready"], 2)
                sp.dma_start(t["w_kinds"].rearrange("n c k d -> c n k d"), f(w_kinds[:])
                             ).then_inc(s["w_stored"], 16)
                sp.wait_ge(s["zeroed"], 1)
                sp.wait_ge(s["ids_in"], 32)
                for n in range(2):
                    ids = [sp.value_load(g["cond_ids"][:, 2 * n + b:2 * n + b + 1], min_val=0,
                                         max_val=NCOND - 1) for b in range(2)]
                    for b in range(2):
                        src = f(w_kinds[:, bass.ds(ids[b], 1), 0:2, :]).rearrange("c n k d -> c (n k) d")
                        sp.dma_start(f(v["v_w"][b * CH:(b + 1) * CH, n, :, b * CH:(b + 1) * CH]), src
                                     ).then_inc(v["w_loaded"][n], 16)
                    if n == 0:
                        load_rows(1)
                        load_two(fourier, "fourier", 2, fourier_in)
                        sp.dma_start(g["const_part"][0:1, :], t["b_base"]).then_inc(s["base_in"], 16)
                load_two(fourier, "fourier", 3, fourier_in)
                sp.wait_ge(s["w_stored"], 16)
                for n in range(2, VAR_A):
                    var_load(sp, t, g, v, n, n % 4)
                    if n in (2, 3, 4, 5):
                        load_two(kf, "w_base_t", n - 2, wbase_in)
                    if n == VAR_A // 2:
                        sp.dma_start(g["blk_raw"][:], left_block(t, 0)).then_inc(g["raw_loaded"], 16)
                        sp.dma_start(av_t[:], t["av_t"]).then_inc(s["av_in"], 16)
                        sp.dma_start(wvd_t[:], t["wvd_t"]).then_inc(s["av_in"], 16)
                sp.wait_ge(s["logrel_split"], 1)
                sp.wait_ge(s["router_ready"], 1)
                for row, src in ((BOT, logrel_hi), (BOT + 1, logrel_lo)):
                    for h in range(2):
                        sp.dma_start(f(g["router_b"][row:row + 1, h * NSLOT:(h + 1) * NSLOT]), f(src[:])
                                     ).then_inc(s["logrel_placed"], 16)
                var_load(sp, t, g, v, VAR_A, VAR_A % 4)
                sp.wait_ge(s["wa_split_ready"], 1)
                sp.dma_start(t["wa_split"].rearrange("l p s r -> p l s r"), f(wa_split[:])
                             ).then_inc(s["wa_stored"], 16)
                sp.wait_ge(s["base_in"], 32)
                sp.wait_ge(s["logrel_placed"], 64)
                sp.wait_ge(s["wa_stored"], 16)

            @block.scalar
            def _(act):
                def load_a(c):
                    act.dma_start(a_raw[:], t["lora_a"][c * LPB:(c + 1) * LPB].rearrange("l p (k r) -> p l k r", r=RANK)
                                  ).then_inc(s["a_in"], 16)

                act.dma_start(wr[:], t["wr"]).then_inc(s["wr_in"], 16)
                act.dma_start(keys[:], t["keys_t"]).then_inc(s["keys_in"], 16)
                act.dma_start(logrel[:], t["log_rel"]).then_inc(s["logrel_in"], 16)
                act.dma_start(enc[:], t["enc"]).then_inc(s["enc_in"], 16)
                act.wait_ge(s["w_in"], 32)
                act.copy(w_kinds[:, :, 0, :], w_raw[:]).then_inc(s["w_hi_ready"], 1)
                act.wait_ge(s["w_plus_ready"], 1)
                act.copy(w_kinds[:, :, 2, :], w_plus[:]).then_inc(s["w_hi_ready"], 1)
                act.wait_ge(s["enc_in"], 16)
                act.copy(enc_hi[:], enc[:]).then_inc(s["enc_hi_ready"], 1)
                def k_high(k):
                    act.wait_ge(s["k_sum_ready"], k + 1)
                    act.copy(k_hi[:, k, :], kf[:, k, :]).then_inc(s["k_hi_ready"], 1)

                def a_high(c):
                    if c == 0:
                        act.wait_ge(s["wvu_in"], 16)
                        act.copy(g["wvu_hi"][:], wvu[:]).then_inc(s["wvu_hi_ready"], 1)
                    else:
                        act.wait_ge(s["wa_mm_done"], c)
                    act.wait_ge(s["a_in"], 16 * (c + 1))
                    act.copy(a_hi[:], a_raw[:]).then_inc(s["a_hi_ready"], 1)

                for n in range(VAR_A):
                    var_hi(act, v, n, n % 4)
                    if n == 0:
                        act.dma_start(wvu[:], t["wvu"]).then_inc(s["wvu_in"], 16)
                        load_a(0)
                        act.dma_start(g["lora_mask"][:], t["lora_mask"]).then_inc(s["base_in"], 16)
                    if beside(n, "CS") == 2:
                        act.wait_ge(s["cs_mm_done"], 1)
                        act.mul(cs_hi[:], k_ps[0:RENC, :], 0.5).then_inc(s["cs_hi_ready"], 1)
                    if (i := beside(n + 1, "WA")) is not None:
                        a_high(i)
                    if (i := beside(n - 1, "K")) is not None:
                        k_high(i)
                    if (i := beside(n, "WA")) is not None and i + 1 < LBLK:
                        act.wait_ge(s["a_split_ready"], i + 1)
                        load_a(i + 1)

            @block.gpsimd
            def _(pool):
                pool.memset(g["ones"][:], 1.0)
                pool.memset(f(g["router_b"][:]), 0.0)
                pool.memset(g["const_part"][:], 0.0)
                pool.memset(f(v["v_w"][:]), 0.0).then_inc(s["zeroed"], 1)
                def k_low(k):
                    pool.wait_ge(s["k_hi_ready"], k + 1)
                    pool.tensor_tensor(k_lo[:, k, RIGHT], kf[:, k, RIGHT], f(k_hi[:, k, RIGHT]), ALU.subtract)

                for n in range(VAR_A):
                    var_lo(pool, v, n, n % 4)
                    if (i := beside(n - 1, "K")) is not None:
                        k_low(i)

            @block.tensor
            def _(pe):
                pe.wait_ge(s["wr_in"], 16)
                pe.matmul(small[0:BOT, 0:2 * BOT], wr[:, 0:BOT], wr[:], start=True, stop=True
                          ).then_inc(s["wtw_mm_done"], 1)
                pe.wait_ge(s["keys_in"], 16)
                pe.wait_ge(s["wtw_ready"], 1)
                pe.matmul(small[:, 0:NSLOT], wtw[:], keys[0:BOT, :], start=True, stop=True
                          ).then_inc(s["g_mm_done"], 1)

                def cs_part(part):
                    pe.wait_ge(s["wsum_ready"], 1)
                    for k in CS_PARTS[part]:
                        pe.wait_ge(fourier_in[k // 2], 16)
                        for c in (LEFT, RIGHT):
                            last = pe.matmul(k_ps[0:RENC, c], coefs[:, 0, k * RENC:(k + 1) * RENC],
                                             fourier[:, k, c], start=(k == 0), stop=(k == KC - 1))
                    if k == KC - 1:
                        last.then_inc(s["cs_mm_done"], 1)

                def k_chunk(k):
                    if k:
                        pe.wait_ge(s["k_sum_ready"], k)
                    else:
                        pe.wait_ge(s["enc_split"], 1)
                        pe.wait_ge(s["cs_split"], 1)
                    e = slice(k * P, (k + 1) * P)
                    for c in (LEFT, RIGHT):
                        last = product3(pe, k_ps[:, c], enc_hi[:, e], enc_lo[:, e], cs_hi[:, c], cs_lo[:, c],
                                        True, True)
                    last.then_inc(s["k_mm_done"], 1)

                def wa_block(c):
                    pe.wait_ge(s["wvu_split"], 1)
                    pe.wait_ge(s["a_split_ready"], c + 1)
                    for k in range(KC):
                        last = product3(pe, wa_bank[:, c * P:(c + 1) * P],
                                        g["wvu_hi"][:, k, :], g["wvu_lo"][:, k, :],
                                        a_hi[:, :, k, :], a_lo[:, :, k, :], k == 0, k == KC - 1)
                    last.then_inc(s["wa_mm_done"], 1)

                def value_operand(_):
                    pe.wait_ge(s["av_in"], 32)
                    pe.wait_ge(s["router_ready"], 1)
                    for b in range(2):
                        for k in range(KC):
                            last = pe.matmul(small[:, b * BOT:(b + 1) * BOT], av_t[:, k, b * P:(b + 1) * P],
                                             wvd_t[:, k, :], start=(k == 0), stop=(k == KC - 1))
                    last.then_inc(s["vd_mm_done"], 1)

                for n in range(VAR_A):
                    for work, i in BESIDE.get(n, ()):
                        {"CS": cs_part, "K": k_chunk, "WA": wa_block, "VD": value_operand}[work](i)
                    var_mm(pe, v, n, n % 4)

            @block.vector
            def _(dve):
                spacer = g["spacer"][:]
                chain = [0]

                def link(ins):
                    chain[0] += 1
                    ins.then_inc(s["s_chain"], 1)
                    dve.wait_ge(s["s_chain"], chain[0])

                dve.wait_ge(s["w_in"], 32)
                id_b = g["ident"][0:CH, 0:CH].unsqueeze(1).broadcast_to([CH, NCOND, CH])
                dve.tensor_tensor(w_plus[:], w_raw[:], id_b, ALU.add).then_inc(s["w_plus_ready"], 1)
                dve.wait_ge(s["wtw_mm_done"], 1)
                dve.tensor_copy(wtw[:], small[0:BOT, 0:2 * BOT]).then_inc(s["wtw_ready"], 1)
                dve.wait_ge(s["coefs_in"], 32)
                link(dve.tensor_tensor(coefs[:], coefs[:], masks[:].bitcast(U8), ALU.mult))
                link(dve.tensor_tensor(coefs[:, 0, :], coefs[:, 0, :], coefs[:, 1, :], ALU.add))
                dve.tensor_tensor(coefs[:, 0, :], coefs[:, 0, :], coefs[:, 2, :], ALU.add
                                  ).then_inc(s["wsum_ready"], 1)
                dve.wait_ge(s["w_hi_ready"], 1)
                dve.tensor_tensor(w_kinds[:, :, 1, :], w_raw[:], f(w_kinds[:, :, 0, :]), ALU.subtract
                                  ).then_inc(s["w_kinds_ready"], 1)
                dve.wait_ge(s["w_hi_ready"], 2)
                dve.tensor_tensor(w_kinds[:, :, 3, :], w_plus[:], f(w_kinds[:, :, 2, :]), ALU.subtract
                                  ).then_inc(s["w_kinds_ready"], 1)
                dve.wait_ge(s["enc_hi_ready"], 1)
                dve.tensor_tensor(enc_lo[:], enc[:], f(enc_hi[:]), ALU.subtract).then_inc(s["enc_split"], 1)
                dve.wait_ge(s["logrel_in"], 16)
                link(dve.tensor_copy(logrel_hi[:], logrel[:]))
                dve.tensor_tensor(logrel_lo[:], logrel[:], f(logrel_hi[:]), ALU.subtract
                                  ).then_inc(s["logrel_split"], 1)
                dve.wait_ge(s["g_mm_done"], 1)
                dve.tensor_scalar(router[:, 0:NSLOT], small[:, 0:NSLOT], float(RDIM) ** -0.5, None, ALU.mult)
                link(dve.tensor_scalar(router[:, NSLOT:], keys[:], float(BOT) ** -0.5, None, ALU.mult))
                link(dve.tensor_copy(g["router_a"][:], router[:]))
                dve.wait_ge(s["zeroed"], 1)
                dve.tensor_tensor(g["router_b"][0:BOT, :], router[0:BOT, :], f(g["router_a"][0:BOT, :]),
                                  ALU.subtract).then_inc(s["router_ready"], 1)

                def k_sum(k):
                    dve.wait_ge(wbase_in[k // 2], 16)
                    dve.wait_ge(s["k_mm_done"], k + 1)
                    dve.tensor_tensor(kf[:, k, :], kf[:, k, :], k_ps[:, :], ALU.add).then_inc(s["k_sum_ready"], 1)

                def k_low(k):
                    dve.wait_ge(s["k_hi_ready"], k + 1)
                    dve.tensor_tensor(k_lo[:, k, LEFT], kf[:, k, LEFT], f(k_hi[:, k, LEFT]), ALU.subtract)

                def a_low(c):
                    if c == 0:
                        dve.wait_ge(s["wvu_hi_ready"], 1)
                        dve.tensor_tensor(g["wvu_lo"][:], wvu[:], f(g["wvu_hi"][:]), ALU.subtract
                                          ).then_inc(s["wvu_split"], 1)
                    dve.wait_ge(s["a_hi_ready"], c + 1)
                    dve.tensor_tensor(a_lo[:], a_raw[:], f(a_hi[:]), ALU.subtract).then_inc(s["a_split_ready"], 1)

                for n in range(VAR_A):
                    if beside(n, "CS") == 2:
                        dve.wait_ge(s["cs_hi_ready"], 1)
                        dve.scalar_tensor_tensor(cs_lo[:], k_ps[0:RENC, :], 0.5, f(cs_hi[:]), ALU.mult,
                                                 ALU.subtract).then_inc(s["cs_split"], 1)
                    if (i := beside(n, "K")) is not None:
                        k_sum(i)
                    if (i := beside(n - 1, "K")) is not None:
                        k_low(i)
                    if (i := beside(n + 1, "WA")) is not None:
                        a_low(i)
                    var_stats(dve, spacer, g, v, n, n % 4)
                    if beside(n, "VD") is not None:
                        dve.wait_ge(s["vd_mm_done"], 1)
                        dve.tensor_copy(g["vd"][:], small[:, 0:2 * BOT].rearrange("p (b v) -> p b v", b=2))
                    if beside(n, "WA") == LBLK - 1:
                        dve.wait_ge(s["wa_mm_done"], LBLK)
                        wa3 = wa_bank.rearrange("p (l r) -> p l r", r=RANK)
                        link(dve.tensor_copy(wa_split[:, :, 0, :], wa3))
                        dve.tensor_tensor(wa_split[:, :, 1, :], wa3, f(wa_split[:, :, 0, :]), ALU.subtract
                                          ).then_inc(s["wa_split_ready"], 1)
    return k_hi, k_lo




def left_block(t, off):
    return bass.AP(t["left_blocks"].tensor, off, [[HID, P], [P, KC], [1, P]])


def fold_block(nc, t, g, v, pair, sem, tile, k_hi, k_lo, m_hi, m_lo):
    with ExitStack() as st:
        blk_raw = g["blk_raw"]
        blk_hi = tile(st, "blk_hi", [P, 2, KC, P], F32R)
        blk_lo = tile(st, "blk_lo", [P, 2, KC, P], F32R)
        bk_hi, bk_lo = m_hi[:, KC - 1, :], m_lo[:, KC - 1, :]
        bb = tile(st, "bb", [P, KC])

        names = ("bhi_ready blo_ready blk_done evac_hi_ready banks_free bk_stored bias_in "
                 "c_chain").split()
        s = {n: sem(n) for n in names}
        zpair = pair[2:4]
        NB = LBLK + KC
        per = (NT - VAR_A) // NB

        with nc.Block() as block:

            @block.sync
            def _(sp):
                sp.dma_start(bb[:], t["cond_bias"]).then_inc(s["bias_in"], 16)

                def load_block(b):
                    split, off = sp.snap(b), sp.snap(b * (P * HID))
                    sp.wait_ge(s["blo_ready"], split)
                    sp.dma_start(blk_raw[:], left_block(t, off)).then_inc(g["raw_loaded"], 16)

                def row_load(b, q):
                    var_load(sp, t, g, v, b * per + (VAR_A + q), q % per)

                sp.wait_ge(s["blo_ready"], 1)
                sp.dma_start(blk_raw[:], left_block(t, P * HID)).then_inc(g["raw_loaded"], 16)
                with sp.Fori(0, NB - 2) as b:
                    for q in range(1, per + 1):
                        row_load(b, q)
                    load_block(b + 2)
                for q in range(1, 2 * per):
                    row_load(NB - 2, q)

            @block.scalar
            def _(act):
                def block_hi(b, i):
                    act.wait_ge(g["raw_loaded"], b * 16 + 16)
                    act.copy(blk_hi[:, i], blk_raw[:]).then_inc(s["bhi_ready"], 1)

                def row_hi(b, q):
                    var_hi(act, v, b * per + (VAR_A + q), q)

                def one(b, i, evac, last=False, old_rows=False):
                    row_hi(b, 1)
                    if old_rows:
                        store(b - 1)
                    row_hi(b, 2)
                    if not last:
                        block_hi(b + 1, 1 - i)
                    row_hi(b, 3)
                    if not last:
                        row_hi(b + 1, 0)
                    act.wait_ge(s["blk_done"], b + 1)
                    evac(zpair[i])

                def evac_m(b):
                    def go(z):
                        act.copy(m_hi[:, bass.ds(b - LBLK, 1), :].rearrange("p a n -> p (a n)"), z[:]
                                 ).then_inc(s["evac_hi_ready"], 1)
                    return go

                def evac_bk(b):
                    def go(z):
                        if b:
                            act.wait_ge(s["bk_stored"], b * 32)
                        act.copy(bk_hi, z[:]).then_inc(s["evac_hi_ready"], 1)
                    return go

                def store(b):
                    act.wait_ge(s["banks_free"], b + 3)
                    for part, src in (("bk_hi", bk_hi), ("bk_lo", bk_lo)):
                        act.dma_start(t[part][b * P:(b + 1) * P, :], f(src)).then_inc(s["bk_stored"], 16)

                block_hi(0, 0)
                row_hi(0, 0)
                for b in range(LBLK):
                    one(b, b % 2, evac_bk(b), old_rows=b > 0)
                store(LBLK - 1)
                with act.Fori(0, KC // 2 - 1) as j:
                    b = j * 2 + LBLK
                    one(b, 0, evac_m(b))
                    one(b + 1, 1, evac_m(b + 1))
                one(NB - 2, 0, evac_m(NB - 2))
                act.wait_ge(s["bk_stored"], 32 * LBLK)
                one(NB - 1, 1, evac_m(NB - 1), last=True)

            @block.gpsimd
            def _(pool):
                def row_lo(b, q):
                    var_lo(pool, v, b * per + (VAR_A + q), q)

                def split(b, i):
                    ready = b + 1 if isinstance(b, int) else pool.snap(b + 1)
                    pool.wait_ge(s["bhi_ready"], ready)
                    pool.tensor_tensor(blk_lo[:, i], blk_raw[:], f(blk_hi[:, i]), ALU.subtract
                                       ).then_inc(s["blo_ready"], 1)

                def one(b, i, last=False):
                    row_lo(b, 1)
                    row_lo(b, 2)
                    if not last:
                        split(b + 1, 1 - i)
                    row_lo(b, 3)
                    if not last:
                        row_lo(b + 1, 0)

                row_lo(0, 0)
                with pool.Fori(0, NB // 2 - 1) as j:
                    b = j * 2
                    one(b, 0)
                    one(b + 1, 1)
                one(NB - 2, 0)
                one(NB - 1, 1, last=True)

            @block.tensor
            def _(pe):
                def one(b, i, identity=False):
                    pe.wait_ge(s["blo_ready"], b + 1)
                    pe.wait_ge(s["banks_free"], b + 1)
                    z = zpair[i]
                    for q in range(per):
                        h, k0 = q // 2, (q % 2) * (KC // 2)
                        c = slice(h * HALF, (h + 1) * HALF)
                        for k in range(k0, k0 + KC // 2):
                            last = product3(pe, z[:, c], blk_hi[:, i, k, :], blk_lo[:, i, k, :],
                                            k_hi[:, k, c], k_lo[:, k, c], k == 0,
                                            k == KC - 1 and not identity, skip=identity)
                        if q == per - 1:
                            if identity:
                                d = z[:, bass.ds((b - LBLK) * P, P)]
                                last = pe.matmul(d, g["ident_r"][:], g["ident_r"][:], start=False, stop=True,
                                                 skip_group_check=True)
                            last.then_inc(s["blk_done"], 1)
                        var_mm(pe, v, b * per + (VAR_A + q), q)

                with pe.Fori(0, LBLK // 2) as j:
                    b = j * 2
                    one(b, 0)
                    one(b + 1, 1)
                with pe.Fori(0, KC // 2) as j:
                    b = j * 2 + LBLK
                    one(b, 0, identity=True)
                    one(b + 1, 1, identity=True)

            @block.vector
            def _(dve):
                spacer = g["spacer"][:]

                def one(b, i, lo, hi, beside=None):
                    for q in range(per):
                        var_stats(dve, spacer, g, v, b * per + (VAR_A + q), q)
                        if beside is not None:
                            beside(b, q)
                    dve.wait_ge(s["evac_hi_ready"], b + 1)
                    dve.tensor_tensor(lo, zpair[i][:], f(hi), ALU.subtract).then_inc(s["banks_free"], 1)

                def const_step(b, q):
                    n = b * per + q
                    k, src = n // 2, (k_hi, k_lo)[n % 2]
                    if n:
                        dve.wait_ge(s["c_chain"], n)
                    else:
                        dve.wait_ge(s["bias_in"], 16)
                    dve.scalar_tensor_tensor(part[:], f(src[:, k, :]), bb[:, k:k + 1], part[:], ALU.mult,
                                             ALU.add).then_inc(s["c_chain"], 1)

                def m_rows(b):
                    return [m[:, bass.ds(b - LBLK, 1), :].rearrange("p a n -> p (a n)") for m in (m_lo, m_hi)]

                part = g["const_part"]
                dve.wait_ge(s["bhi_ready"], 1)
                dve.tensor_tensor(blk_lo[:, 0], blk_raw[:], f(blk_hi[:, 0]), ALU.subtract
                                  ).then_inc(s["blo_ready"], 1)
                dve.tensor_copy(g["ident_r"][:], g["ident"][:]).then_inc(s["banks_free"], 2)
                for b in range(LBLK):
                    one(b, b % 2, bk_lo, bk_hi, const_step)
                with dve.Fori(0, KC // 2) as j:
                    b = j * 2 + LBLK
                    one(b, 0, *m_rows(b))
                    one(b + 1, 1, *m_rows(b + 1))



def main_block(nc, t, g, pair, sem, tile, m_hi, m_lo):
    with ExitStack() as st:
        b = {}
        for name, shape, dt in (
            ("narrow", [P, 2 + NUG + NQG + 2, 2, KC, GRP], F32R),
            ("a_raw", [P, 2, 2, KC * GRP], F32),
            ("xt", [P, 2, HID], F32), ("xt_hi", [P, 2, HID], F32R), ("xt_lo", [P, 2, HID], F32R),
            ("pm_hi", [P, HID], F32R), ("pm_lo", [P, HID], F32R),
            ("pa_hi", [P, 2, PAW], F32R), ("pa_lo", [P, 2, PAW], F32R),
            ("out_sb", [P, 2, HID], F32),
            ("rhs_a", [P, HID], F32R), ("rhs_b", [P, 2, HID], F32R), ("rhs_c", [P, 2, HID], F32R),
            ("bd", [P, 2, 4, P], F32R), ("wa", [P, 2, 2, 2, RANK], F32R),
            ("lhs_a", [P, P], F32R), ("lhs_b", [P, P], F32R), ("lhs_c", [P, P], F32R),
            ("query", [P, P], F32R), ("q_a", [P, P], F32R), ("q_b", [P, P], F32R),
            ("u_sb", [P, P], F32R), ("e_t", [P, 2, P], F32), ("hm", [2 * RANK, P], F32),
            ("z", [P, NUNC], F32), ("z2", [P, NUNC], F32),
            ("arg", [P, NUNC], F32), ("th", [P, NUNC], F32), ("gelu", [P, NUNC], F32), ("dot", [P, NUNC], F32),
            ("bu1", [P, NUNC], F32), ("wu2", [P, NUNC], F32),
            ("rest", [P, NSLOT], F32), ("penalty", [P, NSLOT], F32), ("logits", [P, NSLOT], F32),
            ("probs", [P, NSLOT], F32),
            ("top8", [P, 8], F32), ("col", [P, 16], F32), ("gates", [P, 8], F32),
            ("mean", [P, 4], F32), ("lv_u", [P, NT], F32), ("lv_d", [P, NT], F32), ("lv_is1", [P, NT], F32),
            ("lv_ln", [P, NT], F32), ("lv_num", [P, NT], F32), ("lv_log", [P, NT], F32),
        ):
            b[name] = tile(st, "t_" + name, shape, dt)

        def wu_raw():
            return b["out_sb"][:].rearrange("p a (g c) -> p (a g) c", c=KC * GRP)

        def wq_raw(half):
            return b[("probs", "logits")[half]][:].rearrange("p (g c) -> p g c", c=KC * GRP)

        def lora_groups(p, part):
            return b["narrow"][:, A_GROUP[p]:A_GROUP[p] + 2, part].rearrange("p g k r -> p g (k r)")

        def wu_groups(part):
            return b["narrow"][:, 2:2 + NUG, part].rearrange("p g k r -> p g (k r)")

        def wq_groups(half, part):
            first = 2 + NUG + half * (NQG // 2)
            return b["narrow"][:, first:first + NQG // 2, part].rearrange("p g k r -> p g (k r)")

        col = b["col"]
        ROWMAX, NEGMAX, ESUM, LSUM, LTANH, UNC, CLIP, SCALED, UNORM, GTANH, GATE, GATED, RSUM, SCALE = range(14)

        def c1(n):
            return col[:, n:n + 1]

        HQ = (slice(2 * RANK, PAW), slice(0, HQW))
        LORA = (slice(0, 2 * RANK), slice(HQW, PAW))
        A_GROUP = (0, 2 + NUG + NQG)

        out_ps = pair[0]
        pm_ps = pair[1]
        pa_ps = pair[2][:, 0:HALF]
        mix_ps = pair[2][:, HALF:HID]
        score_ps = pair[3][:, 0:HALF]
        misc_ps = pair[3][:, HALF:HID]

        loaded = {n: [sem(f"{n}_loaded{p}") for p in range(2)] for n in ("xt", "lora")}
        moved = [sem(f"out_slot_moved{p}") for p in range(2)]
        names = ("wq_in row_in gate_in const_cleared const_done const_hi_ready const_placed lvu_ready "
                 "ln_ready lsum1_ready "
                 "mean_done norm_ready wu_hi_ready wu_split wq_hi_ready wq_split cleared "
                 "v_mm_ready va_ready vb_ready gates_ready m_chain "
                 "xhi_ready xlo_ready s1a_done s1b_done mixq_done qt_done score_done et_done u_done ut_done "
                 "h_done out_done pa_hi_ready pa_lo_ready pm_hi0_ready pm_hi1_ready pm_lo1_ready "
                 "q_hi_ready q_split z_ready z2_ready arg_ready tanh_ready gelu_ready lsum_ready "
                 "ltanh_ready unc_ready clip_ready scaled_ready unorm_ready gtanh_ready gate_ready gated_ready "
                 "qt_ready top8_ready rest_ready penalty_ready logits_ready negmax_ready exp_ready rsum_ready "
                 "scale_ready et_ready uhi_ready u_split ut_ready hm_ready hhi_ready h_ready out_ready").split()
        s = {n: sem("m_" + n) for n in names}
        XPT = 16 * 3
        LPT = 16 * 10

        with nc.Block() as block:

            @block.sync
            def _(sp):
                def load_x(i, p):
                    off = sp.snap(i * (P * HID)) if not isinstance(i, int) else i * P * HID
                    split = sp.snap(i - 1) if not isinstance(i, int) else i - 1
                    lora = [sp.value_load(g["lora_ids"][:, bass.ds(i * 2 + n, 1)], min_val=0,
                                          max_val=NLORA - 1) for n in range(2)]
                    a_off = [sp.snap(c * (P * KC * RANK)) for c in lora]
                    if known_positive(split):
                        sp.wait_ge(s["xlo_ready"], split)
                    sp.dma_start(b["xt"][:, p, :], bass.AP(t["x_t"].tensor, off, [[HID, P], [1, HID]])
                                 ).then_inc(loaded["xt"][p], 16)
                    for n in range(2):
                        sp.dma_start(b["a_raw"][:, p, n, :],
                                     bass.AP(t["lora_a"].tensor, a_off[n], [[KC * RANK, P], [1, KC * RANK]])
                                     ).then_inc(loaded["xt"][p], 16)

                load_x(0, 0)
                for p in range(2):
                    sp.dma_start(b["out_sb"][:, p, :], t["wu1_t"][:, p, :]).then_inc(moved[p], 16)
                sp.dma_start(b["probs"][:], t["wq_t"][:, 0:NSLOT]).then_inc(s["wq_in"], 16)
                sp.dma_start(b["logits"][:], t["wq_t"][:, NSLOT:]).then_inc(s["wq_in"], 16)

                def load_picked(i, p):
                    used = sp.snap(i - 1) if not isinstance(i, int) else i - 1
                    cond = [sp.value_load(g["cond_ids"][:, bass.ds(i * 2 + n, 1)], min_val=0,
                                          max_val=NCOND - 1) for n in range(2)]
                    lora = [sp.value_load(g["lora_ids"][:, bass.ds(i * 2 + n, 1)], min_val=0,
                                          max_val=NLORA - 1) for n in range(2)]
                    w_off = [sp.snap(c * (CH * 4 * CH)) for c in cond]
                    wa_off = [sp.snap(c * (P * 2 * RANK)) for c in lora]
                    bk_off = [sp.snap(c * (RANK * HID)) for c in lora]
                    if known_positive(used):
                        sp.wait_ge(s["out_done"], used)
                    done = loaded["lora"][p]
                    for n in range(2):
                        rows = slice(n * CH, (n + 1) * CH)
                        sp.dma_start(f(b["bd"][rows, p, :, rows]),
                                     bass.AP(t["w_kinds"].tensor, w_off[n], [[4 * CH, CH], [CH, 4], [1, CH]])
                                     ).then_inc(done, 16)
                        sp.dma_start(f(b["wa"][:, p, :, n, :]),
                                     bass.AP(t["wa_split"].tensor, wa_off[n], [[2 * RANK, P], [RANK, 2], [1, RANK]])
                                     ).then_inc(done, 16)
                        bk_h = bass.AP(t["bk_hi"].tensor, bk_off[n], [[HID, RANK], [1, HID]])
                        bk_l = bass.AP(t["bk_lo"].tensor, bk_off[n], [[HID, RANK], [1, HID]])
                        for base, dst, src in ((BOT, "rhs_b", bk_h), (BOT + 2 * RANK, "rhs_b", bk_h),
                                               (0, "rhs_c", bk_l)):
                            r0 = base + n * RANK
                            sp.dma_start(f(b[dst][r0:r0 + RANK, p, :]), src).then_inc(done, 16)

                def store(j, p):
                    off = sp.snap(j * (P * HID)) if not isinstance(j, int) else j * P * HID
                    ready = sp.snap(j + 1) if not isinstance(j, int) else j + 1
                    sp.wait_ge(s["out_ready"], ready)
                    sp.dma_start(bass.AP(t["out"].tensor, off, [[HID, P], [1, HID]]), b["out_sb"][:, p, :]
                                 ).then_inc(moved[p], 16)

                sp.dma_start(b["gates"][:, 0:3], t["gate_params"]).then_inc(s["gate_in"], 16)
                sp.wait_ge(s["cleared"], 1)
                load_picked(0, 0)
                load_x(1, 1)
                sp.dma_start(b["bu1"][:], t["bu1"]).then_inc(s["row_in"], 16)
                sp.dma_start(b["wu2"][:], t["wu2"]).then_inc(s["row_in"], 16)
                load_x(2, 0)
                load_picked(1, 1)
                with sp.Fori(0, NT // 2 - 2) as j:
                    i = j * 2 + 2
                    load_x(i + 1, 1)
                    load_picked(i, 0)
                    store(i - 2, 0)
                    load_x(i + 2, 0)
                    load_picked(i + 1, 1)
                    store(i - 1, 1)
                load_x(NT - 1, 1)
                load_picked(NT - 2, 0)
                store(NT - 4, 0)
                load_picked(NT - 1, 1)
                store(NT - 3, 1)
                store(NT - 2, 0)
                store(NT - 1, 1)
                for p in range(2):
                    sp.wait_ge(moved[p], 16 * (NT // 2 + 1))

            def steps(eng, step):
                step(0, 0)
                with eng.Fori(0, NT // 2 - 1) as j:
                    n = j * 2 + 1
                    step(n, 1)
                    step(n + 1, 0)
                step(NT - 1, 1)
                step(NT, 0)

            def has_new(n):
                return not isinstance(n, int) or n < NT

            def has_old(n):
                return not isinstance(n, int) or n > 0

            def arrived(n, p, each):
                return (n - p) * (each // 2) + each

            @block.scalar
            def _(act):
                def split_x(i, p):
                    act.wait_ge(loaded["xt"][p], arrived(i, p, XPT))
                    if known_positive(i - 1):
                        act.wait_ge(s["s1b_done"], i - 1)
                    act.copy(lora_groups(p, 0), b["a_raw"][:, p])
                    act.copy(b["xt_hi"][:, p, :], b["xt"][:, p, :]).then_inc(s["xhi_ready"], 1)

                act.wait_ge(s["lvu_ready"], 1)
                act.activation(b["lv_ln"][:], b["lv_u"][:], ACT.Ln).then_inc(s["ln_ready"], 1)
                split_x(0, 0)
                for p in range(2):
                    act.wait_ge(moved[p], 16)
                act.copy(wu_groups(0), wu_raw()).then_inc(s["wu_hi_ready"], 1)
                act.wait_ge(s["wq_in"], 32)
                act.copy(wq_groups(0, 0), wq_raw(0))
                act.copy(wq_groups(1, 0), wq_raw(1)).then_inc(s["wq_hi_ready"], 1)
                act.wait_ge(s["const_done"], 1)
                act.wait_ge(s["const_cleared"], 1)
                for row in (2 * RANK, BOT):
                    for p in range(2):
                        last = act.copy(b["rhs_c"][row:row + 1, p, :], pm_ps[row:row + 1, :])
                last.then_inc(s["const_hi_ready"], 1)
                act.wait_ge(s["v_mm_ready"], 1)
                act.copy(b["rhs_a"][:], out_ps[:]).then_inc(s["va_ready"], 1)
                act.wait_ge(s["gates_ready"], 1)

                def step(n, p):
                    if has_old(n):
                        act.wait_ge(s["s1b_done"], n)
                        act.copy(b["pm_hi"][:, 0:HALF], pm_ps[:, 0:HALF]).then_inc(s["pm_hi0_ready"], 1)
                        act.copy(b["pm_hi"][:, HALF:], pm_ps[:, HALF:]).then_inc(s["pm_hi1_ready"], 1)
                        act.wait_ge(s["ut_done"], n)
                        act.copy(b["lhs_a"][:], misc_ps[:, 0:P])
                        act.copy(b["lhs_b"][0:BOT, :], misc_ps[0:BOT, 0:P]).then_inc(s["ut_ready"], 1)
                    if has_new(n):
                        act.wait_ge(s["s1a_done"], n + 1)
                        act.copy(b["pa_hi"][:, p, :], pa_ps[:, 0:PAW]).then_inc(s["pa_hi_ready"], 1)
                    if not isinstance(n, int) or n + 1 < NT:
                        split_x(n + 1, 1 - p)
                    if has_old(n):
                        act.wait_ge(s["out_done"], n)
                        act.wait_ge(moved[1 - p], arrived(n - 1, 1 - p, 16))
                        act.copy(b["out_sb"][:, 1 - p, :], out_ps[:]).then_inc(s["out_ready"], 1)
                    if has_new(n):
                        act.wait_ge(s["qt_done"], n + 1)
                        act.copy(b["q_a"][:], misc_ps[:, 0:P])
                        act.copy(b["q_b"][0:BOT, :], misc_ps[0:BOT, 0:P]).then_inc(s["qt_ready"], 1)
                        act.wait_ge(s["z_ready"], n + 1)
                        act.activation(b["z2"][:], b["z"][:], ACT.Square, scale=0.044715 ** 0.5
                                       ).then_inc(s["z2_ready"], 1)
                        act.wait_ge(s["arg_ready"], n + 1)
                        act.activation(b["th"][:], b["arg"][:], ACT.Tanh, scale=TANH_C
                                       ).then_inc(s["tanh_ready"], 1)
                        act.wait_ge(s["negmax_ready"], n + 1)
                        act.activation(b["probs"][:], b["logits"][:], ACT.Exp, bias=c1(NEGMAX),
                                       accum_out=c1(ESUM)).then_inc(s["exp_ready"], 1)
                        act.wait_ge(s["lsum_ready"], n + 1)
                        act.activation(c1(LTANH), c1(LSUM), ACT.Tanh, scale=0.25, bias=b["gates"][:, 3:4]
                                       ).then_inc(s["ltanh_ready"], 1)
                        if not has_old(n):
                            act.wait_ge(s["norm_ready"], 1)
                        act.wait_ge(s["ltanh_ready"], n + 1)
                        act.activation(c1(UNC), c1(LTANH), ACT.Identity, scale=1.25,
                                       bias=g["norm_var"][:, bass.ds(n, 1)]).then_inc(s["unc_ready"], 1)
                        act.wait_ge(s["unorm_ready"], n + 1)
                        act.activation(c1(GTANH), c1(UNORM), ACT.Tanh, scale=b["gates"][:, 4:5],
                                       bias=b["gates"][:, 5:6]).then_inc(s["gtanh_ready"], 1)
                        act.wait_ge(s["et_done"], n + 1)
                        act.copy(b["e_t"][:].rearrange("p c n -> p (c n)"), misc_ps[:, P:3 * P]
                                 ).then_inc(s["et_ready"], 1)

                steps(act, step)

            @block.gpsimd
            def _(pool):
                pool.memset(f(b["bd"][:]), 0.0).then_inc(s["cleared"], 1)

                def split_x(i, p):
                    ready = i + 1 if isinstance(i, int) else pool.snap(i + 1)
                    pool.wait_ge(s["xhi_ready"], ready)
                    pool.tensor_tensor(lora_groups(p, 1), b["a_raw"][:, p], f(lora_groups(p, 0)), ALU.subtract)
                    pool.tensor_tensor(b["xt_lo"][:, p, :], b["xt"][:, p, :], f(b["xt_hi"][:, p, :]),
                                       ALU.subtract).then_inc(s["xlo_ready"], 1)

                split_x(0, 0)

                def step(n, p):
                    if not isinstance(n, int) or n + 1 < NT:
                        split_x(n + 1, 1 - p)

                steps(pool, step)

            @block.tensor
            def _(pe):
                for h in range(2):
                    c = slice(h * HALF, (h + 1) * HALF)
                    last = pe.matmul(pm_ps[:, c], g["ones"][:], g["const_part"][:, c], start=True, stop=True)
                last.then_inc(s["const_done"], 1)
                for h in range(2):
                    c = slice(h * HALF, (h + 1) * HALF)
                    for k in range(KC):
                        last = product3(pe, out_ps[:, c], g["wvu_hi"][:, k, :], g["wvu_lo"][:, k, :],
                                        m_hi[:, k, c], m_lo[:, k, c], k == 0, k == KC - 1)
                    if h == 0:
                        pe.wait_ge(s["lsum1_ready"], 1)
                        pe.matmul(score_ps[:, 0:1], g["ones"][:], b["mean"][:, 0:1], start=True, stop=True
                                  ).then_inc(s["mean_done"], 1)
                last.then_inc(s["v_mm_ready"], 1)
                pe.wait_ge(s["wu_split"], 1)
                pe.wait_ge(s["wq_split"], 1)
                pe.wait_ge(s["cleared"], 1)

                def step(n, p):
                    o = 1 - p
                    if has_new(n):
                        pe.wait_ge(s["xlo_ready"], n + 1)
                        if known_positive(n):
                            pe.wait_ge(s["pa_lo_ready"], n)
                    for k in range(KC):
                        if has_new(n):
                            x_h = b["xt_hi"][:, p, k * P:(k + 1) * P]
                            x_l = b["xt_lo"][:, p, k * P:(k + 1) * P]
                            g0 = 2 * p
                            n_h, n_l = (b["narrow"][:, g0:g0 + 2 + NUG + NQG, part, k, :] for part in range(2))
                            last = product3(pe, pa_ps[:, 0:PAW], x_h, x_l, n_h, n_l, k == 0, k == KC - 1)
                            if k == KC - 1:
                                last.then_inc(s["s1a_done"], 1)
                        if not has_old(n):
                            continue
                        if k == 0:
                            pe.wait_ge(s["et_ready"], n)
                            for c in range(2):
                                last = pe.matmul(misc_ps[:, 3 * P:3 * P + BOT], b["e_t"][:, c, :], g["vd"][:, c, :],
                                                 start=(c == 0), stop=(c == 1))
                            last.then_inc(s["u_done"], 1)
                        if k == 4:
                            pe.wait_ge(s["u_split"], n)
                            pe.transpose(misc_ps[:, 0:P], f(b["u_sb"][:]), g["ident"][:]).then_inc(s["ut_done"], 1)
                        if k == KC - 1:
                            pe.wait_ge(s["ut_ready"], n)
                            lo_ps = misc_ps[0:2 * RANK, P:2 * P]
                            w_h, w_l = b["bd"][:, o, 2, :], b["bd"][:, o, 3, :]
                            product3(pe, lo_ps, b["pa_hi"][:, o, LORA[o]], b["pa_lo"][:, o, LORA[o]],
                                     w_h, w_l, True, False)
                            wa_h, wa_l = (b["wa"][:, o, i].rearrange("p n r -> p (n r)") for i in range(2))
                            pe.matmul(lo_ps, wa_h, b["lhs_a"][:], start=False, stop=False)
                            pe.matmul(lo_ps, wa_l[0:BOT, :], b["lhs_b"][0:BOT, :], start=False, stop=True
                                      ).then_inc(s["h_done"], 1)
                    if has_old(n):
                        pe.wait_ge(s["pm_lo1_ready"], n)
                        w_h, w_l = b["bd"][:, o, 2, :], b["bd"][:, o, 3, :]
                        cs = [slice(0, HALF), slice(HALF, HID)]
                        for lhs, rhs, start in ((w_h, "pm_hi", True), (w_h, "pm_lo", False), (w_l, "pm_hi", False)):
                            for c in cs:
                                pe.matmul(out_ps[:, c], lhs, b[rhs][:, c], start=start, stop=False)
                        pe.wait_ge(s["h_ready"], n)
                        nc_rows = BOT + 1
                        for lhs, rhs, end in ((b["lhs_a"][:], b["rhs_a"][:], False),
                                              (b["lhs_b"][:], b["rhs_b"][:, o, :], False),
                                              (b["lhs_c"][0:nc_rows, :], b["rhs_c"][0:nc_rows, o, :], True)):
                            for c in cs:
                                last = pe.matmul(out_ps[:, c], lhs, rhs[:, c], start=False, stop=end)
                        last.then_inc(s["out_done"], 1)
                    if has_new(n):
                        pe.wait_ge(loaded["lora"][p], arrived(n, p, LPT))
                        pe.wait_ge(s["pa_lo_ready"], n + 1)
                        if known_positive(n):
                            pe.wait_ge(s["z_ready"], n)
                        product3(pe, mix_ps[:, 0:HQW], b["bd"][:, p, 0, :], b["bd"][:, p, 1, :],
                                 b["pa_hi"][:, p, HQ[p]], b["pa_lo"][:, p, HQ[p]],
                                 True, True).then_inc(s["mixq_done"], 1)
                        if known_positive(n):
                            pe.wait_ge(s["pm_lo1_ready"], n)
                        if not has_old(n):
                            pe.wait_ge(s["const_placed"], 1)
                        for k in range(KC):
                            x_h = b["xt_hi"][:, p, k * P:(k + 1) * P]
                            x_l = b["xt_lo"][:, p, k * P:(k + 1) * P]
                            first, end = k == 0, k == KC - 1
                            for lhs, m, a, z in ((x_h, m_hi, first, False), (x_h, m_lo, False, False),
                                                 (x_l, m_hi, False, end)):
                                for h in range(2):
                                    c = slice(h * HALF, (h + 1) * HALF)
                                    last = pe.matmul(pm_ps[:, c], lhs, m[:, k, c], start=a, stop=z)
                            if end:
                                last.then_inc(s["s1b_done"], 1)
                            if k == 0:
                                pe.wait_ge(s["q_split"], n + 1)
                                if known_positive(n):
                                    pe.wait_ge(s["hm_ready"], n)
                                pe.transpose(misc_ps[:, 0:P], f(b["query"][:]), g["ident"][:]
                                             ).then_inc(s["qt_done"], 1)
                            if k == 2:
                                pe.wait_ge(s["qt_ready"], n + 1)
                                if known_positive(n):
                                    pe.wait_ge(s["logits_ready"], n)
                                pe.matmul(score_ps, b["q_a"][:], g["router_a"][:], start=True, stop=False)
                                pe.matmul(score_ps, b["q_b"][0:BOT + 2, :], g["router_b"][0:BOT + 2, :],
                                          start=False, stop=True).then_inc(s["score_done"], 1)
                            if k == 6:
                                pe.wait_ge(s["exp_ready"], n + 1)
                                for c in range(2):
                                    last = pe.transpose(misc_ps[:, (c + 1) * P:(c + 2) * P],
                                                        b["probs"][:, c * P:(c + 1) * P], g["ident"][:])
                                last.then_inc(s["et_done"], 1)

                steps(pe, step)

            @block.vector
            def _(dve):
                spacer = g["spacer"][:]
                chain = [0]

                def link(ins):
                    chain[0] += 1
                    ins.then_inc(s["m_chain"], 1)
                    dve.wait_ge(s["m_chain"], chain[0])

                var = g["var"][:]
                dve.tensor_scalar(b["lv_u"][:], var, 1.0, None, ALU.add).then_inc(s["lvu_ready"], 1)
                dve.wait_ge(s["lvu_ready"], 1)
                link(dve.tensor_scalar(b["lv_d"][:], b["lv_u"][:], -1.0, None, ALU.add))
                link(dve.tensor_scalar(b["lv_is1"][:], b["lv_d"][:], 0.0, None, ALU.is_equal))
                link(dve.tensor_tensor(b["lv_d"][:], b["lv_d"][:], b["lv_is1"][:], ALU.add))
                link(dve.reciprocal(b["lv_d"][:], b["lv_d"][:]))
                dve.wait_ge(s["ln_ready"], 1)
                link(dve.tensor_tensor(b["lv_num"][:], b["lv_ln"][:], b["lv_is1"][:], ALU.add))
                link(dve.tensor_tensor(b["lv_num"][:], b["lv_num"][:], b["lv_d"][:], ALU.mult))
                link(dve.tensor_tensor(b["lv_log"][:], b["lv_num"][:], var, ALU.mult))
                dve.tensor_reduce(b["mean"][:, 0:1], b["lv_log"][:], AX.X, ALU.add).then_inc(s["lsum1_ready"], 1)
                dve.memset(f(b["q_b"][BOT:P, :]), 1.0)
                dve.memset(f(b["lhs_c"][:]), 1.0)
                dve.memset(f(b["rhs_c"][2 * RANK:BOT, :, :]), 0.0).then_inc(s["const_cleared"], 1)
                dve.wait_ge(s["wu_hi_ready"], 1)
                dve.tensor_tensor(wu_groups(1), wu_raw(), f(wu_groups(0)), ALU.subtract
                                  ).then_inc(s["wu_split"], 1)
                dve.wait_ge(s["wq_hi_ready"], 1)
                for half in range(2):
                    last = dve.tensor_tensor(wq_groups(half, 1), wq_raw(half), f(wq_groups(half, 0)), ALU.subtract)
                last.then_inc(s["wq_split"], 1)
                dve.wait_ge(s["const_hi_ready"], 1)
                for p in range(2):
                    last = dve.tensor_tensor(b["rhs_c"][BOT:BOT + 1, p, :], pm_ps[BOT:BOT + 1, :],
                                             f(b["rhs_c"][BOT:BOT + 1, p, :]), ALU.subtract)
                last.then_inc(s["const_placed"], 1)
                dve.wait_ge(s["gate_in"], 16)
                dve.tensor_scalar(b["gates"][:, 3:6], b["gates"][:, 0:3], 0.5, None, ALU.mult
                                  ).then_inc(s["gates_ready"], 1)
                dve.wait_ge(s["va_ready"], 1)
                for p in range(2):
                    last = dve.tensor_tensor(b["rhs_b"][0:BOT, p, :], out_ps[0:BOT, :],
                                             f(b["rhs_a"][0:BOT, :]), ALU.subtract)
                last.then_inc(s["vb_ready"], 1)
                dve.wait_ge(s["mean_done"], 1)
                link(dve.tensor_scalar(b["mean"][:, 1:2], score_ps[:, 0:1], 1.0 / (NT * P), 1e-6, ALU.mult, ALU.add))
                link(dve.reciprocal(b["mean"][:, 2:3], b["mean"][:, 1:2]))
                link(dve.tensor_scalar(b["lv_num"][:], b["lv_log"][:], b["mean"][:, 2:3], 0.5, ALU.mult, ALU.mult))
                dve.tensor_scalar(g["norm_var"][:], b["lv_num"][:], 1.25, None, ALU.add
                                  ).then_inc(s["norm_ready"], 1)
                dve.wait_ge(s["row_in"], 32)

                def step(n, p):
                    if has_old(n):
                        dve.wait_ge(s["pm_hi0_ready"], n)
                        dve.tensor_tensor(b["pm_lo"][:, 0:HALF], pm_ps[:, 0:HALF], f(b["pm_hi"][:, 0:HALF]),
                                          ALU.subtract)
                        u_ps = misc_ps[:, 3 * P:3 * P + BOT]
                        dve.wait_ge(s["u_done"], n)
                        dve.wait_ge(s["scale_ready"], n)
                        dve.tensor_scalar(b["u_sb"][:, 0:BOT], u_ps, c1(SCALE), None, ALU.mult
                                          ).then_inc(s["uhi_ready"], 1)
                        dve.wait_ge(s["uhi_ready"], n)
                        dve.scalar_tensor_tensor(b["u_sb"][:, BOT:], u_ps, c1(SCALE), f(b["u_sb"][:, 0:BOT]),
                                                 ALU.mult, ALU.subtract).then_inc(s["u_split"], 1)
                        dve.wait_ge(s["pm_hi1_ready"], n)
                        dve.tensor_tensor(b["pm_lo"][:, HALF:], pm_ps[:, HALF:], f(b["pm_hi"][:, HALF:]),
                                          ALU.subtract).then_inc(s["pm_lo1_ready"], 1)
                        dve.wait_ge(s["h_done"], n)
                        dve.tensor_tensor(b["hm"][:], misc_ps[0:2 * RANK, P:2 * P], g["lora_mask"][:], ALU.mult
                                          ).then_inc(s["hm_ready"], 1)
                        dve.wait_ge(s["hm_ready"], n)
                        dve.tensor_copy(b["lhs_c"][0:2 * RANK, :], b["hm"][:]).then_inc(s["hhi_ready"], 1)
                        dve.tensor_copy(b["lhs_b"][BOT:BOT + 2 * RANK, :], b["hm"][:])
                        dve.wait_ge(s["hhi_ready"], n)
                        dve.tensor_tensor(b["lhs_b"][BOT + 2 * RANK:, :], b["hm"][:], f(b["lhs_c"][0:2 * RANK, :]),
                                          ALU.subtract).then_inc(s["h_ready"], 1)
                    if has_new(n):
                        dve.wait_ge(s["pa_hi_ready"], n + 1)
                        dve.tensor_tensor(b["pa_lo"][:, p, :], pa_ps[:, 0:PAW], f(b["pa_hi"][:, p, :]),
                                          ALU.subtract).then_inc(s["pa_lo_ready"], 1)
                        q_ps = mix_ps[:, NUNC:NUNC + BOT]
                        dve.wait_ge(s["mixq_done"], n + 1)
                        dve.tensor_copy(b["query"][:, 0:BOT], q_ps).then_inc(s["q_hi_ready"], 1)
                        dve.wait_ge(s["q_hi_ready"], n + 1)
                        dve.tensor_tensor(b["query"][:, BOT:], q_ps, f(b["query"][:, 0:BOT]), ALU.subtract
                                          ).then_inc(s["q_split"], 1)
                        dve.tensor_tensor(b["z"][:], mix_ps[:, 0:NUNC], b["bu1"][:], ALU.add
                                          ).then_inc(s["z_ready"], 1)
                        dve.wait_ge(s["z2_ready"], n + 1)
                        dve.scalar_tensor_tensor(b["arg"][:], b["z2"][:], 1.0, b["z"][:], ALU.add, ALU.mult
                                                 ).then_inc(s["arg_ready"], 1)
                        wait_apart(dve, spacer, s["score_done"], n + 1)
                        dve.max(b["top8"][:], score_ps[:, 0:NSLOT]).then_inc(s["top8_ready"], 1)
                        wait_apart(dve, spacer, s["top8_ready"], n + 1)
                        dve.match_replace(b["rest"][:], b["top8"][:], score_ps[:, 0:NSLOT], REPLACED
                                          ).then_inc(s["rest_ready"], 1)
                        dve.wait_ge(s["rest_ready"], n + 1)
                        dve.tensor_scalar(b["penalty"][:], b["rest"][:], REPLACED, NEG, ALU.not_equal, ALU.mult
                                          ).then_inc(s["penalty_ready"], 1)
                        wait_apart(dve, spacer, s["penalty_ready"], n + 1)
                        dve.tensor_tensor_reduce(out=b["logits"][:], in0=b["penalty"][:],
                                                 in1=score_ps[:, NSLOT:2 * NSLOT], scale=1.0, scalar=-3.0e38,
                                                 op0=ALU.add, op1=ALU.max, accum_out=c1(ROWMAX)
                                                 ).then_inc(s["logits_ready"], 1)
                        dve.wait_ge(s["logits_ready"], n + 1)
                        dve.tensor_scalar(c1(NEGMAX), c1(ROWMAX), -1.0, None, ALU.mult
                                          ).then_inc(s["negmax_ready"], 1)
                        dve.wait_ge(s["tanh_ready"], n + 1)
                        dve.scalar_tensor_tensor(b["gelu"][:], b["th"][:], 1.0, b["z"][:], ALU.add, ALU.mult
                                                 ).then_inc(s["gelu_ready"], 1)
                        dve.wait_ge(s["gelu_ready"], n + 1)
                        dve.tensor_tensor_reduce(out=b["dot"][:], in0=b["gelu"][:], in1=b["wu2"][:], scale=1.0,
                                                 scalar=0.0, op0=ALU.mult, op1=ALU.add, accum_out=c1(LSUM)
                                                 ).then_inc(s["lsum_ready"], 1)
                        dve.wait_ge(s["exp_ready"], n + 1)
                        dve.reciprocal(c1(RSUM), c1(ESUM)).then_inc(s["rsum_ready"], 1)
                        dve.wait_ge(s["unc_ready"], n + 1)
                        dve.tensor_scalar(c1(CLIP), c1(UNC), 0.0, 5.0, ALU.max, ALU.min).then_inc(s["clip_ready"], 1)
                        dve.wait_ge(s["clip_ready"], n + 1)
                        dve.tensor_scalar(c1(SCALED), c1(CLIP), -0.5, 1.0 / 1.5, ALU.add, ALU.mult
                                          ).then_inc(s["scaled_ready"], 1)
                        dve.wait_ge(s["scaled_ready"], n + 1)
                        dve.tensor_scalar(c1(UNORM), c1(SCALED), 0.0, 1.0, ALU.max, ALU.min
                                          ).then_inc(s["unorm_ready"], 1)
                        dve.wait_ge(s["gtanh_ready"], n + 1)
                        dve.tensor_scalar(c1(GATE), c1(GTANH), 0.5, 0.5, ALU.mult, ALU.add).then_inc(s["gate_ready"], 1)
                        dve.wait_ge(s["gate_ready"], n + 1)
                        dve.scalar_tensor_tensor(c1(GATED), c1(GATE), 0.05, c1(GATE), ALU.is_ge, ALU.mult
                                                 ).then_inc(s["gated_ready"], 1)
                        dve.wait_ge(s["gated_ready"], n + 1)
                        dve.wait_ge(s["rsum_ready"], n + 1)
                        dve.tensor_tensor(c1(SCALE), c1(GATED), c1(RSUM), ALU.mult).then_inc(s["scale_ready"], 1)

                steps(dve, step)



def fourier_matrix(n):
    m = np.zeros((n, n))
    pos = np.arange(n)
    m[0] = n ** -0.5
    for fr in range(1, (n - 1) // 2 + 1):
        ang = 2 * np.pi * ((fr * pos) % n) / n
        m[2 * fr - 1] = np.sqrt(2.0 / n) * np.cos(ang)
        m[2 * fr] = np.sqrt(2.0 / n) * np.sin(ang)
    m[n - 1] = n ** -0.5 * (1 - 2 * (pos % 2))
    return m.astype(np.float32)


def kernel(**inputs):
    import concourse.bacc as bacc
    from concourse.bass_utils import run_bass_kernel_spmd

    a = {k: np.asarray(x) for k, x in inputs.items()}

    def chunks(m):
        return m.reshape(KC, P, -1).transpose(1, 0, 2)

    def groups(m):
        return m.T.reshape(KC, P, -1, GRP).transpose(1, 2, 0, 3).reshape(P, -1)

    x = a["x"].reshape(NT, P, HID)
    lora_a = a["L1_cond_lora_A_w"]
    lora_b = a["L1_cond_lora_B_w"]
    coefs = np.concatenate([a["L1_ffn_coefs0"], a["L1_ffn_coefs1"]], axis=2)
    masks = np.concatenate([a["L1_ffn_mask0"], a["L1_ffn_mask1"]], axis=2).view(np.uint8)

    def expert(m):
        return m.reshape(NEXP, KC, P, RENC).transpose(2, 0, 1, 3).reshape(P, NEXP, KC * RENC)

    rows = np.broadcast_to
    wvu = chunks(a["L0_ffn_Wvu"])
    data = {
        "x": x,
        "x_t": x.reshape(NT, P, KC, P).transpose(0, 3, 2, 1).reshape(NT, P, HID),
        "cond_ids": a["itok_B_0_15"].reshape(1, BATCH),
        "lora_ids": a["itok_B_6_15"].reshape(1, BATCH),
        "cond_w": a["L0_cond_weights"].transpose(1, 0, 2),
        "ident": np.eye(P, dtype=np.float32),
        "lora_mask": np.kron(np.eye(2), np.ones((RANK, CH))).astype(np.float32),
        "wvu": np.concatenate([wvu, wvu], axis=2),
        "wr": np.concatenate([a["L0_ffn_Wr"]] * 2, axis=1),
        "keys_t": np.concatenate([a["L0_ffn_aux_keys"].T] * 2, axis=0),
        "log_rel": a["L0_ffn_log_rel"].reshape(1, NSLOT),
        "lora_a": lora_a.reshape(NLORA, RANK, KC, P).transpose(0, 3, 2, 1).reshape(NLORA, P, KC * RANK),
        "av_t": chunks(a["L0_ffn_aux_values"].T),
        "wvd_t": chunks(a["L0_ffn_Wvd"].T),
        "coefs": expert(coefs),
        "masks": np.ascontiguousarray(expert(masks)).view(np.int32),
        "enc": np.concatenate([a["L1_ffn_enc0"], a["L1_ffn_enc1"]], axis=0),
        "fourier": fourier_matrix(HID).reshape(KC, P, HID),
        "w_base_t": a["L1_ffn_W_base"].T.reshape(KC, P, HID),
        "left_blocks": np.concatenate([
            lora_b.reshape(LBLK, LPB, KC, P, RANK).transpose(0, 3, 2, 1, 4).reshape(LBLK, P, KC, P),
            a["L1_cond_base_weight"].reshape(KC, P, KC, P).transpose(2, 1, 0, 3)]),
        "cond_bias": a["L1_cond_base_bias"].reshape(KC, P).T,
        "b_base": a["L1_ffn_b_base"].reshape(1, HID),
        "wu1_t": groups(a["L0_ffn_Wu1"]).reshape(P, 2, HID),
        "wq_t": groups(a["L0_ffn_Wq"]),
        "bu1": rows(a["L0_ffn_bu1"].reshape(1, NUNC), (P, NUNC)),
        "wu2": rows(a["L0_ffn_Wu2"].reshape(1, NUNC), (P, NUNC)),
        "gate_params": np.stack([rows(a[n].reshape(-1)[:1], (P,)) for n in
                                 ("L0_ffn_bu2", "L0_ffn_gate_w1", "L0_ffn_gate_bias")], axis=1),
    }
    nc = bacc.Bacc("TRN2", target_bir_lowering=False, num_devices=1)
    arrays, aps = {}, {}
    for name, value in data.items():
        value = np.ascontiguousarray(value)
        arrays["in_" + name] = value
        aps[name] = nc.dram_tensor("in_" + name, value.shape, mybir.dt.from_np(value.dtype),
                                   kind="ExternalInput").ap()
    aps["out"] = nc.dram_tensor("out", (NT, P, HID), F32, kind="ExternalOutput").ap()
    build(nc, aps)
    r = run_bass_kernel_spmd(nc, [arrays], core_ids=[0])
    return np.asarray(r.results[0]["out"]).reshape(BATCH, CH, HID)
```
